# Optimizing a Trainium2 kernel written in Bass

```python
import numpy as np
import jax
import jax.numpy as jnp

def _softmax(x, axis=-1):
    return jax.nn.softmax(x, axis=axis)

def _gelu(x):
    return jax.nn.gelu(x, approximate=True)

def _silu(x):
    return jax.nn.silu(x)

def _sigmoid(x):
    return jax.nn.sigmoid(x)

def _layernorm(x, axis=-1, eps=1e-05):
    m = jnp.mean(x, axis=axis, keepdims=True)
    v = jnp.var(x, axis=axis, keepdims=True)
    return (x - m) / jnp.sqrt(v + eps)

def _scatter_add(tgt, idx, src, axis=0):
    return tgt.at[idx].add(src)

def _segment_sum(src, seg, n):
    return jax.ops.segment_sum(src, seg, n)
kernel_name = 'mk_conv_preact_d2_conv_nchw192_r2_d7508c'

def setup_inputs(seed: int=0):
    np.random.seed(seed)
    _w = jnp.asarray

    def _rec_inputs():
        import jax
        import jax.numpy as jnp
        _gk = jax.random.key(seed)
        x = -0.0005058 + 1 * jax.random.normal(jax.random.fold_in(_gk, 1), (8, 96, 48, 48), jnp.float32)
        return x
    x = _rec_inputs()

    def _L0_conv_setup():
        import jax, jax.numpy as jnp
        import numpy as np
        B, C, H, W = (8, 96, 48, 48)
        D_EXP = 192
        D_INNER = 192
        K = 4
        N = 16
        R = 12

        def selective_scan(u, delta, A, Bs, Cs, Dskip):
            uT = u.transpose(3, 0, 1, 2)
            dT = delta.transpose(3, 0, 1, 2)
            BT = Bs.transpose(3, 0, 1, 2)
            CT = Cs.transpose(3, 0, 1, 2)
            h0 = jnp.zeros((u.shape[0], K, u.shape[2], A.shape[-1]), u.dtype)

            def step(h, xs_t):
                d_t, u_t, B_t, C_t = xs_t
                dA = jnp.exp(d_t[..., None] * A)
                h = h * dA + (d_t * u_t)[..., None] * B_t[:, :, None, :]
                y = jnp.einsum('bkdn,bkn->bkd', h, C_t)
                return (h, y)
            _, ys = jax.lax.scan(step, h0, (dT, uT, BT, CT))
            ys = ys.transpose(1, 2, 3, 0)
            return ys + u * Dskip[None, :, :, None]
        key = jax.random.key(seed)
        ks = jax.random.split(key, 9)
        return {'x': jax.random.normal(ks[0], (B, C, H, W), jnp.float32), 'in_proj_w': jax.random.normal(ks[1], (2 * D_EXP, C), jnp.float32) * 0.02, 'conv_w': jax.random.normal(ks[2], (D_EXP, 1, 3, 3), jnp.float32) * 0.1, 'conv_b': jax.random.normal(ks[3], (D_EXP,), jnp.float32) * 0.02, 'x_proj_w': jax.random.normal(ks[4], (K, R + 2 * N, D_INNER), jnp.float32) * 0.05, 'dt_w': jax.random.normal(ks[5], (K, D_INNER, R), jnp.float32) * 0.1, 'dt_b': jax.random.normal(ks[6], (K, D_INNER), jnp.float32) * 0.1, 'A_logs': jax.random.uniform(ks[7], (K * D_INNER, N), jnp.float32, -1.0, 1.0), 'Ds': jnp.ones((K * D_INNER,), jnp.float32), 'ln_w': jnp.ones((D_INNER,), jnp.float32), 'ln_b': jnp.zeros((D_INNER,), jnp.float32), 'out_proj_w': jax.random.normal(ks[8], (C, D_EXP), jnp.float32) * 0.02}
    _L0_conv_all = _L0_conv_setup()
    _L0_conv_in = {k: v for k, v in _L0_conv_all.items() if k in ('in_proj_w', 'conv_w', 'conv_b', 'x_proj_w', 'dt_w', 'dt_b', 'A_logs', 'Ds', 'ln_w', 'ln_b', 'out_proj_w')}
    del _L0_conv_all

    def _L1_conv_setup():
        import jax, jax.numpy as jnp
        import numpy as np
        DIM = 96
        HEADS = 8
        HEAD_DIM = DIM // HEADS
        SCALE = HEAD_DIM ** (-0.5)
        H = W = 32
        EPS = 1e-12
        key = jax.random.key(seed)
        k1, k2, k3, k4 = jax.random.split(key, 4)
        x = jax.random.normal(k1, (1, DIM, H, W), jnp.float32)
        w_qkv = jax.random.normal(k2, (3 * DIM, DIM), jnp.float32) * 0.05
        w_dw = jax.random.normal(k3, (3 * DIM, 1, 3, 3), jnp.float32) * 0.05
        w_proj = jax.random.normal(k4, (DIM, DIM), jnp.float32) * 0.05
        return {'x': x, 'w_qkv': w_qkv, 'w_dw': w_dw, 'w_proj': w_proj}
    _L1_conv_all = _L1_conv_setup()
    _L1_conv_in = {k: v for k, v in _L1_conv_all.items() if k in ('w_qkv', 'w_dw', 'w_proj')}
    del _L1_conv_all
    return {'x': x, 'L0_conv_in_proj_w': _L0_conv_in['in_proj_w'], 'L0_conv_conv_w': _L0_conv_in['conv_w'], 'L0_conv_conv_b': _L0_conv_in['conv_b'], 'L0_conv_x_proj_w': _L0_conv_in['x_proj_w'], 'L0_conv_dt_w': _L0_conv_in['dt_w'], 'L0_conv_dt_b': _L0_conv_in['dt_b'], 'L0_conv_A_logs': _L0_conv_in['A_logs'], 'L0_conv_Ds': _L0_conv_in['Ds'], 'L0_conv_ln_w': _L0_conv_in['ln_w'], 'L0_conv_ln_b': _L0_conv_in['ln_b'], 'L0_conv_out_proj_w': _L0_conv_in['out_proj_w'], 'L1_conv_w_qkv': _L1_conv_in['w_qkv'], 'L1_conv_w_dw': _L1_conv_in['w_dw'], 'L1_conv_w_proj': _L1_conv_in['w_proj']}

def reference(x, L0_conv_in_proj_w, L0_conv_conv_w, L0_conv_conv_b, L0_conv_x_proj_w, L0_conv_dt_w, L0_conv_dt_b, L0_conv_A_logs, L0_conv_Ds, L0_conv_ln_w, L0_conv_ln_b, L0_conv_out_proj_w, L1_conv_w_qkv, L1_conv_w_dw, L1_conv_w_proj):
    import jax
    import jax.numpy as jnp

    def _L0_conv_ref(x, in_proj_w, conv_w, conv_b, x_proj_w, dt_w, dt_b, A_logs, Ds, ln_w, ln_b, out_proj_w):
        import jax, jax.numpy as jnp
        import numpy as np
        B, C, H, W = (8, 96, 48, 48)
        D_EXP = 192
        D_INNER = 192
        K = 4
        N = 16
        R = 12

        def selective_scan(u, delta, A, Bs, Cs, Dskip):
            uT = u.transpose(3, 0, 1, 2)
            dT = delta.transpose(3, 0, 1, 2)
            BT = Bs.transpose(3, 0, 1, 2)
            CT = Cs.transpose(3, 0, 1, 2)
            h0 = jnp.zeros((u.shape[0], K, u.shape[2], A.shape[-1]), u.dtype)

            def step(h, xs_t):
                d_t, u_t, B_t, C_t = xs_t
                dA = jnp.exp(d_t[..., None] * A)
                h = h * dA + (d_t * u_t)[..., None] * B_t[:, :, None, :]
                y = jnp.einsum('bkdn,bkn->bkd', h, C_t)
                return (h, y)
            _, ys = jax.lax.scan(step, h0, (dT, uT, BT, CT))
            ys = ys.transpose(1, 2, 3, 0)
            return ys + u * Dskip[None, :, :, None]
        xz = jnp.einsum('bchw,oc->bohw', x, in_proj_w)
        xx, z = jnp.split(xz, 2, axis=1)
        z1 = jax.nn.gelu(z, approximate=False)
        xx = jax.lax.conv_general_dilated(xx, conv_w, (1, 1), 'SAME', feature_group_count=D_EXP, dimension_numbers=('NCHW', 'OIHW', 'NCHW')) + conv_b[None, :, None, None]
        xx = jax.nn.gelu(xx, approximate=False)
        Bb, Dd, Hh, Ww = xx.shape
        L = Hh * Ww
        x_hw = xx.reshape(Bb, Dd, L)
        x_wh = xx.transpose(0, 1, 3, 2).reshape(Bb, Dd, L)
        xs = jnp.stack([x_hw, x_wh, x_hw[..., ::-1], x_wh[..., ::-1]], axis=1)
        x_dbl = jnp.einsum('bkdl,kcd->bkcl', xs, x_proj_w)
        dts, Bs_, Cs_ = jnp.split(x_dbl, [R, R + N], axis=2)
        dts = jnp.einsum('bkrl,kdr->bkdl', dts, dt_w)
        delta = jax.nn.softplus(dts + dt_b[None, :, :, None])
        A = -jnp.exp(A_logs).reshape(K, D_INNER, N)
        ys = selective_scan(xs, delta, A, Bs_, Cs_, Ds.reshape(K, D_INNER))
        ys = ys[:, 0:2] + ys[:, 2:4, :, ::-1]
        y = ys[:, 0] + ys[:, 1].reshape(Bb, Dd, Ww, Hh).transpose(0, 1, 3, 2).reshape(Bb, Dd, L)
        y = y.transpose(0, 2, 1)
        mu = y.mean(-1, keepdims=True)
        var = ((y - mu) ** 2).mean(-1, keepdims=True)
        y = (y - mu) / jnp.sqrt(var + 1e-05) * ln_w + ln_b
        y = y.reshape(Bb, Hh, Ww, Dd).transpose(0, 3, 1, 2)
        y = y * z1
        out = jnp.einsum('bdhw,cd->bchw', y, out_proj_w)
        return out

    def _L1_conv_ref(x, w_qkv, w_dw, w_proj):
        import jax, jax.numpy as jnp
        import numpy as np
        DIM = 96
        HEADS = 8
        HEAD_DIM = DIM // HEADS
        SCALE = HEAD_DIM ** (-0.5)
        H = W = 32
        EPS = 1e-12
        B, C, h, w = x.shape
        n = h * w
        qkv = jnp.einsum('oc,bchw->bohw', w_qkv, x)
        qkv = jax.lax.conv_general_dilated(qkv, w_dw, window_strides=(1, 1), padding='SAME', dimension_numbers=('NCHW', 'OIHW', 'NCHW'), feature_group_count=3 * C)
        q, k, v = jnp.split(qkv, 3, axis=1)

        def to_heads(t):
            return t.reshape(B, HEADS, HEAD_DIM, n).transpose(0, 1, 3, 2)
        q, k, v = (to_heads(q), to_heads(k), to_heads(v))
        q = q / jnp.maximum(jnp.linalg.norm(q, axis=-1, keepdims=True), EPS)
        k = k / jnp.maximum(jnp.linalg.norm(k, axis=-1, keepdims=True), EPS)
        attn = jax.nn.softmax(jnp.einsum('bhnd,bhmd->bhnm', q, k) * SCALE, axis=-1)
        out = jnp.einsum('bhnm,bhmd->bhnd', attn, v)
        out = out.transpose(0, 1, 3, 2).reshape(B, C, h, w)
        return jnp.einsum('oc,bchw->bohw', w_proj, out)

    def _gn(v, G=32, eps=1e-05):
        B_, C_, H_, W_ = v.shape
        g = v.reshape(B_, G, C_ // G, H_, W_)
        m = jnp.mean(g, axis=(2, 3, 4), keepdims=True)
        s = jnp.var(g, axis=(2, 3, 4), keepdims=True)
        return ((g - m) / jnp.sqrt(s + eps)).reshape(v.shape)

    def _ln_c(v, eps=1e-06):
        m = jnp.mean(v, axis=1, keepdims=True)
        s = jnp.var(v, axis=1, keepdims=True)
        return (v - m) / jnp.sqrt(s + eps)

    def _ln_t(v, eps=1e-05):
        m = jnp.mean(v, axis=-1, keepdims=True)
        s = jnp.var(v, axis=-1, keepdims=True)
        return (v - m) / jnp.sqrt(s + eps)

    def _to_tokens(v):
        B_, C_, H_, W_ = v.shape
        return v.reshape(B_, C_, H_ * W_).transpose(0, 2, 1)

    def _from_tokens(t, like):
        B_, C_, H_, W_ = like.shape
        return t.transpose(0, 2, 1).reshape(B_, C_, H_, W_)
    x = x + _L0_conv_ref(_gn(x), L0_conv_in_proj_w, L0_conv_conv_w, L0_conv_conv_b, L0_conv_x_proj_w, L0_conv_dt_w, L0_conv_dt_b, L0_conv_A_logs, L0_conv_Ds, L0_conv_ln_w, L0_conv_ln_b, L0_conv_out_proj_w)
    x = x + _L1_conv_ref(_gn(x), L1_conv_w_qkv, L1_conv_w_dw, L1_conv_w_proj)
    return x

_drawn_inputs = setup_inputs


def setup_inputs(seed=0):
    import zlib

    import numpy as np

    out = dict(_drawn_inputs(seed))
    spreads = {'L0_conv_Ds': (1.0, 0.6), 'L0_conv_ln_w': (1.0, 0.6), 'L0_conv_ln_b': (0.0, 0.8)}
    factors = {'L0_conv_conv_b': 6.095,
     'L0_conv_x_proj_w': 8.0,
     'L0_conv_dt_w': 28.148,
     'L0_conv_dt_b': 26.367,
     'L0_conv_A_logs': 8.0,
     'L1_conv_w_qkv': 8.0,
     'L1_conv_w_dw': 8.0,
     'L1_conv_w_proj': 8.0}
    for name, (base, spread) in spreads.items():
        noise = np.random.default_rng([zlib.crc32(name.encode()), seed]).standard_normal(out[name].shape)
        drawn = base * np.exp(spread * noise) if base else spread * noise
        out[name] = jnp.asarray(drawn.astype(out[name].dtype))
    for name, factor in factors.items():
        out[name] = (out[name] * factor).astype(out[name].dtype)
    return out
```

```python
from contextlib import ExitStack

import concourse.bass as bass
from concourse import mybir

F32 = mybir.dt.float32
BF16 = mybir.dt.bfloat16
ALU = mybir.AluOpType
ACT = mybir.ActivationFunctionType

C, H, W = 96, 48, 48
L = H * W
DI, DA, DB = 192, 128, 64
K, N, R = 4, 16, 12
PC = 384
NPC = L // PC
SC = 2 * PC
NG = DI // 32
TG = 4
SPT = L // SC
SPG = TG * SPT
QL = L // 4
HQ = QL // 2
HEADS, HD = 8, 12
HG = 4
MB = L // 128
TERMS = 9
KS_ORDER = (0, 2, 1, 3)
SCALE = float(HD) ** -0.5
GN_EPS, LN_EPS, NORM_EPS = 1e-5, 1e-5, 1e-12
PADW = W + 2
PADL = (H + 2) * PADW
LN_EXP_TABLES = "natural_log_exp_and_others"
DVE_CHAIN, ACT_CHAIN = 95, 2


class Chain:

    def __init__(self, engine, sem, b, count):
        self.engine, self.sem, self.base, self.count, self.n = engine, sem, b * count, count, 0

    def mark(self, ins):
        ins.then_inc(self.sem, 1)
        self.n += 1
        return self.n

    def wait(self, n=None):
        self.engine.wait_ge(self.sem, self.base + (self.n if n is None else n))

    def link(self, ins):
        self.mark(ins)
        self.wait()

    def end(self):
        assert self.n == self.count, (self.n, self.count)


def build(nc, NB, a, out):
    ctx = ExitStack()
    with ctx:
        def sb(name, shape, dt=F32):
            return ctx.enter_context(nc.sbuf_tensor(name, shape, dt))

        def sem(name):
            return ctx.enter_context(nc.semaphore(name))

        in_proj = sb("in_proj", [C, 2 * DI])
        taps = [sb("taps_a", [DA, 9]), sb("taps_b", [DB, 9])]
        conv_bias = [sb("conv_bias_a", [DA, 1]), sb("conv_bias_b", [DB, 1])]
        xdt = [sb("xdt_a", [DA, K * 32]), sb("xdt_b", [DB, K * 32])]
        xbc = [sb("xbc_a", [DA, K * 32]), sb("xbc_b", [DB, K * 32])]
        dt_proj = sb("dt_proj", [128, K * DI])
        dt_bias = [sb("dt_bias_a", [DA, K]), sb("dt_bias_b", [DB, K])]
        a_cols = sb("a_cols", [128, K * NG * TG])
        skip = [sb("skip_a", [DA, K]), sb("skip_b", [DB, K])]
        skip_sum = [sb("skip_sum_a", [DA, 1]), sb("skip_sum_b", [DB, 1])]
        ln_w = [sb("ln_w_a", [DA, 1]), sb("ln_w_b", [DB, 1])]
        ln_b = [sb("ln_b_a", [DA, 1]), sb("ln_b_b", [DB, 1])]
        out_proj = [sb("out_proj_a", [DA, C]), sb("out_proj_b", [DB, C])]
        qkv_w = sb("qkv_w", [C, 3 * C])
        qkv_taps = sb("qkv_taps", [C, 27])
        proj_w = sb("proj_w", [128, 2 * C])
        pick_channel = sb("pick_channel", [96, TG * 128], BF16)
        sum_states = sb("sum_states", [128, TG * 32])
        group_mean = sb("group_mean", [C, C])
        mean192 = sb("mean192", [128, 128])
        head_ones = sb("head_ones", [C, C])
        ident = sb("ident", [C, C])
        pick_den = sb("pick_den", [128, 128])
        gn_eps = sb("gn_eps", [128, 1])

        xres = sb("xres", [C, L])
        xn = sb("xn", [C, L])
        u_buf = sb("u_buf", [128, 4 * L])
        dts = sb("dts", [128, L])
        rep = sb("rep", [128, 2 * L])
        em = sb("em", [128, 2 * L])
        parts_in = sb("parts_in", [128, 2 * L])
        work = sb("work", [128, 4 * L])
        y_acc = sb("y_acc", [128, NG * QL])
        b_third = sb("b_third", [128, SC])
        stats = sb("stats", [C, NPC * 6])
        mv = sb("mv", [C, 2])
        gn = sb("gn", [C, 6])

        u = [u_buf[:, 0:L], u_buf[0:DB, L:2 * L]]
        ut = [u_buf[:, 2 * L:3 * L], u_buf[0:DB, 3 * L:4 * L]]
        pads = [work[:, 0:PADL], work[0:DB, PADL:2 * PADL]]
        bc_stage = work[:, 3 * L:4 * L]
        b_rep, c_rep = rep[:, 0:L], rep[:, L:2 * L]
        P_OF = (DA, DB)
        delta = [em[0:p, 0:L] for p in P_OF]
        du = [em[0:p, L:2 * L] for p in P_OF]
        half = work[:, :].bitcast(BF16)
        parts = [[half[:, (3 * q + s) * L:(3 * q + s + 1) * L] for s in range(3)] for q in range(2)]
        slots = parts_in[:, :].bitcast(BF16)
        st = [[slots[0:96, (2 * s + q) * L:(2 * s + q + 1) * L] for q in range(2)] for s in range(2)]
        da_ring = [work[:, i * SC:(i + 1) * SC] for i in range(2)]
        b_ring = [work[:, (2 + i) * SC:(3 + i) * SC] for i in range(2)] + [b_third[:, :]]
        h_ring = [work[:, (4 + i) * SC:(5 + i) * SC] for i in range(2)]
        hc = [work[:, (2 + i) * L:(3 + i) * L] for i in range(2)]
        y = [em[:, 0:L], em[0:DB, L:2 * L]]
        yt = [work[:, 0:L], work[0:DB, L:2 * L]]
        std = work[:, 2 * L:3 * L]
        sq = [[work[0:p, 3 * L + (2 * s + t) * PC:3 * L + (2 * s + t + 1) * PC] for t, p in enumerate(P_OF)]
              for s in range(2)]
        zg = [[rep[0:p, (2 * s + t) * PC:(2 * s + t + 1) * PC] for t, p in enumerate(P_OF)] for s in range(2)]
        qkv_pads = [u_buf[0:C, t * PADL:(t + 1) * PADL] for t in range(3)]
        qkv = [dts[0:C, :], rep[0:C, 0:L], rep[0:C, L:2 * L]]
        nsq = [work[0:C, 3 * L + i * PC:3 * L + (i + 1) * PC] for i in range(2)]
        nrt = [work[0:C, 3 * L + (2 + i) * PC:3 * L + (3 + i) * PC] for i in range(2)]
        k_parts = em[:, :].bitcast(BF16)[0:TERMS * HD, :].rearrange("p (h l) -> p h l", h=HG)
        q_parts = [slots[0:TERMS * HD, s * HG * PC:(s + 1) * HG * PC].rearrange("p (h l) -> p h l", h=HG)
                   for s in range(2)]
        probs = [parts_in[:, (4 + i) * PC:(5 + i) * PC] for i in range(8)]
        v_cols = y_acc[:, 0:MB * HEADS * 13].rearrange("p (m d) -> p m d", d=13)
        ATT = MB * HEADS * 13
        att_o, att_r, att_n = (y_acc[:, ATT + i * PC:ATT + (i + 1) * PC] for i in range(3))

        ps = ctx.enter_context(nc.psum_tensor("ps", [128, 8, 512], F32))

        bc_dram = nc.dram_tensor("bc_scratch", [128, L], F32).ap()
        part_dram = [nc.dram_tensor(f"part_scratch{q}", [NG, 3, 32, L], BF16).ap() for q in range(2)]
        y_dram = nc.dram_tensor("y_scratch", [2, DI, L], F32).ap()
        qk_dram = nc.dram_tensor("qk_scratch", [2, 3, C, L], BF16).ap()

        names = """w_loaded const_set eps_set skip_summed x_loaded gn_stat gn_mean gn_dev gn_var gn_std xn_ready
            inp_mm inp_ev pads_zero conv_done u_ready xd_mm xd_ev bc_stored rep_loaded
            dt_mm dt_ev dt_max sp_ln delta_ready s1_ready r1_ready s2_ready s3_ready
            dbc ubc da_ready b_ready h_ready hc_ready hc_used y_ev y_stored y_loaded y_summed
            ln_mean ln_cent ln_sq ln_var ln_std z_mm z_act g_ready o_mm o_ev
            qkv_mm qkv_ev qkv_zero qkv_conv n_sq n_ss n_rt n_mul a_s1 a_r1 a_s2 a_s3 a_stored
            v_tr v_ev v_ones pv_zero ks_loaded s_done exp_done pv_done o_copied den_done on_ready pj_done
            xo_done out_stored dve_chain act_chain""".split()
        s = {n: sem(n) for n in names}
        passed = {e.engine: sem(f"passed_{n}") for n, e in (("act", nc.scalar), ("dve", nc.vector),
                                                            ("pool", nc.gpsimd), ("sp", nc.sync))}
        part_stored = [sem(f"part_stored{q}") for q in range(2)]
        st_loaded = [sem(f"st_loaded{i}") for i in range(2)]
        qs_loaded = [sem(f"qs_loaded{i}") for i in range(2)]

        def piece(c):
            return slice(c * PC, (c + 1) * PC)

        def bank(i, p=128, n=PC):
            return ps[0:p, i, 0:n]

        def square(ap):
            return ap.rearrange("p (h w) -> p h w", w=W)

        def swapped(ap):
            return ap.rearrange("p (h w) -> p w h", w=W)

        def window(pad, tap):
            dy, dx = divmod(tap, 3)
            return pad.rearrange("p (h w) -> p h w", w=PADW)[:, dy:dy + H, dx:dx + W]

        def pad_rows(pad, c):
            rows = PC // W
            return pad.rearrange("p (h w) -> p h w", w=PADW)[:, 1 + c * rows:1 + (c + 1) * rows, 1:1 + W]

        loads = [(in_proj, "in_projT"), (taps[0], "taps_a"), (taps[1], "taps_b"),
                 (conv_bias[0], "conv_b_a"), (conv_bias[1], "conv_b_b"), (xdt[0], "xdt_a"), (xdt[1], "xdt_b"),
                 (xbc[0], "xbc_a"), (xbc[1], "xbc_b"), (dt_proj, "dt_projT"), (dt_bias[0], "dt_b_a"),
                 (dt_bias[1], "dt_b_b"), (a_cols, "a_logs"), (skip[0], "ds_a"), (skip[1], "ds_b"),
                 (ln_w[0], "ln_w_a"), (ln_w[1], "ln_w_b"), (ln_b[0], "ln_b_a"), (ln_b[1], "ln_b_b"),
                 (out_proj[0], "out_proj_a"), (out_proj[1], "out_proj_b"), (qkv_w, "qkv_wT"),
                 (qkv_taps, "qkv_taps"), (proj_w, "proj_wT"), (pick_channel, "pick_channel"),
                 (sum_states, "sum_states"), (group_mean, "group_mean"), (mean192, "mean192"),
                 (head_ones, "head_ones"), (ident, "ident"), (pick_den, "pick_den")]
        W_LOADED = 16 * len(loads)

        def apart(engine):
            engine.sem_inc(passed[engine.engine], 1)

        block = ctx.enter_context(nc.Block())

        @block.sync
        def _(sp):
            for dst, name in loads:
                sp.dma_start(dst[:, :], a[name]).then_inc(s["w_loaded"], 16)

            def load_parts(kidx, g, slot):
                for q in range(2):
                    src = part_dram[q].rearrange("g s d l -> g (s d) l")
                    sp.dma_start(st[slot][q], src[bass.ds(g, 1), :, :].rearrange("g p l -> (g p) l"))\
                      .then_inc(st_loaded[slot], 16)

            def scan_prep(b, kk):
                kidx, k = b * K + kk, KS_ORDER[kk]
                sp.wait_ge(s["bc_stored"], 16 * (b + 1))
                apart(sp)
                if kk:
                    sp.wait_ge(s["hc_ready"], kidx * (NG * SPG))
                for j, dst in enumerate((b_rep, c_rep)):
                    row = bc_dram[32 * k + N * j:32 * k + N * (j + 1), :]
                    sp.dma_start(dst, bass.AP(row.tensor, row.offset, [[0, 8], [L, N], [1, L]]))\
                      .then_inc(s["rep_loaded"], 16)
                for t in range(2):
                    for q in range(2):
                        sp.wait_ge(s["s3_ready"], kidx * 4 + 2 * t + q + 1)
                        for r in range(3):
                            dst = part_dram[q][4 * t:4 * t + P_OF[t] // 32, r, :, :]
                            sp.dma_start(dst, parts[q][r][0:P_OF[t], :]).then_inc(part_stored[q], 16)

            def scan(b, kk):
                kidx = b * K + kk
                for q in range(2):
                    sp.wait_ge(part_stored[q], 96 * (kidx + 1))
                for g in range(2):
                    load_parts(kidx, g, g)
                with sp.Fori(1, NG // 2) as pair:
                    g = pair * 2
                    for j in range(2):
                        sp.wait_ge(s["ubc"], kidx * (NG * SPG) + g * SPG + (j - 1) * SPG)
                        apart(sp)
                        load_parts(kidx, g + j, j)
                if kk % 2:
                    sp.wait_ge(s["y_ev"], (kidx + 1) * NG)
                    for j in range(4):
                        dst = y_dram[kk // 2, :, j * QL:(j + 1) * QL].rearrange("(g d) r -> d g r", d=32)
                        src = y_acc[32 * j:32 * j + 32, :].rearrange("p (g r) -> p g r", r=QL)
                        sp.dma_start(dst, src).then_inc(s["y_stored"], 16)

            with sp.Fori(0, NB) as b:
                sp.dma_start(xres[:, :], a["x"][bass.ds(b, 1), :, :].rearrange("b c l -> (b c) l"))\
                  .then_inc(s["x_loaded"], 16)
                sp.wait_ge(s["xd_ev"], (b + 1) * NPC)
                sp.dma_start(bc_dram, bc_stage).then_inc(s["bc_stored"], 16)
                for kk in range(K):
                    scan_prep(b, kk)
                    scan(b, kk)
                sp.wait_ge(s["y_stored"], (b + 1) * 128)
                sp.dma_start(y[0], y_dram[0, 0:DA, :]).then_inc(s["y_loaded"], 16)
                sp.dma_start(y[1], y_dram[0, DA:DI, :]).then_inc(s["y_loaded"], 16)
                sp.dma_start(yt[0], y_dram[1, 0:DA, :]).then_inc(s["y_loaded"], 16)
                sp.dma_start(yt[1], y_dram[1, DA:DI, :]).then_inc(s["y_loaded"], 16)
                for t in range(2):
                    sp.wait_ge(s["a_s3"], b * 2 + t + 1)
                    for r in range(3):
                        sp.dma_start(qk_dram[t, r], parts[t][r][0:C, :]).then_inc(s["a_stored"], 16)
                sp.wait_ge(s["a_stored"], (b + 1) * 96)

                def load_q(hg, n, slot):
                    for t in range(TERMS):
                        src = qk_dram[0, t // 3, hg * HG * HD:(hg + 1) * HG * HD, :]\
                            .rearrange("(h d) l -> d h l", d=HD)[:, :, bass.ds(n * PC, PC)]
                        sp.dma_start(q_parts[slot][t * HD:(t + 1) * HD], src).then_inc(qs_loaded[slot], 16)

                for hg in range(2):
                    if hg:
                        sp.wait_ge(s["s_done"], (b * 2 + hg) * NPC * MB * HG)
                    for t in range(TERMS):
                        src = qk_dram[1, t % 3, hg * HG * HD:(hg + 1) * HG * HD, :]\
                            .rearrange("(h d) l -> d h l", d=HD)
                        sp.dma_start(k_parts[t * HD:(t + 1) * HD], src).then_inc(s["ks_loaded"], 16)
                    for n in range(2):
                        load_q(hg, n, n)
                    with sp.Fori(1, NPC // 2) as pair:
                        n = pair * 2
                        for j in range(2):
                            sp.wait_ge(s["s_done"], ((b * 2 + hg) * NPC + n + (j - 1)) * (MB * HG))
                            apart(sp)
                            load_q(hg, n + j, j)
                sp.wait_ge(s["xo_done"], (b + 1) * 2 * NPC)
                apart(sp)
                sp.dma_start(out[bass.ds(b, 1), :, :].rearrange("b c l -> (b c) l"), xres[:, :])\
                  .then_inc(s["out_stored"], 16)
                sp.wait_ge(s["out_stored"], (b + 1) * 16)
                apart(sp)

        @block.gpsimd
        def _(pool):
            def scan_step(kidx, g, i, c, cc, first):
                n = kidx * (NG * SPG) + g * SPG + (i * SPT + c)
                pool.wait_ge(s["h_ready"], n + 1)
                if c == 0 and not (first and i < 2):
                    pool.wait_ge(s["hc_used"], kidx * (NG * TG) + g * TG + (i - 1))
                cols = slice(cc * SC, (cc + 1) * SC)
                pool.tensor_tensor(hc[i % 2][:, cols], h_ring[(i * SPT + c) % 2], c_rep[:, cols], ALU.mult)\
                    .then_inc(s["hc_ready"], 1)

            with pool.Fori(0, NB) as b:
                pool.memset(pads[0], 0.0)
                pool.memset(pads[1], 0.0).then_inc(s["pads_zero"], 1)
                for kk in range(K):
                    kidx = b * K + kk

                    def chunk(c):
                        return SPT - 1 - c if KS_ORDER[kk] >= 2 else c

                    pool.wait_ge(s["rep_loaded"], 32 * (kidx + 1))
                    for i in range(TG):
                        for c in range(SPT):
                            scan_step(kidx, 0, i, c, chunk(c), True)
                    with pool.Fori(1, NG) as g:
                        for i in range(TG):
                            for c in range(SPT):
                                scan_step(kidx, g, i, c, chunk(c), False)
                pool.wait_ge(s["y_summed"], b + 1)
                apart(pool)
                for t in range(3):
                    ins = pool.memset(qkv_pads[t], 0.0)
                ins.then_inc(s["qkv_zero"], 1)
                pool.wait_ge(s["out_stored"], (b + 1) * 16)
                apart(pool)

        @block.scalar
        def _(act):
            act.wait_ge(s["w_loaded"], W_LOADED)
            act.activation(a_cols[:, :], a_cols[:, :], ACT.Exp).then_inc(s["const_set"], 1)
            act.wait_ge(s["const_set"], 1)
            act.mul(a_cols[:, :], a_cols[:, :], -1.0).then_inc(s["const_set"], 1)
            act.wait_ge(s["const_set"], 2)
            act.wait_ge(s["eps_set"], 1)

            def group_std(b, t):
                act.wait_ge(s["gn_var"], b * 2 + t + 1)
                act.activation(gn[:, 2:3], ps[0:C, 6, 0:1], ACT.Sqrt, bias=gn_eps[0:C, :]).then_inc(s["gn_std"], 1)

            def scan_step(kidx, k, g, i, c, first):
                n = kidx * (NG * SPG) + g * SPG + (i * SPT + c)
                act.wait_ge(s["dbc"], n + 1)
                if not (first and i * SPT + c < 2):
                    act.wait_ge(s["h_ready"], n - 1)
                apart(act)
                act.activation(da_ring[(i * SPT + c) % 2].rearrange("p (a r) -> p a r", a=2), ps[:, 0:2, 0:PC],
                               ACT.Exp, scale=a_cols[:, bass.ds(g * TG + (k * NG * TG + i), 1)])\
                    .then_inc(s["da_ready"], 1)

            with act.Fori(0, NB) as b:
                chain = Chain(act, s["act_chain"], b, ACT_CHAIN)
                group_std(b, 0)
                act.wait_ge(s["pads_zero"], b + 1)
                for c in range(NPC):
                    act.wait_ge(s["inp_mm"], b * NPC + c + 1)
                    act.copy(pad_rows(pads[0], c), square(bank(2 * (c % 2))))
                    act.copy(pad_rows(pads[1], c), square(bank(2 * (c % 2) + 1, DB))).then_inc(s["inp_ev"], 1)
                act.wait_ge(s["conv_done"], b + 1)
                for t in range(2):
                    chain.mark(act.activation(u[t], u[t], ACT.Gelu, bias=conv_bias[t][:, :]))
                for t in range(2):
                    chain.wait(1 + t)
                    ins = act.copy(square(ut[t]), swapped(u[t]))
                ins.then_inc(s["u_ready"], 1)
                for c in range(NPC):
                    act.wait_ge(s["xd_mm"], b * NPC + c + 1)
                    act.copy(dts[:, piece(c)], bank(2 * (c % 2)))
                    act.copy(bc_stage[:, piece(c)], bank(2 * (c % 2) + 1)).then_inc(s["xd_ev"], 1)
                act.preload_act_table_set(LN_EXP_TABLES)
                for kk in range(K):
                    kidx, k = b * K + kk, KS_ORDER[kk]
                    if kk:
                        act.wait_ge(s["hc_used"], kidx * (NG * TG))
                    act.wait_ge(s["bc_stored"], 16 * (b + 1))
                    for t in range(2):
                        p = P_OF[t]
                        if t:
                            act.wait_ge(s["s3_ready"], kidx * 4 + 2)
                        for c in range(NPC):
                            m = t * NPC + c
                            act.wait_ge(s["dt_mm"], kidx * 2 * NPC + m + 1)
                            act.activation(delta[t][:, piece(c)], bank(m % 4, p), ACT.Identity,
                                           bias=dt_bias[t][:, k:k + 1]).then_inc(s["dt_ev"], 1)
                        act.wait_ge(s["dt_max"], kidx * 2 + t + 1)
                        act.activation(delta[t], delta[t], ACT.Abs).then_inc(s["sp_ln"], 1)
                        act.wait_ge(s["sp_ln"], kidx * 6 + 3 * t + 1)
                        act.activation(delta[t], delta[t], ACT.Exp, scale=-1.0).then_inc(s["sp_ln"], 1)
                        act.wait_ge(s["sp_ln"], kidx * 6 + 3 * t + 2)
                        act.activation(delta[t], delta[t], ACT.Ln, bias=1.0).then_inc(s["sp_ln"], 1)
                        for q, src in enumerate((delta[t], du[t])):
                            act.wait_ge(s["delta_ready"], kidx * 4 + 2 * t + q + 1)
                            if kk or t:
                                act.wait_ge(part_stored[q], 96 * kidx + 48 * t)
                            act.copy(parts[q][0][0:p, :], src).then_inc(s["s1_ready"], 1)
                        for q, src in enumerate((delta[t], du[t])):
                            act.wait_ge(s["r1_ready"], kidx * 4 + 2 * t + q + 1)
                            act.copy(parts[q][1][0:p, :], src).then_inc(s["s2_ready"], 1)
                    for q in range(2):
                        act.wait_ge(part_stored[q], 96 * (kidx + 1))
                    for i in range(TG):
                        for c in range(SPT):
                            scan_step(kidx, k, 0, i, c, True)
                    with act.Fori(1, NG) as g:
                        for i in range(TG):
                            for c in range(SPT):
                                scan_step(kidx, k, g, i, c, False)
                for c in range(NPC + 1):
                    if c < NPC:
                        act.wait_ge(s["ln_cent"], b * NPC + c + 1)
                        if c >= 2:
                            act.wait_ge(s["ln_var"], b * NPC + c - 1)
                        for t in range(2):
                            ins = act.activation(sq[c % 2][t], y[t][:, piece(c)], ACT.Square)
                        ins.then_inc(s["ln_sq"], 1)
                    if c:
                        act.wait_ge(s["ln_var"], b * NPC + c)
                        act.activation(std[:, piece(c - 1)], bank(2 + (c - 1) % 2), ACT.Sqrt, bias=gn_eps[:, :])\
                            .then_inc(s["ln_std"], 1)
                for c in range(NPC):
                    act.wait_ge(s["z_mm"], b * NPC + c + 1)
                    if c >= 2:
                        act.wait_ge(s["g_ready"], b * NPC + c - 1)
                    for t in range(2):
                        ins = act.activation(zg[c % 2][t], bank(4 + 2 * (c % 2) + t, P_OF[t]), ACT.Gelu)
                    ins.then_inc(s["z_act"], 1)
                group_std(b, 1)
                act.wait_ge(s["qkv_zero"], b + 1)
                for c in range(NPC):
                    act.wait_ge(s["qkv_mm"], b * NPC + c + 1)
                    for t in range(3):
                        ins = act.copy(pad_rows(qkv_pads[t], c), square(bank(3 * (c % 2) + t, C)))
                    ins.then_inc(s["qkv_ev"], 1)
                act.wait_ge(s["qkv_conv"], b + 1)
                n_all = 2 * NPC
                for n in range(n_all + 1):
                    if n < n_all:
                        if n >= 2:
                            act.wait_ge(s["n_ss"], b * n_all + n - 1)
                        act.activation(nsq[n % 2], qkv[n // NPC][:, piece(n % NPC)], ACT.Square)\
                            .then_inc(s["n_sq"], 1)
                    if n:
                        act.wait_ge(s["n_ss"], b * n_all + n)
                        if n >= 3:
                            act.wait_ge(s["n_mul"], b * n_all + n - 2)
                        act.activation(nrt[(n - 1) % 2], bank((n - 1) % 2, C), ACT.Sqrt).then_inc(s["n_rt"], 1)
                for t in range(2):
                    act.wait_ge(s["n_mul"], b * n_all + (t + 1) * NPC)
                    act.copy(parts[t][0][0:C, :], qkv[t]).then_inc(s["a_s1"], 1)
                for t in range(2):
                    act.wait_ge(s["a_r1"], b * 2 + t + 1)
                    act.copy(parts[t][1][0:C, :], qkv[t]).then_inc(s["a_s2"], 1)

                def exps(hg, n, slot, first):
                    col = (b * 2 + hg) * NPC + n
                    for m in range(MB):
                        if not (first and m < 2):
                            act.wait_ge(s["pv_done"], col * MB + (m - 1))
                        for h in range(HG):
                            act.wait_ge(s["s_done"], col * (MB * HG) + (m * HG + h + 1))
                            act.activation(probs[(m % 2) * HG + h], bank(h), ACT.Exp, scale=SCALE)\
                                .then_inc(s["exp_done"], 1)

                for hg in range(2):
                    exps(hg, 0, 0, True)
                    with act.Fori(1, NPC) as n:
                        exps(hg, n, 0, False)
                chain.end()

        @block.vector
        def _(dve):
            dve.memset(gn_eps[:, :], GN_EPS).then_inc(s["eps_set"], 1)
            dve.wait_ge(s["w_loaded"], W_LOADED)
            for t in range(2):
                dve.tensor_reduce(skip_sum[t][:, :], skip[t][:, :], mybir.AxisListType.X, ALU.add)\
                   .then_inc(s["skip_summed"], 1)
            dve.wait_ge(s["skip_summed"], 2)

            def group_norm(b, t, chain):
                for c in range(NPC):
                    ins = dve.bn_stats(stats[:, 6 * c:6 * c + 6], xres[:, piece(c)])
                chain.link(ins)
                apart(dve)
                dve.bn_aggr(mv[:, :], stats[:, :]).then_inc(s["gn_stat"], 1)
                dve.wait_ge(s["gn_mean"], b * 2 + t + 1)
                chain.link(dve.tensor_copy(gn[:, 0:1], ps[0:C, 7, 0:1]))
                chain.link(dve.tensor_tensor(gn[:, 1:2], mv[:, 0:1], gn[:, 0:1], ALU.subtract))
                dve.scalar_tensor_tensor(out=gn[:, 3:4], in0=gn[:, 1:2], scalar=gn[:, 1:2], in1=mv[:, 1:2],
                                         op0=ALU.mult, op1=ALU.add).then_inc(s["gn_dev"], 1)
                dve.wait_ge(s["gn_std"], b * 2 + t + 1)
                chain.link(dve.reciprocal(gn[:, 4:5], gn[:, 2:3]))
                dve.tensor_scalar(xn[:, :], xres[:, :], gn[:, 0:1], gn[:, 4:5], ALU.subtract, ALU.mult)\
                   .then_inc(s["xn_ready"], 1)

            def conv(chain, jobs, done):
                marks = {}
                for tap in range(9):
                    for j, (dst, pad, w) in enumerate(jobs):
                        if tap == 0:
                            ins = dve.tensor_scalar(square(dst), window(pad, 0), w[:, 0:1], None, ALU.mult)
                        else:
                            chain.wait(marks[j])
                            ins = dve.scalar_tensor_tensor(out=square(dst), in0=window(pad, tap),
                                                           scalar=w[:, tap:tap + 1], in1=square(dst),
                                                           op0=ALU.mult, op1=ALU.add)
                        if tap == 8 and j == len(jobs) - 1:
                            ins.then_inc(s[done], 1)
                        else:
                            marks[j] = chain.mark(ins)

            def mult_b(kidx, g, n_in, cc, first):
                n = kidx * (NG * SPG) + g * SPG + n_in
                dve.wait_ge(s["ubc"], n + 1)
                if not (first and n_in < 3):
                    dve.wait_ge(s["h_ready"], n - 2)
                cols = slice(cc * SC, (cc + 1) * SC)
                dve.tensor_tensor(b_ring[n_in % 3].rearrange("p (a r) -> p a r", a=2), ps[:, 2:4, 0:PC],
                                  b_rep[:, cols].rearrange("p (a r) -> p a r", a=2), ALU.mult)\
                   .then_inc(s["b_ready"], 1)

            def scan_step(kidx, g, n_in, back, first):
                n = kidx * (NG * SPG) + g * SPG + n_in
                dve.wait_ge(s["da_ready"], n + 1)
                dve.wait_ge(s["b_ready"], n + 1)
                if not (first and n_in == 0):
                    dve.wait_ge(s["h_ready"], n)
                if n_in % SPT:
                    prev = h_ring[(n_in + 1) % 2]
                    init = prev[:, 0:1] if back else prev[:, SC - 1:SC]
                else:
                    init = 0.0
                if not (first and n_in < 2):
                    dve.wait_ge(s["hc_ready"], n - 1)
                o, d0, d1 = h_ring[n_in % 2], da_ring[n_in % 2], b_ring[n_in % 3]
                if back:
                    o, d0, d1 = o[:, ::-1], d0[:, ::-1], d1[:, ::-1]
                dve.tensor_tensor_scan(o, d0, d1, init, ALU.mult, ALU.add).then_inc(s["h_ready"], 1)

            def y_evacuate(kidx, g, add):
                dve.wait_ge(s["hc_used"], (kidx * NG + g + 1) * TG)
                dst = y_acc[:, bass.ds(g * QL, QL)].rearrange("p (a r) -> p a r", a=2)
                src = ps[:, 4:6, 0:HQ]
                if add:
                    dve.tensor_tensor(dst, src, dst, ALU.add).then_inc(s["y_ev"], 1)
                else:
                    dve.tensor_copy(dst, src).then_inc(s["y_ev"], 1)

            with dve.Fori(0, NB) as b:
                chain = Chain(dve, s["dve_chain"], b, DVE_CHAIN)
                dve.wait_ge(s["x_loaded"], 16 * (b + 1))
                group_norm(b, 0, chain)
                dve.wait_ge(s["inp_ev"], (b + 1) * NPC)
                conv(chain, [(u[t], pads[t], taps[t]) for t in range(2)], "conv_done")
                for kk in range(K):
                    kidx, k = b * K + kk, KS_ORDER[kk]
                    back = k >= 2
                    for t in range(2):
                        p = P_OF[t]
                        dve.wait_ge(s["dt_ev"], kidx * 2 * NPC + (t + 1) * NPC)
                        if t:
                            dve.wait_ge(s["s2_ready"], kidx * 4 + 2)
                        dve.tensor_scalar(du[t], delta[t], 0.0, None, ALU.max).then_inc(s["dt_max"], 1)
                        dve.wait_ge(s["dt_max"], kidx * 2 + t + 1)
                        dve.wait_ge(s["sp_ln"], kidx * 6 + 3 * t + 3)
                        dve.tensor_tensor(delta[t], delta[t], du[t], ALU.add).then_inc(s["delta_ready"], 1)
                        dve.wait_ge(s["delta_ready"], kidx * 4 + 2 * t + 1)
                        dve.tensor_tensor(du[t], delta[t], (ut if k % 2 else u)[t], ALU.mult)\
                           .then_inc(s["delta_ready"], 1)
                        for q, x in enumerate((delta[t], du[t])):
                            if q:
                                dve.wait_ge(s["delta_ready"], kidx * 4 + 2 * t + 2)
                            dve.wait_ge(s["s1_ready"], kidx * 4 + 2 * t + q + 1)
                            dve.tensor_tensor(x, x, parts[q][0][0:p, :], ALU.subtract).then_inc(s["r1_ready"], 1)
                        for q, x in enumerate((delta[t], du[t])):
                            dve.wait_ge(s["r1_ready"], kidx * 4 + 2 * t + q + 1)
                            dve.wait_ge(s["s2_ready"], kidx * 4 + 2 * t + q + 1)
                            dve.tensor_tensor(parts[q][2][0:p, :], x, parts[q][1][0:p, :], ALU.subtract)\
                               .then_inc(s["s3_ready"], 1)
                    dve.wait_ge(s["rep_loaded"], 32 * (kidx + 1))
                    for q in range(2):
                        dve.wait_ge(part_stored[q], 96 * (kidx + 1))
                    if kk == 2:
                        dve.wait_ge(s["y_stored"], b * 128 + 64)

                    def chunk(n_in):
                        return SPT - 1 - n_in % SPT if back else n_in % SPT

                    def group(g, first):
                        mult_b(kidx, g, 0, chunk(0), first)
                        for n_in in range(SPG):
                            if n_in + 1 < SPG:
                                mult_b(kidx, g, n_in + 1, chunk(n_in + 1), first)
                            scan_step(kidx, g, n_in, back, first)
                            if n_in == SPT + 1 and not first:
                                y_evacuate(kidx, g - 1, kk % 2)

                    group(0, True)
                    with dve.Fori(1, NG) as g:
                        group(g, False)
                    y_evacuate(kidx, NG - 1, kk % 2)
                dve.wait_ge(s["y_loaded"], 64 * (b + 1))
                marks = [chain.mark(dve.tensor_tensor(square(y[t]), square(y[t]), swapped(yt[t]), ALU.add))
                         for t in range(2)]
                for t in range(2):
                    chain.wait(marks[t])
                    ins = dve.scalar_tensor_tensor(out=y[t], in0=u[t], scalar=skip_sum[t][:, :], in1=y[t],
                                                   op0=ALU.mult, op1=ALU.add)
                ins.then_inc(s["y_summed"], 1)
                dve.wait_ge(s["y_summed"], b + 1)
                for c in range(NPC):
                    dve.wait_ge(s["ln_mean"], b * NPC + c + 1)
                    for t in range(2):
                        x = y[t][:, piece(c)]
                        ins = dve.tensor_tensor(x, x, bank(c % 2, P_OF[t]), ALU.subtract)
                    ins.then_inc(s["ln_cent"], 1)
                dve.wait_ge(s["ln_cent"], (b + 1) * NPC)
                for c in range(NPC):
                    dve.wait_ge(s["ln_std"], b * NPC + c + 1)
                    chain.link(dve.reciprocal(std[:, piece(c)], std[:, piece(c)]))
                    for t in range(2):
                        x = y[t][:, piece(c)]
                        ins = dve.tensor_tensor(x, x, std[0:P_OF[t], piece(c)], ALU.mult)
                    chain.link(ins)
                    for t in range(2):
                        x = y[t][:, piece(c)]
                        ins = dve.tensor_scalar(x, x, ln_w[t][:, :], ln_b[t][:, :], ALU.mult, ALU.add)
                    chain.link(ins)
                    dve.wait_ge(s["z_act"], b * NPC + c + 1)
                    for t in range(2):
                        x = y[t][:, piece(c)]
                        ins = dve.tensor_tensor(x, x, zg[c % 2][t], ALU.mult)
                    ins.then_inc(s["g_ready"], 1)
                    if c:
                        dve.wait_ge(s["o_mm"], b * NPC + c)
                        x = xres[:, piece(c - 1)]
                        dve.tensor_tensor(x, x, bank((c - 1) % 2, C), ALU.add).then_inc(s["o_ev"], 1)
                dve.wait_ge(s["o_mm"], (b + 1) * NPC)
                x = xres[:, piece(NPC - 1)]
                dve.tensor_tensor(x, x, bank((NPC - 1) % 2, C), ALU.add).then_inc(s["o_ev"], 1)
                dve.wait_ge(s["o_ev"], (b + 1) * NPC)
                group_norm(b, 1, chain)
                dve.wait_ge(s["qkv_ev"], (b + 1) * NPC)
                conv(chain, [(qkv[t], qkv_pads[t], qkv_taps[:, 9 * t:9 * t + 9]) for t in range(3)], "qkv_conv")
                for i in range(2):
                    ins = dve.memset(bank(4 + i), 0.0)
                ins.then_inc(s["pv_zero"], 1)
                dve.memset(v_cols[:, :, HD:HD + 1], 1.0).then_inc(s["v_ones"], 1)
                n_all = 2 * NPC
                for n in range(n_all):
                    dve.wait_ge(s["n_rt"], b * n_all + n + 1)
                    r = nrt[n % 2]
                    chain.link(dve.tensor_scalar(r, r, NORM_EPS, None, ALU.max))
                    chain.link(dve.reciprocal(r, r))
                    x = qkv[n // NPC][:, piece(n % NPC)]
                    dve.tensor_tensor(x, x, r, ALU.mult).then_inc(s["n_mul"], 1)
                dve.wait_ge(s["n_mul"], (b + 1) * n_all)
                for t in range(2):
                    dve.wait_ge(s["a_s1"], b * 2 + t + 1)
                    dve.tensor_tensor(qkv[t], qkv[t], parts[t][0][0:C, :], ALU.subtract).then_inc(s["a_r1"], 1)
                for t in range(2):
                    dve.wait_ge(s["a_r1"], b * 2 + t + 1)
                    dve.wait_ge(s["a_s2"], b * 2 + t + 1)
                    dve.tensor_tensor(parts[t][2][0:C, :], qkv[t], parts[t][1][0:C, :], ALU.subtract)\
                       .then_inc(s["a_s3"], 1)
                for j in range(5):
                    m0, m1 = 4 * j, min(4 * j + 4, MB)
                    dve.wait_ge(s["v_tr"], b * 5 + j + 1)
                    src = ps[:, 2 + j % 2, 0:(m1 - m0) * C].rearrange("p (m d) -> p m d", d=HD)
                    dve.tensor_copy(v_cols[:, m0 * HEADS:m1 * HEADS, 0:HD], src).then_inc(s["v_ev"], 1)

                def finish(hg, n, slot):
                    col = (b * 2 + hg) * NPC + n
                    dve.wait_ge(s["pv_done"], (col + 1) * MB)
                    dve.tensor_copy(att_o, bank(4)).then_inc(s["o_copied"], 1)
                    dve.wait_ge(s["den_done"], col + 1)
                    chain_r = dve.reciprocal(att_r, bank(6))
                    chain_r.then_inc(s["on_ready"], 1)
                    dve.wait_ge(s["on_ready"], col * 2 + 1)
                    dve.tensor_tensor(att_n, att_o, att_r, ALU.mult).then_inc(s["on_ready"], 1)
                    dve.wait_ge(s["pj_done"], col + 1)
                    x = xres[:, bass.ds(n * PC, PC)]
                    dve.tensor_tensor(x, x, bank(7, C), ALU.add).then_inc(s["xo_done"], 1)

                for hg in range(2):
                    with dve.Fori(0, NPC) as n:
                        finish(hg, n, 0)
                chain.end()

        @block.tensor
        def _(pe):
            pe.wait_ge(s["w_loaded"], W_LOADED)

            def group_stats(b, t):
                pe.wait_ge(s["gn_stat"], b * 2 + t + 1)
                pe.matmul(ps[0:C, 7, 0:1], group_mean[:, :], mv[:, 0:1], start=True, stop=True)\
                  .then_inc(s["gn_mean"], 1)
                pe.wait_ge(s["gn_dev"], b * 2 + t + 1)
                pe.matmul(ps[0:C, 6, 0:1], group_mean[:, :], gn[:, 3:4], start=True, stop=True)\
                  .then_inc(s["gn_var"], 1)
                pe.wait_ge(s["xn_ready"], b * 2 + t + 1)

            def broadcast(kidx, g, i, c, cc, slot, first):
                n = kidx * (NG * SPG) + g * SPG + (i * SPT + c)
                pick = pick_channel[:, i * 128:(i + 1) * 128]
                for q, (free, full) in enumerate((("da_ready", "dbc"), ("b_ready", "ubc"))):
                    if not (first and i + c == 0):
                        pe.wait_ge(s[free], n)
                    for j in range(2):
                        col = cc * SC + j * PC
                        ins = pe.matmul(ps[:, 2 * q + j, 0:PC], pick, st[slot][q][:, col:col + PC],
                                        start=True, stop=True)
                    ins.then_inc(s[full], 1)

            def sum_tile(kidx, g, i, first=False):
                pe.wait_ge(s["hc_ready"], (kidx * (NG * TG) + g * TG + (i + 1)) * SPT)
                if i == 0 and not first:
                    pe.wait_ge(s["y_ev"], kidx * NG + g)
                for hh in range(2):
                    for j in range(4):
                        col = j * QL + hh * HQ
                        ins = pe.matmul(ps[32 * j:32 * j + 32, 4 + hh, 0:HQ], sum_states[:, 32 * i:32 * i + 32],
                                        hc[i % 2][:, col:col + HQ], start=(i == 0), stop=(i == TG - 1))
                ins.then_inc(s["hc_used"], 1)

            with pe.Fori(0, NB) as b:
                group_stats(b, 0)
                for c in range(NPC):
                    if c >= 2:
                        pe.wait_ge(s["inp_ev"], b * NPC + c - 1)
                    pe.matmul(bank(2 * (c % 2)), in_proj[:, 0:DA], xn[:, piece(c)], start=True, stop=True)
                    pe.matmul(bank(2 * (c % 2) + 1, DB), in_proj[:, DA:DI], xn[:, piece(c)],
                              start=True, stop=True).then_inc(s["inp_mm"], 1)
                pe.wait_ge(s["u_ready"], b + 1)
                for c in range(NPC):
                    if c >= 2:
                        pe.wait_ge(s["xd_ev"], b * NPC + c - 1)
                    for w, bk in ((xdt, 2 * (c % 2)), (xbc, 2 * (c % 2) + 1)):
                        for t in range(2):
                            for k in range(K):
                                ins = pe.matmul(ps[32 * k:32 * k + 32, bk, 0:PC], w[t][:, 32 * k:32 * k + 32],
                                                (ut if k % 2 else u)[t][:, piece(c)], start=(t == 0), stop=(t == 1))
                    ins.then_inc(s["xd_mm"], 1)
                pe.wait_ge(s["xd_ev"], (b + 1) * NPC)
                for kk in range(K):
                    kidx, k = b * K + kk, KS_ORDER[kk]
                    for t in range(2):
                        for c in range(NPC):
                            m = t * NPC + c
                            if m >= 4:
                                pe.wait_ge(s["dt_ev"], kidx * 2 * NPC + m - 3)
                            col = k * DI + t * DA
                            pe.matmul(bank(m % 4, P_OF[t]), dt_proj[:, col:col + P_OF[t]], dts[:, piece(c)],
                                      start=True, stop=True).then_inc(s["dt_mm"], 1)
                    pe.wait_ge(s["dt_ev"], (kidx + 1) * 2 * NPC)

                    def chunk(c):
                        return SPT - 1 - c if k >= 2 else c

                    def group(g, first, slot):
                        pe.wait_ge(st_loaded[slot], kidx * (32 * NG // 2) + (g - slot) * 16 + 32)
                        for i in range(TG):
                            for c in range(SPT):
                                broadcast(kidx, g, i, c, chunk(c), slot, first)
                            if i:
                                sum_tile(kidx, g, i - 1, first)
                            elif not first:
                                sum_tile(kidx, g - 1, TG - 1)

                    group(0, True, 0)
                    group(1, False, 1)
                    with pe.Fori(1, NG // 2) as pair:
                        g = pair * 2
                        group(g, False, 0)
                        group(g + 1, False, 1)
                    sum_tile(kidx, NG - 1, TG - 1)
                pe.wait_ge(s["y_summed"], b + 1)
                for c in range(NPC + 1):
                    if c < NPC:
                        if c >= 2:
                            pe.wait_ge(s["ln_cent"], b * NPC + c - 1)
                        pe.matmul(bank(c % 2), mean192[:, :], y[0][:, piece(c)], start=True, stop=False)
                        pe.matmul(bank(c % 2), mean192[0:DB, :], y[1][:, piece(c)], start=False, stop=True)\
                          .then_inc(s["ln_mean"], 1)
                    if c:
                        pe.wait_ge(s["ln_sq"], b * NPC + c)
                        if c >= 3:
                            pe.wait_ge(s["ln_std"], b * NPC + c - 2)
                        j = (c - 1) % 2
                        pe.matmul(bank(2 + j), mean192[:, :], sq[j][0], start=True, stop=False)
                        pe.matmul(bank(2 + j), mean192[0:DB, :], sq[j][1], start=False, stop=True)\
                          .then_inc(s["ln_var"], 1)
                pe.wait_ge(s["ln_cent"], (b + 1) * NPC)
                for c in range(NPC + 1):
                    if c < NPC:
                        if c >= 2:
                            pe.wait_ge(s["z_act"], b * NPC + c - 1)
                        for t in range(2):
                            col = DI + t * DA
                            ins = pe.matmul(bank(4 + 2 * (c % 2) + t, P_OF[t]), in_proj[:, col:col + P_OF[t]],
                                            xn[:, piece(c)], start=True, stop=True)
                        ins.then_inc(s["z_mm"], 1)
                    if c:
                        pe.wait_ge(s["g_ready"], b * NPC + c)
                        if c >= 3:
                            pe.wait_ge(s["o_ev"], b * NPC + c - 2)
                        j = (c - 1) % 2
                        pe.matmul(bank(j, C), out_proj[0][:, :], y[0][:, piece(c - 1)], start=True, stop=False)
                        pe.matmul(bank(j, C), out_proj[1][:, :], y[1][:, piece(c - 1)], start=False, stop=True)\
                          .then_inc(s["o_mm"], 1)
                group_stats(b, 1)
                for c in range(NPC):
                    if c >= 2:
                        pe.wait_ge(s["qkv_ev"], b * NPC + c - 1)
                    for t in range(3):
                        ins = pe.matmul(bank(3 * (c % 2) + t, C), qkv_w[:, t * C:(t + 1) * C], xn[:, piece(c)],
                                        start=True, stop=True)
                    ins.then_inc(s["qkv_mm"], 1)
                pe.wait_ge(s["qkv_conv"], b + 1)
                n_all = 2 * NPC
                for n in range(n_all):
                    pe.wait_ge(s["n_sq"], b * n_all + n + 1)
                    if n >= 2:
                        pe.wait_ge(s["n_rt"], b * n_all + n - 1)
                    pe.matmul(bank(n % 2, C), head_ones[:, :], nsq[n % 2], start=True, stop=True)\
                      .then_inc(s["n_ss"], 1)
                for j in range(5):
                    if j >= 2:
                        pe.wait_ge(s["v_ev"], b * 5 + j - 1)
                    for m in range(4 * j, min(4 * j + 4, MB)):
                        col = (m % 4) * C
                        ins = pe.transpose(ps[:, 2 + j % 2, col:col + C], qkv[2][:, m * 128:(m + 1) * 128],
                                           ident[:, :])
                    ins.then_inc(s["v_tr"], 1)
                pe.wait_ge(s["v_ev"], (b + 1) * 5)
                pe.wait_ge(s["v_ones"], b + 1)
                pe.wait_ge(s["pv_zero"], b + 1)
                pe.wait_ge(s["n_rt"], (b + 1) * n_all)

                def scores(hg, n, slot, m, first):
                    col = ((b * 2 + hg) * NPC + n) * (MB * HG) + m * HG
                    for h in range(HG):
                        if not (first and m == 0):
                            pe.wait_ge(s["exp_done"], col + (h - HG + 1))
                        pe.matmul(bank(h), k_parts[:, h, m * 128:(m + 1) * 128], q_parts[slot][:, h, :],
                                  start=True, stop=True).then_inc(s["s_done"], 1)

                def values(hg, n, m, first):
                    col = (b * 2 + hg) * NPC + n
                    pe.wait_ge(s["exp_done"], col * (MB * HG) + (m + 1) * HG)
                    if m == 0 and not (hg == 0 and first):
                        pe.wait_ge(s["o_copied"], col)
                    for h in range(HG):
                        ins = pe.matmul(ps[32 * h:32 * h + 13, 4, 0:PC], v_cols[:, m * HEADS + hg * HG + h, :],
                                        probs[(m % 2) * HG + h], start=(m == 0), stop=(m == MB - 1))
                    ins.then_inc(s["pv_done"], 1)

                def denominators(hg, n):
                    col = (b * 2 + hg) * NPC + n
                    pe.wait_ge(s["o_copied"], col + 1)
                    pe.matmul(bank(6), pick_den[:, :], att_o, start=True, stop=True).then_inc(s["den_done"], 1)

                def project(hg, n):
                    col = (b * 2 + hg) * NPC + n
                    pe.wait_ge(s["on_ready"], col * 2 + 2)
                    pe.matmul(bank(7, C), proj_w[:, hg * C:(hg + 1) * C], att_n, start=True, stop=True)\
                      .then_inc(s["pj_done"], 1)

                def columns(hg, n, slot, first):
                    pe.wait_ge(qs_loaded[slot], (b * 2 + hg) * (3 * 16 * TERMS) + (n - slot) * (8 * TERMS)
                               + 16 * TERMS)
                    for m in range(MB):
                        scores(hg, n, slot, m, first)
                        if m:
                            values(hg, n, m - 1, first)
                        if m == 3 and not first:
                            denominators(hg, n - 1)
                        if m == 9 and not first:
                            project(hg, n - 1)
                    values(hg, n, MB - 1, first)

                for hg in range(2):
                    pe.wait_ge(s["ks_loaded"], (b * 2 + hg + 1) * 16 * TERMS)
                    columns(hg, 0, 0, True)
                    columns(hg, 1, 1, False)
                    with pe.Fori(1, NPC // 2) as pair:
                        n = pair * 2
                        columns(hg, n, 0, False)
                        columns(hg, n + 1, 1, False)
                    denominators(hg, NPC - 1)
                    project(hg, NPC - 1)
                pe.wait_ge(s["xo_done"], (b + 1) * 2 * NPC)


def kernel(**inputs):
    import ml_dtypes
    import numpy as np
    import concourse.bacc as bacc
    from concourse.bass_utils import run_bass_kernel_spmd

    x = np.asarray(inputs["x"])
    NB = x.shape[0]
    w = {n.replace("L0_conv_", "").replace("L1_conv_", "l1_"): np.asarray(v) for n, v in inputs.items()}

    def cols(m):
        m = np.ascontiguousarray(m)
        return m[0:DA], m[DA:DI]

    f32 = np.float32
    arrays = {"x": x.reshape(NB, C, L), "in_projT": w["in_proj_w"].T}
    arrays["taps_a"], arrays["taps_b"] = cols(w["conv_w"].reshape(DI, 9))
    arrays["conv_b_a"], arrays["conv_b_b"] = cols(w["conv_b"].reshape(DI, 1))
    xdt, xbc = np.zeros((DI, K, 32), f32), np.zeros((DI, K, 32), f32)
    dt_proj = np.zeros((128, K, DI), f32)
    for k in range(K):
        xdt[:, k, 0:R] = w["x_proj_w"][k, 0:R].T
        xbc[:, k, :] = w["x_proj_w"][k, R:R + 2 * N].T
        dt_proj[32 * k:32 * k + R, k, :] = w["dt_w"][k].T
    arrays["xdt_a"], arrays["xdt_b"] = cols(xdt.reshape(DI, K * 32))
    arrays["xbc_a"], arrays["xbc_b"] = cols(xbc.reshape(DI, K * 32))
    arrays["dt_projT"] = dt_proj.reshape(128, K * DI)
    arrays["dt_b_a"], arrays["dt_b_b"] = cols(w["dt_b"].T)
    arrays["a_logs"] = w["A_logs"].reshape(K * NG * TG, 128).T
    arrays["ds_a"], arrays["ds_b"] = cols(w["Ds"].reshape(K, DI).T)
    arrays["ln_w_a"], arrays["ln_w_b"] = cols(w["ln_w"].reshape(DI, 1))
    arrays["ln_b_a"], arrays["ln_b_b"] = cols(w["ln_b"].reshape(DI, 1))
    arrays["out_proj_a"], arrays["out_proj_b"] = cols(w["out_proj_w"].T)
    arrays["qkv_wT"] = w["l1_w_qkv"].T
    arrays["qkv_taps"] = w["l1_w_dw"].reshape(3, C, 9).transpose(1, 0, 2).reshape(C, 27)
    proj = np.zeros((128, 2, C), f32)
    for h in range(HEADS):
        r = 32 * (h % HG)
        proj[r:r + HD, h // HG, :] = w["l1_w_proj"][:, h * HD:(h + 1) * HD].T
    arrays["proj_wT"] = proj.reshape(128, 2 * C)
    pick = np.zeros((3, 32, TG, 8, N), f32)
    states = np.zeros((8, N, TG, 32), f32)
    for i in range(TG):
        for d in range(8):
            pick[:, 8 * i + d, i, d, :] = 1
            states[d, :, i, 8 * i + d] = 1
    arrays["pick_channel"] = pick.reshape(96, TG * 128).astype(ml_dtypes.bfloat16)
    arrays["sum_states"] = states.reshape(128, TG * 32)
    per = C // 32
    arrays["group_mean"] = np.kron(np.eye(32), np.full((per, per), 1.0 / per)).astype(f32)
    arrays["mean192"] = np.full((128, 128), 1.0 / DI, f32)
    arrays["head_ones"] = np.kron(np.eye(HEADS), np.ones((HD, HD))).astype(f32)
    arrays["ident"] = np.eye(C, dtype=f32)
    den = np.zeros((128, 128), f32)
    for h in range(HG):
        den[32 * h + HD, 32 * h:32 * h + 32] = 1
    arrays["pick_den"] = den
    arrays = {f"in_{n}": np.ascontiguousarray(v) for n, v in arrays.items()}

    nc = bacc.Bacc("TRN2", target_bir_lowering=False, num_devices=1)
    aps = {n[3:]: nc.dram_tensor(n, v.shape, mybir.dt.from_np(v.dtype), kind="ExternalInput").ap()
           for n, v in arrays.items()}
    out = nc.dram_tensor("out", (NB, C, L), F32, kind="ExternalOutput").ap()
    build(nc, NB, aps, out)
    got = run_bass_kernel_spmd(nc, [arrays], core_ids=[0]).results[0]["out"]
    return got.reshape(NB, C, H, W)
```

```python
from contextlib import ExitStack

import concourse.bass as bass
from concourse import mybir

F32 = mybir.dt.float32
BF16 = mybir.dt.bfloat16
ALU = mybir.AluOpType
ACT = mybir.ActivationFunctionType

C, H, W = 96, 48, 48
L = H * W
HL = L // 2
DI, DA, DB = 192, 128, 64
K, N, R = 4, 16, 12
PC = 384
NPC = L // PC
SC = 2 * PC
NG = DI // 32
TG = 4
SPT = L // SC
SPG = TG * SPT
DSTEPS = NG * SPG
BODY = 2 * SPG
NS = NG // 2
QL = L // 4
HQ = QL // 2
HEADS, HD = 8, 12
HG = 4
MB = L // 128
TERMS = 9
KS_ORDER = (0, 2, 1, 3)
SCALE = float(HD) ** -0.5
GN_EPS, LN_EPS, NORM_EPS = 1e-5, 1e-5, 1e-12
PADW = W + 2
PADL = (H + 2) * PADW
PAD2 = (H // 2 + 2) * PADW
LN_EXP_TABLES = "natural_log_exp_and_others"
DVE_CHAIN, ACT_CHAIN = 89, 2

PIECES = MB * HG
PER_STEP = PIECES // BODY
STRETCHES = K * NS
COPY_O, DEN_MM, DEN_LN, DEN_EXP, DIVIDE, PROJ_MM, PROJ_EV, RESIDUAL = 1, 2, 2, 3, 5, 7, 7, 8

JOBS = 3
JOB_START = (3, 10, 14)
ACT_STAGES = {"abs": 0, "relu": 0, "exp": 1, "ln": 2, "d0": 4, "u0": 5, "d1": 6, "u1": 7}
DVE_STAGES = {"add": 3, "times_u": 4, "d_rest": 5, "u_rest": 6, "d2": 7, "u2": 8}
ACT_JOBS = sorted((JOB_START[j] + t, j, i, n) for j in range(JOBS) for i, (n, t) in enumerate(ACT_STAGES.items()))
DVE_JOBS = sorted((JOB_START[j] + t, j, i, n) for j in range(JOBS) for i, (n, t) in enumerate(DVE_STAGES.items()))
NA, ND = len(ACT_JOBS), len(DVE_JOBS)


def place(jobs, j, name):
    return 1 + next(i for i, x in enumerate(jobs) if x[1] == j and x[3] == name)


def ring_slots(att, prev, prep):
    order = []
    for t in range(BODY):
        scores = [("score", PER_STEP * t + i) for i in range(PER_STEP)] if att else []
        order += scores[:2]
        if prev and t == DEN_MM:
            order.append(("den", 0))
        if prev and t == PROJ_MM:
            order.append(("proj", 0))
        if prep and t in JOB_START:
            order.append(("job", JOB_START.index(t)))
        order += scores[2:]
    return {x: 5 + i % 2 for i, x in enumerate(order)}, order


class Chain:

    def __init__(self, engine, sem, b, count):
        self.engine, self.sem, self.base, self.count, self.n = engine, sem, b * count, count, 0

    def mark(self, ins):
        ins.then_inc(self.sem, 1)
        self.n += 1
        return self.n

    def wait(self, n=None):
        self.engine.wait_ge(self.sem, self.base + (self.n if n is None else n))

    def link(self, ins):
        self.mark(ins)
        self.wait()

    def end(self):
        assert self.n == self.count, (self.n, self.count)


def build(nc, NB, a, out):
    ctx = ExitStack()
    with ctx:
        def sb(name, shape, dt=F32):
            return ctx.enter_context(nc.sbuf_tensor(name, shape, dt))

        def sem(name):
            return ctx.enter_context(nc.semaphore(name))

        in_proj = sb("in_proj", [C, 2 * DI])
        taps = [sb("taps_a", [128, 9]), sb("taps_b", [128, 9])]
        conv_bias = [sb("conv_bias_a", [128, 1]), sb("conv_bias_b", [128, 1])]
        xdt = [sb("xdt_a", [128, K * 32]), sb("xdt_b", [128, K * 32])]
        xbc = [sb("xbc_a", [128, K * 32]), sb("xbc_b", [128, K * 32])]
        dt_proj = [sb("dt_proj_a", [128, K * DA]), sb("dt_proj_b", [128, K * 192])]
        dt_bias = [sb("dt_bias_a", [128, K]), sb("dt_bias_b", [128, K])]
        a_cols = sb("a_cols", [128, K * NG * TG])
        skip = [sb("skip_a", [128, K]), sb("skip_b", [128, K])]
        skip_sum = [sb("skip_sum_a", [128, 1]), sb("skip_sum_b", [128, 1])]
        ln_w = [sb("ln_w_a", [128, 1]), sb("ln_w_b", [128, 1])]
        ln_b = [sb("ln_b_a", [128, 1]), sb("ln_b_b", [128, 1])]
        out_proj = [sb("out_proj_a", [128, C]), sb("out_proj_b", [128, C])]
        qkv_w = sb("qkv_w", [C, 3 * C])
        qkv_taps = sb("qkv_taps", [C, 27])
        proj_w = sb("proj_w", [128, 2 * C])
        pick_channel = sb("pick_channel", [96, TG * 128], BF16)
        sum_states = sb("sum_states", [128, TG * 32])
        group_mean = sb("group_mean", [C, C])
        mean192 = sb("mean192", [128, 128])
        head_ones = sb("head_ones", [C, C])
        ident = sb("ident", [C, C])
        pick_den = sb("pick_den", [128, 128])
        gn_eps = sb("gn_eps", [128, 1])

        xres = sb("xres", [C, L])
        xn = sb("xn", [C, L])
        u_buf = sb("u_buf", [128, 2 * L])
        dts = sb("dts", [128, L])
        rep = sb("rep", [128, 2 * L])
        st_buf = sb("st_buf", [128, 2 * L])
        rings = sb("rings", [128, 9 * PC])
        hc_buf = sb("hc_buf", [128, 2 * L])
        y_acc = sb("y_acc", [128, NG * QL])
        job_f = sb("job_f", [128, 4 * PC])
        job_p = sb("job_p", [128, 2 * 6 * PC], BF16)
        kp_buf = sb("kp_buf", [TERMS * HD, HG * L], BF16)
        qp_buf = sb("qp_buf", [TERMS * HD, NS * HG * PC], BF16)
        probs_buf = sb("probs_buf", [128, 2 * HG * PC])
        v_buf = sb("v_buf", [128, MB * HEADS * 13])
        att_buf = sb("att_buf", [128, 3 * PC])
        stats = sb("stats", [C, NPC * 6])
        mv = sb("mv", [C, 2])
        gn = sb("gn", [C, 6])

        u = [u_buf[:, 0:L], u_buf[:, L:L + HL]]
        ut_b = u_buf[:, L + HL:2 * L]
        xin = st_buf[0:C, L:2 * L]
        bc_stage = st_buf[:, 0:L]
        pads = [hc_buf[:, 0:PADL], rings[:, 0:PAD2]]
        b_rep, c_rep = rep[:, 0:L], rep[:, L:2 * L]
        jobs_f = [[job_f[:, (2 * i + q) * PC:(2 * i + q + 1) * PC] for q in range(2)] for i in range(2)]
        jobs_p = [job_p[:, 6 * i * PC:6 * (i + 1) * PC].rearrange("p (r l) -> p r l", r=6) for i in range(2)]
        st = [[st_buf[:, :].bitcast(BF16)[0:96, (2 * i + q) * L:(2 * i + q + 1) * L] for q in range(2)]
              for i in range(2)]
        da_ring = [rings[:, i * SC:(i + 1) * SC] for i in range(2)]
        b_ring = [rings[:, (4 + i) * PC:(5 + i) * PC] for i in range(3)]
        h_ring = [rings[:, (7 + i) * PC:(8 + i) * PC] for i in range(2)]
        hc = [hc_buf[:, i * L:(i + 1) * L] for i in range(2)]
        y = [st_buf[:, 0:L], st_buf[:, L:L + HL]]
        yt = [hc_buf[:, 0:L], hc_buf[:, L:2 * L]]
        rstd = y_acc[:, 0:L]
        sq = [[rings[:, (2 * i + t) * PC:(2 * i + t + 1) * PC] for t in range(2)] for i in range(2)]
        zg = [[rep[:, (2 * i + t) * PC:(2 * i + t + 1) * PC] for t in range(2)] for i in range(2)]
        qkv_pads = [u_buf[0:C, 0:PADL], hc_buf[0:C, 0:PADL], st_buf[0:C, 0:PADL]]
        qkv = [dts[0:C, :], rep[0:C, 0:L], rep[0:C, L:2 * L]]
        nsq = [rings[0:C, i * PC:(i + 1) * PC] for i in range(2)]
        nrt = [rings[0:C, (2 + i) * PC:(3 + i) * PC] for i in range(2)]
        half = [hc_buf[:, :].bitcast(BF16), st_buf[:, :].bitcast(BF16)]
        parts = [[half[q][0:C, r * L:(r + 1) * L] for r in range(3)] for q in range(2)]
        k_parts = kp_buf[:, :].rearrange("p (h l) -> p h l", h=HG)
        q_ring = qp_buf[:, :].rearrange("p (s h l) -> p s h l", s=NS, h=HG)
        probs = [probs_buf[:, i * PC:(i + 1) * PC] for i in range(2 * HG)]
        v_cols = v_buf[:, :].rearrange("p (m d) -> p m d", d=13)
        att_o, att_r, att_n = (att_buf[:, i * PC:(i + 1) * PC] for i in range(3))

        ps = ctx.enter_context(nc.psum_tensor("ps", [128, 8, 512], F32))
        BANK_U, BANK_Y, BANK_PV = 2, 3, 7

        bc_dram = nc.dram_tensor("bc_scratch", [128, L], F32).ap()
        part_dram = nc.dram_tensor("part_scratch", [2, NG, 6, 32, L], BF16).ap()
        y_dram = nc.dram_tensor("y_scratch", [2, DI, L], F32).ap()
        qk_dram = nc.dram_tensor("qk_scratch", [2, 3, C, L], BF16).ap()

        names = """w_loaded const_set eps_set skip_summed x_loaded xr_loaded gn_stat gn_mean gn_dev gn_var
            gn_std xn_ready inp_mm inp_ev pads_zero conv_done u_ready xd_mm xd_ev bc_stored
            dt_mm job_act job_dve dbc ubc da_ready b_ready h_ready hc_ready hc_used y_ev y_stored y_loaded
            y_summed ln_mean ln_cent ln_sq ln_var ln_log ln_rstd z_mm z_act g_ready o_mm o_ev
            qkv_mm qkv_ev qkv_zero qkv_conv n_sq n_ss n_rt n_mul a_s1 a_r1 a_s2 a_s3 a_stored
            v_tr v_ev v_ones pv_zero qs_loaded s_done exp_done pv_done o_copied den_done den_act on_ready
            pj_done pj_ev xo_done out_stored dve_chain act_chain""".split()
        s = {n: sem(n) for n in names}
        passed = {e.engine: sem(f"passed_{n}") for n, e in (("act", nc.scalar), ("dve", nc.vector),
                                                            ("pool", nc.gpsimd), ("sp", nc.sync))}
        part_stored = [sem(f"part_stored{i}") for i in range(2)]
        st_loaded = [sem(f"st_loaded{i}") for i in range(2)]
        rep_loaded = [sem(f"rep_loaded{i}") for i in range(SPT)]
        ks_loaded = [sem(f"ks_loaded{i}") for i in range(SPT)]

        def piece(c):
            return slice(c * PC, (c + 1) * PC)

        def bank(i, p=128, n=PC):
            return ps[0:p, i, 0:n]

        def rows(c):
            hf = c // (NPC // 2)
            return slice(64 * hf, 64 * hf + 64), piece(c % (NPC // 2))

        def square(ap):
            return ap.rearrange("p (h w) -> p h w", w=W)

        def swapped(ap):
            return ap.rearrange("p (h w) -> p w h", w=W)

        def window(pad, tap, n=H):
            dy, dx = divmod(tap, 3)
            return pad.rearrange("p (h w) -> p h w", w=PADW)[:, dy:dy + n, dx:dx + W]

        def pad_rows(pad, r, n=PC // W):
            return pad.rearrange("p (h w) -> p h w", w=PADW)[:, r:r + n, 1:1 + W]

        def natural(kk, v):
            return 2 * SPT - 1 - v if KS_ORDER[kk] >= 2 else v

        loads = [(in_proj, "in_projT"), (taps[0], "taps_a"), (taps[1], "taps_b"),
                 (conv_bias[0], "conv_b_a"), (conv_bias[1], "conv_b_b"), (xdt[0], "xdt_a"), (xdt[1], "xdt_b"),
                 (xbc[0], "xbc_a"), (xbc[1], "xbc_b"), (dt_proj[0], "dt_proj_a"), (dt_proj[1], "dt_proj_b"),
                 (dt_bias[0], "dt_b_a"), (dt_bias[1], "dt_b_b"), (a_cols, "a_logs"), (skip[0], "ds_a"),
                 (skip[1], "ds_b"), (ln_w[0], "ln_w_a"), (ln_w[1], "ln_w_b"), (ln_b[0], "ln_b_a"),
                 (ln_b[1], "ln_b_b"), (out_proj[0], "out_proj_a"), (out_proj[1], "out_proj_b"),
                 (qkv_w, "qkv_wT"), (qkv_taps, "qkv_taps"), (proj_w, "proj_wT"),
                 (pick_channel, "pick_channel"), (sum_states, "sum_states"), (group_mean, "group_mean"),
                 (mean192, "mean192"), (head_ones, "head_ones"), (ident, "ident"), (pick_den, "pick_den")]
        W_LOADED = 16 * len(loads)

        def apart(engine):
            engine.sem_inc(passed[engine.engine], 1)

        def batches(engine, front, directions, back, attention):
            front(0)
            directions(0, None)
            back(0)
            if NB > 1:
                with engine.Fori(1, NB) as b:
                    front(b)
                    directions(b, b - 1)
                    back(b)
            attention(NB - 1)

        def stretches(engine, body):
            body(0, True)
            with engine.Fori(1, NS) as q:
                body(q, False)

        block = ctx.enter_context(nc.Block())

        @block.sync
        def _(sp):
            for dst, name in loads:
                sp.dma_start(dst[:, :], a[name]).then_inc(s["w_loaded"], 16)

            def load_st(kk, g):
                for q in range(2):
                    src = part_dram[kk % 2, g, 3 * q:3 * q + 3, :, :].rearrange("s d l -> (s d) l")
                    sp.dma_start(st[g % 2][q], src).then_inc(st_loaded[g % 2], 16)

            def load_first(b, kk):
                k = KS_ORDER[kk]
                for c in range(SPT):
                    cc = SPT - 1 - c if k >= 2 else c
                    for j, dst in enumerate((b_rep, c_rep)):
                        row = bc_dram[32 * k + N * j:32 * k + N * (j + 1), cc * SC:(cc + 1) * SC]
                        sp.dma_start(dst[:, cc * SC:(cc + 1) * SC],
                                     bass.AP(row.tensor, row.offset, [[0, 8], [L, N], [1, SC]]))\
                          .then_inc(rep_loaded[cc], 16)
                    if c == 0:
                        kidx = b * K + kk
                        sp.wait_ge(part_stored[0], (kidx + 1) * NS * 128)
                        apart(sp)
                        sp.wait_ge(part_stored[1], (kidx + 1) * NS * 64)
                        for g in range(2):
                            load_st(kk, g)

            def store_job(b, kk, q, j):
                BI = (b * K + kk) * NS + q
                sp.wait_ge(s["job_dve"], BI * ND + place(DVE_JOBS, j, "u2"))
                for g in range(4):
                    src = jobs_p[j % 2][32 * g:32 * g + 32, :, :]
                    if j < 2:
                        group, col = g, (2 * q + j) * PC
                    else:
                        group, col = 4 + g % 2, (g // 2) * HL + q * PC
                    dst = part_dram[kk % 2, group, :, :, col:col + PC].rearrange("r d l -> d r l")
                    sp.dma_start(dst, src).then_inc(part_stored[j % 2], 16)

            def load_keys(hg, c):
                for t in range(TERMS):
                    src = qk_dram[1, t % 3, hg * HG * HD:(hg + 1) * HG * HD, c * SC:(c + 1) * SC]\
                        .rearrange("(h d) l -> d h l", d=HD)
                    sp.dma_start(k_parts[t * HD:(t + 1) * HD, :, c * SC:(c + 1) * SC], src)\
                      .then_inc(ks_loaded[c], 16)

            def load_queries(i):
                hg, n = divmod(i, NPC)
                for t in range(TERMS):
                    src = qk_dram[0, t // 3, hg * HG * HD:(hg + 1) * HG * HD, piece(n)]\
                        .rearrange("(h d) l -> d h l", d=HD)
                    sp.dma_start(q_ring[t * HD:(t + 1) * HD, i % NS, :, :], src).then_inc(s["qs_loaded"], 16)

            def next_keys(ab, i, c):
                sp.wait_ge(s["s_done"], (ab * STRETCHES + i) * PIECES + (c + 1) * (PIECES // SPT))
                load_keys(1, c)

            def stretch(b, kk, q, ab):
                kidx, i = b * K + kk, kk * NS + q
                prep = kk + 1 < K and b is not None
                if ab is not None and i + 1 < STRETCHES:
                    sp.wait_ge(s["s_done"], (ab * STRETCHES + i) * PIECES + 1)
                    load_queries(i + 1)
                turn = ab is not None and i + 1 == NPC
                if turn:
                    next_keys(ab, i, 0)
                if prep:
                    store_job(b, kk + 1, q, 0)
                if q + 1 < NS:
                    sp.wait_ge(s["ubc"], (kidx * DSTEPS + q * BODY + SPG) * 2)
                    load_st(kk, 2 * q + 2)
                if turn:
                    next_keys(ab, i, 1)
                if prep:
                    store_job(b, kk + 1, q, 1)
                    store_job(b, kk + 1, q, 2)
                if q + 1 < NS:
                    sp.wait_ge(s["ubc"], (kidx * DSTEPS + (q + 1) * BODY) * 2)
                    load_st(kk, 2 * q + 3)
                if turn:
                    next_keys(ab, i, 2)

            def front(b):
                sp.dma_start(xin, a["x"][bass.ds(b, 1), :, :].rearrange("b c l -> (b c) l"))\
                  .then_inc(s["x_loaded"], 16)
                sp.wait_ge(s["xd_ev"], (b + 1) * NPC)
                apart(sp)
                sp.dma_start(bc_dram, bc_stage).then_inc(s["bc_stored"], 16)
                sp.wait_ge(s["bc_stored"], 16 * (b + 1))
                apart(sp)
                for q in range(NS):
                    for j in range(JOBS):
                        store_job(b, 0, q, j)

            def directions(b, ab):
                for kk in range(K):
                    kidx = b * K + kk
                    if kk:
                        sp.wait_ge(s["hc_ready"], kidx * (2 * DSTEPS))
                    load_first(b, kk)
                    for q in range(NS):
                        stretch(b, kk, q, ab)
                    if kk % 2:
                        sp.wait_ge(s["y_ev"], (kidx + 1) * NG)
                        for j in range(4):
                            dst = y_dram[kk // 2, :, j * QL:(j + 1) * QL].rearrange("(g d) r -> d g r", d=32)
                            src = y_acc[32 * j:32 * j + 32, :].rearrange("p (g r) -> p g r", r=QL)
                            sp.dma_start(dst, src).then_inc(s["y_stored"], 16)
                if ab is not None:
                    store_out(ab)

            def store_out(ab):
                sp.wait_ge(s["xo_done"], (ab + 1) * STRETCHES)
                apart(sp)
                sp.dma_start(out[bass.ds(ab, 1), :, :].rearrange("b c l -> (b c) l"), xres[:, :])\
                  .then_inc(s["out_stored"], 16)
                sp.wait_ge(s["out_stored"], (ab + 1) * 16)
                apart(sp)

            def back(b):
                sp.wait_ge(s["y_stored"], (b + 1) * 128)
                apart(sp)
                sp.dma_start(y[0], y_dram[0, 0:DA, :]).then_inc(s["y_loaded"], 16)
                sp.dma_start(yt[0], y_dram[1, 0:DA, :]).then_inc(s["y_loaded"], 16)
                for hf in range(2):
                    p = slice(64 * hf, 64 * hf + 64)
                    sp.dma_start(y[1][p, :], y_dram[0, DA:DI, hf * HL:(hf + 1) * HL]).then_inc(s["y_loaded"], 16)
                    sp.dma_start(yt[1][p, :], y_dram[1, DA:DI, :]).then_inc(s["y_loaded"], 16)
                sp.dma_start(xres[:, :], a["x"][bass.ds(b, 1), :, :].rearrange("b c l -> (b c) l"))\
                  .then_inc(s["xr_loaded"], 16)
                for t in range(2):
                    sp.wait_ge(s["a_s3"], b * 2 + t + 1)
                    for r in range(3):
                        sp.dma_start(qk_dram[t, r], parts[t][r]).then_inc(s["a_stored"], 16)
                sp.wait_ge(s["a_stored"], (b + 1) * 96)
                apart(sp)
                load_queries(0)
                for c in range(SPT):
                    load_keys(0, c)

            def attention(ab):
                for i in range(STRETCHES):
                    if i + 1 < STRETCHES:
                        sp.wait_ge(s["s_done"], (ab * STRETCHES + i) * PIECES + 1)
                        load_queries(i + 1)
                    if i + 1 == NPC:
                        for c in range(SPT):
                            next_keys(ab, i, c)
                store_out(ab)

            batches(sp, front, directions, back, attention)

        @block.gpsimd
        def _(pool):
            def front(b):
                pool.memset(pads[0], 0.0)
                pool.memset(pads[1], 0.0).then_inc(s["pads_zero"], 1)

            def directions(b, ab):
                for kk in range(K):
                    kidx = b * K + kk

                    def stretch(q, first):
                        for x in range(2 * BODY):
                            X = kidx * (2 * DSTEPS) + q * (2 * BODY) + x
                            tile, v = divmod(x, 2 * SPT)
                            cols = piece(natural(kk, v))
                            if first and tile == 0 and v % 2 == 0:
                                pool.wait_ge(rep_loaded[natural(kk, v) // 2], 32 * (kidx + 1))
                            if v == 0 and not (first and tile < 2):
                                pool.wait_ge(s["hc_used"], kidx * (NG * TG) + q * (2 * TG) + (tile - 1))
                            pool.wait_ge(s["h_ready"], X + 1)
                            pool.tensor_tensor(hc[tile % 2][:, cols], h_ring[x % 2], c_rep[:, cols], ALU.mult)\
                                .then_inc(s["hc_ready"], 1)

                    stretches(pool, stretch)

            def back(b):
                pool.wait_ge(s["y_summed"], b + 1)
                apart(pool)
                pool.memset(qkv_pads[0], 0.0)
                pool.memset(qkv_pads[1], 0.0)
                pool.wait_ge(s["o_mm"], (b + 1) * NPC)
                apart(pool)
                pool.memset(qkv_pads[2], 0.0).then_inc(s["qkv_zero"], 1)
                pool.wait_ge(s["a_stored"], (b + 1) * 96)
                apart(pool)

            batches(pool, front, directions, back, lambda ab: None)

        @block.scalar
        def _(act):
            act.wait_ge(s["w_loaded"], W_LOADED)
            act.activation(a_cols[:, :], a_cols[:, :], ACT.Exp).then_inc(s["const_set"], 1)
            act.wait_ge(s["const_set"], 1)
            act.mul(a_cols[:, :], a_cols[:, :], -1.0).then_inc(s["const_set"], 1)
            act.wait_ge(s["const_set"], 2)
            act.wait_ge(s["eps_set"], 1)

            def group_std(b, t):
                act.wait_ge(s["gn_var"], b * 2 + t + 1)
                act.activation(gn[:, 2:3], ps[0:C, 6, 0:1], ACT.Sqrt, bias=gn_eps[0:C, :]).then_inc(s["gn_std"], 1)

            def job_stage(kidx, k, q, j, name, bk, first):
                BI = kidx * NS + q
                d, m = jobs_f[j % 2]
                bias = dt_bias[j // 2][:, k:k + 1]

                def own(stage):
                    act.wait_ge(s["job_act"], BI * NA + place(ACT_JOBS, j, stage))

                def dve_done(stage):
                    act.wait_ge(s["job_dve"], BI * ND + place(DVE_JOBS, j, stage))

                if name == "abs":
                    if j == 2:
                        act.wait_ge(s["job_dve"], BI * ND + place(DVE_JOBS, 0, "u2"))
                    elif not first:
                        act.wait_ge(s["job_dve"], BI * ND)
                    act.wait_ge(s["dt_mm"], BI * JOBS + j + 1)
                    ins = act.activation(d, bank(bk), ACT.Abs, bias=bias)
                elif name == "relu":
                    ins = act.activation(m, bank(bk), ACT.Relu, bias=bias)
                elif name == "exp":
                    own("abs")
                    ins = act.activation(d, d, ACT.Exp, scale=-1.0)
                elif name == "ln":
                    own("exp")
                    ins = act.activation(d, d, ACT.Ln, bias=1.0)
                elif name in ("d0", "u0"):
                    if j == 2:
                        act.wait_ge(part_stored[0], BI * 128 + 64)
                    elif not first:
                        act.wait_ge(part_stored[j], BI * (128, 64)[j])
                    dve_done("add" if name == "d0" else "times_u")
                    r, src = (0, d) if name == "d0" else (3, m)
                    ins = act.copy(jobs_p[j % 2][:, r, :], src)
                else:
                    dve_done("d_rest" if name == "d1" else "u_rest")
                    r, src = (1, d) if name == "d1" else (4, m)
                    ins = act.copy(jobs_p[j % 2][:, r, :], src)
                ins.then_inc(s["job_act"], 1)

            def stretch(b, kk, q, first, ab, scan=True):
                kidx, k = b * K + kk if scan else None, KS_ORDER[kk]
                att, att_first = ab is not None, first and kk == 0
                prep = scan and kk + 1 < K
                slots, _ = ring_slots(att, att and not att_first, prep)
                if att:
                    f = ab * STRETCHES + kk * NS + q
                for t in range(BODY):
                    if scan:
                        n = kidx * DSTEPS + q * BODY + t
                        if not (first and t < 2):
                            act.wait_ge(s["h_ready"], n * 2 - 2)
                        act.wait_ge(s["dbc"], n + 1)
                        apart(act)
                        act.activation(da_ring[t % 2].rearrange("p (a r) -> p a r", a=2), ps[:, 0:2, 0:PC],
                                       ACT.Exp, scale=a_cols[:, bass.ds(q * (2 * TG) + (k * NG * TG + t // SPT), 1)])\
                            .then_inc(s["da_ready"], 1)
                    for p in range(PER_STEP * t, PER_STEP * (t + 1) if att else 0):
                        m, h = divmod(p, HG)
                        if h == 0 and not (att_first and m < 2):
                            act.wait_ge(s["pv_done"], f * MB + (m - 1))
                        act.wait_ge(s["s_done"], f * PIECES + (p + 1))
                        act.activation(probs[(m % 2) * HG + h], bank(slots["score", p]), ACT.Exp, scale=SCALE)\
                            .then_inc(s["exp_done"], 1)
                    if att and not att_first:
                        leftover(f, t, slots["den", 0], slots["proj", 0])
                    if prep:
                        for when, j, _, name in ACT_JOBS:
                            if when == t:
                                job_stage(kidx + 1, KS_ORDER[kk + 1], q, j, name, slots["job", j], first)

            def leftover(f, t, den_bank, proj_bank):
                if t == DEN_LN:
                    act.wait_ge(s["den_done"], f)
                    act.activation(att_r, bank(den_bank), ACT.Ln).then_inc(s["den_act"], 1)
                if t == DEN_EXP:
                    act.wait_ge(s["den_act"], f * 2 - 1)
                    act.activation(att_r, att_r, ACT.Exp, scale=-1.0).then_inc(s["den_act"], 1)
                if t == PROJ_EV:
                    act.wait_ge(s["pj_done"], f)
                    act.copy(att_r[0:C, :], bank(proj_bank, C)).then_inc(s["pj_ev"], 1)

            def last_leftover(ab):
                for t in (DEN_LN, DEN_EXP, PROJ_EV):
                    leftover((ab + 1) * STRETCHES, t, 5, 6)

            def front(b):
                chain = Chain(act, s["act_chain"], b, ACT_CHAIN)
                group_std(b, 0)
                act.wait_ge(s["pads_zero"], b + 1)
                for c in range(NPC):
                    act.wait_ge(s["inp_mm"], b * NPC + c + 1)
                    act.copy(pad_rows(pads[0], 1 + 8 * c), square(bank(2 * (c % 2))))
                    part, _ = rows(c)
                    src = square(ps[part, 2 * (c % 2) + 1, 0:PC])
                    if c == 2:
                        act.copy(pad_rows(pads[1][64:128, :], 0, 1), src[:, 7:8, :])
                    if c == 3:
                        act.copy(pad_rows(pads[1][0:64, :], H // 2 + 1, 1), src[:, 0:1, :])
                    act.copy(pad_rows(pads[1][part, :], 1 + 8 * (c % 3)), src).then_inc(s["inp_ev"], 1)
                act.wait_ge(s["conv_done"], b + 1)
                chain.mark(act.activation(u[1], u[1], ACT.Gelu, bias=conv_bias[1][:, :]))
                chain.mark(act.activation(u[0], u[0], ACT.Gelu, bias=conv_bias[0][:, :]))
                chain.wait(1)
                for hh in range(2):
                    for wh in range(2):
                        dst = ut_b[64 * wh:64 * wh + 64, :].rearrange("p (w h) -> p w h", h=H)
                        src = square(u[1][64 * hh:64 * hh + 64, :])[:, :, 24 * wh:24 * wh + 24]
                        ins = act.copy(dst[:, :, 24 * hh:24 * hh + 24], src.rearrange("p h w -> p w h"))
                chain.wait()
                ins.then_inc(s["u_ready"], 1)
                for c in range(NPC):
                    act.wait_ge(s["xd_mm"], b * NPC + c + 1)
                    act.copy(dts[:, piece(c)], bank(2 * (c % 2)))
                    act.copy(bc_stage[:, piece(c)], bank(2 * (c % 2) + 1)).then_inc(s["xd_ev"], 1)
                chain.end()
                act.preload_act_table_set(LN_EXP_TABLES)

                def first_jobs(q, first):
                    for when, j, _, name in ACT_JOBS:
                        job_stage(b * K, KS_ORDER[0], q, j, name, 5 + j % 2, first)

                stretches(act, first_jobs)

            def directions(b, ab):
                for kk in range(K):
                    stretches(act, lambda q, first: stretch(b, kk, q, first, ab))
                if ab is not None:
                    last_leftover(ab)

            def back(b):
                for c in range(NPC + 1):
                    if c < NPC:
                        act.wait_ge(s["ln_cent"], b * NPC + c + 1)
                        if c >= 2:
                            act.wait_ge(s["ln_var"], b * NPC + c - 1)
                        part, cols = rows(c)
                        act.activation(sq[c % 2][0], y[0][:, piece(c)], ACT.Square)
                        act.activation(sq[c % 2][1][part, :], y[1][part, cols], ACT.Square).then_inc(s["ln_sq"], 1)
                    if c:
                        act.wait_ge(s["ln_var"], b * NPC + c)
                        act.activation(rstd[:, piece(c - 1)], bank(2 + (c - 1) % 2), ACT.Ln, bias=gn_eps[:, :])\
                            .then_inc(s["ln_log"], 1)
                for j in range(3):
                    act.wait_ge(s["ln_log"], b * NPC + 2 * j + 2)
                    x = rstd[:, 2 * j * PC:(2 * j + 2) * PC]
                    act.activation(x, x, ACT.Exp, scale=-0.5).then_inc(s["ln_rstd"], 1)
                for c in range(NPC):
                    act.wait_ge(s["z_mm"], b * NPC + c + 1)
                    if c >= 2:
                        act.wait_ge(s["g_ready"], b * NPC + c - 1)
                    part, _ = rows(c)
                    j = 4 + 2 * (c % 2)
                    act.activation(zg[c % 2][0], bank(j), ACT.Gelu)
                    act.activation(zg[c % 2][1][part, :], ps[part, j + 1, 0:PC], ACT.Gelu).then_inc(s["z_act"], 1)
                group_std(b, 1)
                act.wait_ge(s["qkv_zero"], b + 1)
                for c in range(NPC):
                    act.wait_ge(s["qkv_mm"], b * NPC + c + 1)
                    for t in range(3):
                        ins = act.copy(pad_rows(qkv_pads[t], 1 + 8 * c), square(bank(3 * (c % 2) + t, C)))
                    ins.then_inc(s["qkv_ev"], 1)
                act.wait_ge(s["qkv_conv"], b + 1)
                n_all = 2 * NPC
                for n in range(n_all + 1):
                    if n < n_all:
                        if n >= 2:
                            act.wait_ge(s["n_ss"], b * n_all + n - 1)
                        act.activation(nsq[n % 2], qkv[n // NPC][:, piece(n % NPC)], ACT.Square)\
                            .then_inc(s["n_sq"], 1)
                    if n:
                        act.wait_ge(s["n_ss"], b * n_all + n)
                        if n >= 3:
                            act.wait_ge(s["n_mul"], b * n_all + n - 2)
                        act.activation(nrt[(n - 1) % 2], bank((n - 1) % 2, C), ACT.Sqrt).then_inc(s["n_rt"], 1)
                for t in range(2):
                    act.wait_ge(s["n_mul"], b * n_all + (t + 1) * NPC)
                    act.copy(parts[t][0], qkv[t]).then_inc(s["a_s1"], 1)
                for t in range(2):
                    act.wait_ge(s["a_r1"], b * 2 + t + 1)
                    act.copy(parts[t][1], qkv[t]).then_inc(s["a_s2"], 1)
                act.preload_act_table_set(LN_EXP_TABLES)

            def attention(ab):
                for kk in range(K):
                    stretches(act, lambda q, first: stretch(None, kk, q, first, ab, False))
                last_leftover(ab)

            batches(act, front, directions, back, attention)

        @block.vector
        def _(dve):
            dve.memset(gn_eps[:, :], GN_EPS).then_inc(s["eps_set"], 1)
            dve.wait_ge(s["w_loaded"], W_LOADED)
            for t in range(2):
                dve.tensor_reduce(skip_sum[t][:, :], skip[t][:, :], mybir.AxisListType.X, ALU.add)\
                   .then_inc(s["skip_summed"], 1)
            dve.wait_ge(s["skip_summed"], 2)

            def group_norm(b, t, chain, x):
                for c in range(NPC):
                    ins = dve.bn_stats(stats[:, 6 * c:6 * c + 6], x[:, piece(c)])
                chain.link(ins)
                apart(dve)
                dve.bn_aggr(mv[:, :], stats[:, :]).then_inc(s["gn_stat"], 1)
                dve.wait_ge(s["gn_mean"], b * 2 + t + 1)
                chain.link(dve.tensor_copy(gn[:, 0:1], ps[0:C, 7, 0:1]))
                chain.link(dve.tensor_tensor(gn[:, 1:2], mv[:, 0:1], gn[:, 0:1], ALU.subtract))
                dve.scalar_tensor_tensor(out=gn[:, 3:4], in0=gn[:, 1:2], scalar=gn[:, 1:2], in1=mv[:, 1:2],
                                         op0=ALU.mult, op1=ALU.add).then_inc(s["gn_dev"], 1)
                dve.wait_ge(s["gn_std"], b * 2 + t + 1)
                chain.link(dve.reciprocal(gn[:, 4:5], gn[:, 2:3]))
                dve.tensor_scalar(xn[:, :], x, gn[:, 0:1], gn[:, 4:5], ALU.subtract, ALU.mult)\
                   .then_inc(s["xn_ready"], 1)

            def conv(chain, work, done):
                marks = {}
                for tap in range(9):
                    for j, (dst, pad, w, n) in enumerate(work):
                        if tap == 0:
                            ins = dve.tensor_scalar(square(dst), window(pad, 0, n), w[:, 0:1], None, ALU.mult)
                        else:
                            chain.wait(marks[j])
                            ins = dve.scalar_tensor_tensor(out=square(dst), in0=window(pad, tap, n),
                                                           scalar=w[:, tap:tap + 1], in1=square(dst),
                                                           op0=ALU.mult, op1=ALU.add)
                        if tap == 8 and j == len(work) - 1:
                            ins.then_inc(s[done], 1)
                        else:
                            marks[j] = chain.mark(ins)
                chain.wait()

            def job_stage(kidx, k, q, j, name):
                BI = kidx * NS + q
                d, m = jobs_f[j % 2]
                P = jobs_p[j % 2]

                def own(stage):
                    dve.wait_ge(s["job_dve"], BI * ND + place(DVE_JOBS, j, stage))

                def act_done(stage):
                    dve.wait_ge(s["job_act"], BI * NA + place(ACT_JOBS, j, stage))

                if name == "add":
                    act_done("ln")
                    ins = dve.tensor_tensor(d, d, m, ALU.add)
                elif name == "times_u":
                    own("add")
                    if j == 2:
                        x = (ut_b if k % 2 else u[1])[:, bass.ds(q * PC, PC)]
                        ins = dve.tensor_tensor(m, d, x, ALU.mult)
                    elif k % 2:
                        x = swapped(u[0])[:, bass.ds(q * 16 + 8 * j, 8), :]
                        ins = dve.tensor_tensor(square(m), square(d), x, ALU.mult)
                    else:
                        ins = dve.tensor_tensor(m, d, u[0][:, bass.ds(q * (2 * PC) + j * PC, PC)], ALU.mult)
                elif name == "d_rest":
                    act_done("d0")
                    own("times_u")
                    ins = dve.tensor_tensor(d, d, P[:, 0, :], ALU.subtract)
                elif name == "u_rest":
                    act_done("u0")
                    ins = dve.tensor_tensor(m, m, P[:, 3, :], ALU.subtract)
                elif name == "d2":
                    act_done("d1")
                    ins = dve.tensor_tensor(P[:, 2, :], d, P[:, 1, :], ALU.subtract)
                else:
                    act_done("u1")
                    ins = dve.tensor_tensor(P[:, 5, :], m, P[:, 4, :], ALU.subtract)
                ins.then_inc(s["job_dve"], 1)

            def mult_b(kidx, kk, q, x, first):
                X = kidx * (2 * DSTEPS) + q * (2 * BODY) + x
                v = natural(kk, x % (2 * SPT))
                if first and x < 2 * SPT and x % 2 == 0:
                    dve.wait_ge(rep_loaded[v // 2], 32 * (kidx + 1))
                if not (first and x < 3):
                    dve.wait_ge(s["h_ready"], X - 2)
                dve.wait_ge(s["ubc"], X + 1)
                dve.tensor_tensor(b_ring[x % 3], bank(BANK_U), b_rep[:, piece(v)], ALU.mult)\
                   .then_inc(s["b_ready"], 1)

            def scan_half(kidx, kk, q, x, first):
                X = kidx * (2 * DSTEPS) + q * (2 * BODY) + x
                back = KS_ORDER[kk] >= 2
                v = natural(kk, x % (2 * SPT))
                if x % 2 == 0:
                    dve.wait_ge(s["da_ready"], kidx * DSTEPS + q * BODY + (x // 2 + 1))
                if not (first and x < 2):
                    dve.wait_ge(s["hc_ready"], X - 1)
                if not (first and x == 0):
                    dve.wait_ge(s["h_ready"], X)
                dve.wait_ge(s["b_ready"], X + 1)
                init = 0.0
                if x % (2 * SPT):
                    prev = h_ring[(x + 1) % 2]
                    init = prev[:, 0:1] if back else prev[:, PC - 1:PC]
                o, d0, d1 = h_ring[x % 2], da_ring[x // 2 % 2][:, piece(v % 2)], b_ring[x % 3]
                if back:
                    o, d0, d1 = o[:, ::-1], d0[:, ::-1], d1[:, ::-1]
                dve.tensor_tensor_scan(o, d0, d1, init, ALU.mult, ALU.add).then_inc(s["h_ready"], 1)

            def y_evacuate(kidx, g, add):
                dve.wait_ge(s["hc_used"], (kidx * NG + g + 1) * TG)
                dst = y_acc[:, bass.ds(g * QL, QL)].rearrange("p (a r) -> p a r", a=2)
                src = ps[:, BANK_Y:BANK_Y + 2, 0:HQ]
                if add:
                    dve.tensor_tensor(dst, src, dst, ALU.add).then_inc(s["y_ev"], 1)
                else:
                    dve.tensor_copy(dst, src).then_inc(s["y_ev"], 1)

            def leftover(f, t, n):
                if t == COPY_O:
                    dve.wait_ge(s["pv_done"], f * MB)
                    dve.tensor_copy(att_o, bank(BANK_PV)).then_inc(s["o_copied"], 1)
                if t == DIVIDE:
                    dve.wait_ge(s["den_act"], f * 2)
                    dve.tensor_tensor(att_n, att_o, att_r, ALU.mult).then_inc(s["on_ready"], 1)
                if t == RESIDUAL:
                    dve.wait_ge(s["pj_ev"], f)
                    x = xres[:, bass.ds(n * PC, PC)]
                    dve.tensor_tensor(x, x, att_r[0:C, :], ALU.add).then_inc(s["xo_done"], 1)

            def last_leftover(ab):
                for t in (COPY_O, DIVIDE, RESIDUAL):
                    leftover((ab + 1) * STRETCHES, t, NPC - 1)

            def stretch(b, kk, q, first, ab, scan=True):
                kidx = b * K + kk if scan else None
                att, att_first = ab is not None, first and kk == 0
                if scan:
                    mult_b(kidx, kk, q, 0, first)
                for t in range(BODY):
                    if scan:
                        for x in (2 * t, 2 * t + 1):
                            if x + 1 < 2 * BODY:
                                mult_b(kidx, kk, q, x + 1, first)
                            scan_half(kidx, kk, q, x, first)
                        if t == SPT and not first:
                            y_evacuate(kidx, q * 2 - 1, kk % 2)
                        if t == SPG + SPT:
                            y_evacuate(kidx, q * 2, kk % 2)
                    if att and not att_first:
                        n = (kk % 2) * NS + q - 1 if not (first and kk == 2) else NPC - 1
                        leftover(ab * STRETCHES + kk * NS + q, t, n)
                    if scan and kk + 1 < K:
                        for when, j, _, name in DVE_JOBS:
                            if when == t:
                                job_stage(kidx + 1, KS_ORDER[kk + 1], q, j, name)

            def front(b):
                chain = Chain(dve, s["dve_chain"], b, DVE_CHAIN)
                dve.wait_ge(s["x_loaded"], 16 * (b + 1))
                group_norm(b, 0, chain, xin)
                dve.wait_ge(s["inp_ev"], (b + 1) * NPC)
                conv(chain, [(u[1], pads[1], taps[1], H // 2), (u[0], pads[0], taps[0], H)], "conv_done")
                fronts[0] = chain.n

                def first_jobs(q, first):
                    for when, j, _, name in DVE_JOBS:
                        job_stage(b * K, KS_ORDER[0], q, j, name)

                stretches(dve, first_jobs)

            fronts = [0]

            def directions(b, ab):
                for kk in range(K):
                    kidx = b * K + kk
                    if kk == 2:
                        dve.wait_ge(s["y_stored"], b * 128 + 64)
                    stretches(dve, lambda q, first: stretch(b, kk, q, first, ab))
                    y_evacuate(kidx, NG - 1, kk % 2)
                if ab is not None:
                    last_leftover(ab)

            def back(b):
                chain = Chain(dve, s["dve_chain"], b, DVE_CHAIN)
                chain.n = fronts[0]
                dve.wait_ge(s["y_loaded"], 96 * (b + 1))
                marks = [chain.mark(dve.tensor_tensor(square(y[0]), square(y[0]), swapped(yt[0]), ALU.add))]
                for hf in range(2):
                    p = slice(64 * hf, 64 * hf + 64)
                    x = square(y[1][p, :])
                    ins = dve.tensor_tensor(x, x, swapped(yt[1][p, :])[:, 24 * hf:24 * hf + 24, :], ALU.add)
                marks.append(chain.mark(ins))
                for t in range(2):
                    chain.wait(marks[t])
                    ins = dve.scalar_tensor_tensor(out=y[t], in0=u[t], scalar=skip_sum[t][:, :], in1=y[t],
                                                   op0=ALU.mult, op1=ALU.add)
                ins.then_inc(s["y_summed"], 1)
                dve.wait_ge(s["y_summed"], b + 1)

                def both(c):
                    part, cols = rows(c)
                    return ((0, slice(0, 128), y[0][:, piece(c)]), (1, part, y[1][part, cols]))

                for c in range(NPC):
                    dve.wait_ge(s["ln_mean"], b * NPC + c + 1)
                    for t, p, x in both(c):
                        ins = dve.tensor_tensor(x, x, ps[p, c % 2, 0:PC], ALU.subtract)
                    ins.then_inc(s["ln_cent"], 1)
                dve.wait_ge(s["ln_cent"], (b + 1) * NPC)
                dve.wait_ge(s["xr_loaded"], (b + 1) * 16)
                for c in range(NPC):
                    dve.wait_ge(s["ln_rstd"], b * 3 + c // 2 + 1)
                    for t, p, x in both(c):
                        ins = dve.tensor_tensor(x, x, rstd[p, piece(c)], ALU.mult)
                    chain.link(ins)
                    for t, p, x in both(c):
                        ins = dve.tensor_scalar(x, x, ln_w[t][p, :], ln_b[t][p, :], ALU.mult, ALU.add)
                    chain.link(ins)
                    dve.wait_ge(s["z_act"], b * NPC + c + 1)
                    for t, p, x in both(c):
                        ins = dve.tensor_tensor(x, x, zg[c % 2][t][p, :], ALU.mult)
                    ins.then_inc(s["g_ready"], 1)
                    if c:
                        dve.wait_ge(s["o_mm"], b * NPC + c)
                        x = xres[:, piece(c - 1)]
                        dve.tensor_tensor(x, x, bank((c - 1) % 2, C), ALU.add).then_inc(s["o_ev"], 1)
                dve.wait_ge(s["o_mm"], (b + 1) * NPC)
                x = xres[:, piece(NPC - 1)]
                dve.tensor_tensor(x, x, bank((NPC - 1) % 2, C), ALU.add).then_inc(s["o_ev"], 1)
                dve.wait_ge(s["o_ev"], (b + 1) * NPC)
                group_norm(b, 1, chain, xres[:, :])
                dve.wait_ge(s["qkv_ev"], (b + 1) * NPC)
                conv(chain, [(qkv[t], qkv_pads[t], qkv_taps[:, 9 * t:9 * t + 9], H) for t in range(3)], "qkv_conv")
                dve.memset(bank(BANK_PV), 0.0).then_inc(s["pv_zero"], 1)
                dve.memset(v_cols[:, :, HD:HD + 1], 1.0).then_inc(s["v_ones"], 1)
                n_all = 2 * NPC
                for n in range(n_all):
                    dve.wait_ge(s["n_rt"], b * n_all + n + 1)
                    r = nrt[n % 2]
                    chain.link(dve.tensor_scalar(r, r, NORM_EPS, None, ALU.max))
                    chain.link(dve.reciprocal(r, r))
                    x = qkv[n // NPC][:, piece(n % NPC)]
                    dve.tensor_tensor(x, x, r, ALU.mult).then_inc(s["n_mul"], 1)
                dve.wait_ge(s["n_mul"], (b + 1) * n_all)
                for t in range(2):
                    dve.wait_ge(s["a_s1"], b * 2 + t + 1)
                    dve.tensor_tensor(qkv[t], qkv[t], parts[t][0], ALU.subtract).then_inc(s["a_r1"], 1)
                for t in range(2):
                    dve.wait_ge(s["a_r1"], b * 2 + t + 1)
                    dve.wait_ge(s["a_s2"], b * 2 + t + 1)
                    dve.tensor_tensor(parts[t][2], qkv[t], parts[t][1], ALU.subtract).then_inc(s["a_s3"], 1)
                for j in range(5):
                    m0, m1 = 4 * j, min(4 * j + 4, MB)
                    dve.wait_ge(s["v_tr"], b * 5 + j + 1)
                    src = ps[:, 2 + j % 2, 0:(m1 - m0) * C].rearrange("p (m d) -> p m d", d=HD)
                    dve.tensor_copy(v_cols[:, m0 * HEADS:m1 * HEADS, 0:HD], src).then_inc(s["v_ev"], 1)
                chain.end()

            def attention(ab):
                for kk in range(K):
                    stretches(dve, lambda q, first: stretch(None, kk, q, first, ab, False))
                last_leftover(ab)

            batches(dve, front, directions, back, attention)

        @block.tensor
        def _(pe):
            pe.wait_ge(s["w_loaded"], W_LOADED)

            def group_stats(b, t):
                pe.wait_ge(s["gn_stat"], b * 2 + t + 1)
                pe.matmul(ps[0:C, 7, 0:1], group_mean[:, :], mv[:, 0:1], start=True, stop=True)\
                  .then_inc(s["gn_mean"], 1)
                pe.wait_ge(s["gn_dev"], b * 2 + t + 1)
                pe.matmul(ps[0:C, 6, 0:1], group_mean[:, :], gn[:, 3:4], start=True, stop=True)\
                  .then_inc(s["gn_var"], 1)
                pe.wait_ge(s["xn_ready"], b * 2 + t + 1)

            def pick(t):
                i = t // SPT % TG
                return pick_channel[:, i * 128:(i + 1) * 128]

            def broadcast_delta(kidx, kk, q, t, first):
                n = kidx * DSTEPS + q * BODY + t
                if not (first and t == 0):
                    pe.wait_ge(s["da_ready"], n)
                x = 2 * t % (2 * SPT)
                for v in sorted((natural(kk, x), natural(kk, x + 1))):
                    ins = pe.matmul(bank(v % 2), pick(t), st[t // SPG][0][:, piece(v)], start=True, stop=True)
                ins.then_inc(s["dbc"], 1)

            def broadcast_u(kidx, kk, q, x, first):
                X = kidx * (2 * DSTEPS) + q * (2 * BODY) + x
                if not (first and x == 0):
                    pe.wait_ge(s["b_ready"], X)
                v = natural(kk, x % (2 * SPT))
                pe.matmul(bank(BANK_U), pick(x // 2), st[x // 2 // SPG][1][:, piece(v)], start=True, stop=True)\
                  .then_inc(s["ubc"], 1)

            def sum_tile(kidx, q, T, hh, first=False):
                i = T % TG
                if hh == 0:
                    pe.wait_ge(s["hc_ready"], (kidx * DSTEPS + q * BODY + (T + 1) * SPT) * 2)
                    if i == 0 and not (first and T == 0):
                        pe.wait_ge(s["y_ev"], kidx * NG + q * 2 + T // TG)
                for j in range(4):
                    col = j * QL + hh * HQ
                    ins = pe.matmul(ps[32 * j:32 * j + 32, BANK_Y + hh, 0:HQ], sum_states[:, 32 * i:32 * i + 32],
                                    hc[i % 2][:, col:col + HQ], start=(i == 0), stop=(i == TG - 1))
                if hh:
                    ins.then_inc(s["hc_used"], 1)

            def values(hg, f, m, wait_copied):
                pe.wait_ge(s["exp_done"], f * PIECES + (m + 1) * HG)
                if wait_copied:
                    pe.wait_ge(s["o_copied"], f)
                for h in range(HG):
                    ins = pe.matmul(ps[32 * h:32 * h + 13, BANK_PV, 0:PC], v_cols[:, m * HEADS + hg * HG + h, :],
                                    probs[(m % 2) * HG + h], start=(m == 0), stop=(m == MB - 1))
                ins.then_inc(s["pv_done"], 1)

            def denominators(f, bk):
                pe.wait_ge(s["o_copied"], f)
                pe.matmul(bank(bk), pick_den[:, :], att_o, start=True, stop=True).then_inc(s["den_done"], 1)

            def project(hg, f, bk):
                pe.wait_ge(s["on_ready"], f)
                pe.matmul(bank(bk, C), proj_w[:, hg * C:(hg + 1) * C], att_n, start=True, stop=True)\
                  .then_inc(s["pj_done"], 1)

            def job(k, j, q, bk):
                if j < 2:
                    ins = pe.matmul(bank(bk), dt_proj[0][:, k * DA:(k + 1) * DA],
                                    dts[:, bass.ds(q * (2 * PC) + j * PC, PC)], start=True, stop=True)
                else:
                    for hf in range(2):
                        col = k * 192 + 64 * (1 - hf)
                        ins = pe.matmul(bank(bk), dt_proj[1][:, col:col + 128],
                                        dts[:, bass.ds(q * PC + hf * HL, PC)], start=(hf == 0), stop=(hf == 1))
                ins.then_inc(s["dt_mm"], 1)

            def stretch(b, kk, q, first, ab, scan=True):
                kidx, hg = b * K + kk if scan else None, kk // 2
                att, att_first = ab is not None, first and kk == 0
                prev = att and not att_first
                prev_hg = (kk * NS - 1) // NPC if first else hg
                prep = scan and kk + 1 < K
                slots, order = ring_slots(att, prev, prep)
                f = ab * STRETCHES + kk * NS + q if att else None
                BI = (kidx + 1) * NS + q if prep else None

                def free(item):
                    i = order.index(item)
                    if i < 2:
                        if prev:
                            pe.wait_ge(s["exp_done"], f * PIECES)
                        elif not first and prep:
                            pe.wait_ge(s["job_act"], BI * NA)
                        return
                    kind, n = order[i - 2]
                    if kind == "score":
                        pe.wait_ge(s["exp_done"], f * PIECES + (n + 1))
                    elif kind == "den":
                        pe.wait_ge(s["den_act"], f * 2 - 1)
                    elif kind == "proj":
                        pe.wait_ge(s["pj_ev"], f)
                    else:
                        pe.wait_ge(s["job_act"], BI * NA + place(ACT_JOBS, n, "relu"))

                def score(p):
                    m, h = divmod(p, HG)
                    free(("score", p))
                    if h == 0 and m % (MB // SPT) == 0 and (first and kk % 2 == 0):
                        pe.wait_ge(ks_loaded[m // (MB // SPT)], (ab * 2 + hg + 1) * (16 * TERMS))
                    pe.matmul(bank(slots["score", p]), k_parts[:, h, m * 128:(m + 1) * 128],
                              q_ring[:, bass.ds(q, 1), h, :].rearrange("p s l -> p (s l)"),
                              start=True, stop=True).then_inc(s["s_done"], 1)

                if scan:
                    pe.wait_ge(st_loaded[0], (kidx * NS + q + 1) * 32)
                if att:
                    pe.wait_ge(s["qs_loaded"], (f + 1) * (16 * TERMS))
                next_m = 0
                for t in range(BODY):
                    if scan:
                        if t == SPG:
                            pe.wait_ge(st_loaded[1], (kidx * NS + q + 1) * 32)
                        broadcast_delta(kidx, kk, q, t, first)
                        broadcast_u(kidx, kk, q, 2 * t, first)
                    if att:
                        score(PER_STEP * t)
                        score(PER_STEP * t + 1)
                        if t == 0 and prev:
                            values(prev_hg, f - 1, MB - 1, False)
                    if prev and t == DEN_MM:
                        free(("den", 0))
                        denominators(f, slots["den", 0])
                    if prev and t == PROJ_MM:
                        free(("proj", 0))
                        project(prev_hg, f, slots["proj", 0])
                    if prep and t in JOB_START:
                        j = JOB_START.index(t)
                        free(("job", j))
                        job(KS_ORDER[kk + 1], j, q, slots["job", j])
                    while att and next_m * HG + HG - 1 < PER_STEP * t:
                        values(hg, f, next_m, next_m == 0 and prev)
                        next_m += 1
                    if scan:
                        broadcast_u(kidx, kk, q, 2 * t + 1, first)
                    if att:
                        score(PER_STEP * t + 2)
                    if scan and t % SPT:
                        T, hh = t // SPT - 1, t % SPT - 1
                        if T >= 0:
                            sum_tile(kidx, q, T, hh, first)
                        elif not first:
                            sum_tile(kidx, q - 1, 2 * TG - 1, hh)

            def last_leftover(ab):
                f = (ab + 1) * STRETCHES
                values(1, f - 1, MB - 1, False)
                denominators(f, 5)
                project(1, f, 6)

            def front(b):
                group_stats(b, 0)
                for c in range(NPC):
                    if c >= 2:
                        pe.wait_ge(s["inp_ev"], b * NPC + c - 1)
                    part, _ = rows(c)
                    pe.matmul(bank(2 * (c % 2)), in_proj[:, 0:DA], xn[:, piece(c)], start=True, stop=True)
                    pe.matmul(ps[part, 2 * (c % 2) + 1, 0:PC], in_proj[:, DA:DI], xn[:, piece(c)],
                              start=True, stop=True).then_inc(s["inp_mm"], 1)
                pe.wait_ge(s["u_ready"], b + 1)
                for c in range(NPC):
                    if c >= 2:
                        pe.wait_ge(s["xd_ev"], b * NPC + c - 1)
                    part, cols = rows(c)
                    for w, bk in ((xdt, 2 * (c % 2)), (xbc, 2 * (c % 2) + 1)):
                        for t in range(2):
                            for k in range(K):
                                if t:
                                    lhs, x = w[1][part, 32 * k:32 * k + 32], (ut_b if k % 2 else u[1])[part, cols]
                                    x = square(x)
                                else:
                                    lhs = w[0][:, 32 * k:32 * k + 32]
                                    x = (swapped if k % 2 else square)(u[0])[:, 8 * c:8 * c + 8, :]
                                ins = pe.matmul(square(ps[32 * k:32 * k + 32, bk, 0:PC]), lhs, x,
                                                start=(t == 0), stop=(t == 1))
                    ins.then_inc(s["xd_mm"], 1)
                pe.wait_ge(s["xd_ev"], (b + 1) * NPC)

                def first_jobs(q, first):
                    BI = b * (K * NS) + q
                    for j in range(JOBS):
                        if j == 2:
                            pe.wait_ge(s["job_act"], BI * NA + place(ACT_JOBS, 0, "relu"))
                        elif not first:
                            pe.wait_ge(s["job_act"], BI * NA)
                        job(KS_ORDER[0], j, q, 5 + j % 2)

                stretches(pe, first_jobs)

            def directions(b, ab):
                for kk in range(K):
                    stretches(pe, lambda q, first: stretch(b, kk, q, first, ab))
                    for hh in range(2):
                        sum_tile(b * K + kk, NS - 1, 2 * TG - 1, hh)
                if ab is not None:
                    last_leftover(ab)

            def back(b):
                pe.wait_ge(s["y_summed"], b + 1)

                def over_channels(dst, w, x, c):
                    part, cols = rows(c)
                    pe.matmul(dst, w[0], x[0], start=True, stop=False)
                    return pe.matmul(dst, w[1][part, :], x[1], start=False, stop=True)

                for c in range(NPC + 1):
                    if c < NPC:
                        if c >= 2:
                            pe.wait_ge(s["ln_cent"], b * NPC + c - 1)
                        part, cols = rows(c)
                        over_channels(bank(c % 2), (mean192[:, :], mean192), (y[0][:, piece(c)], y[1][part, cols]),
                                      c).then_inc(s["ln_mean"], 1)
                    if c:
                        pe.wait_ge(s["ln_sq"], b * NPC + c)
                        if c >= 3:
                            pe.wait_ge(s["ln_log"], b * NPC + c - 2)
                        j = (c - 1) % 2
                        part, _ = rows(c - 1)
                        over_channels(bank(2 + j), (mean192[:, :], mean192), (sq[j][0], sq[j][1][part, :]), c - 1)\
                            .then_inc(s["ln_var"], 1)
                pe.wait_ge(s["ln_cent"], (b + 1) * NPC)
                for c in range(NPC + 1):
                    if c < NPC:
                        if c >= 2:
                            pe.wait_ge(s["z_act"], b * NPC + c - 1)
                        part, _ = rows(c)
                        j = 4 + 2 * (c % 2)
                        pe.matmul(bank(j), in_proj[:, DI:DI + DA], xn[:, piece(c)], start=True, stop=True)
                        pe.matmul(ps[part, j + 1, 0:PC], in_proj[:, DI + DA:2 * DI], xn[:, piece(c)],
                                  start=True, stop=True).then_inc(s["z_mm"], 1)
                    if c:
                        pe.wait_ge(s["g_ready"], b * NPC + c)
                        if c >= 3:
                            pe.wait_ge(s["o_ev"], b * NPC + c - 2)
                        part, cols = rows(c - 1)
                        over_channels(bank((c - 1) % 2, C), (out_proj[0][:, :], out_proj[1]),
                                      (y[0][:, piece(c - 1)], y[1][part, cols]), c - 1).then_inc(s["o_mm"], 1)
                group_stats(b, 1)
                for c in range(NPC):
                    if c >= 2:
                        pe.wait_ge(s["qkv_ev"], b * NPC + c - 1)
                    for t in range(3):
                        ins = pe.matmul(bank(3 * (c % 2) + t, C), qkv_w[:, t * C:(t + 1) * C], xn[:, piece(c)],
                                        start=True, stop=True)
                    ins.then_inc(s["qkv_mm"], 1)
                pe.wait_ge(s["qkv_conv"], b + 1)
                n_all = 2 * NPC
                for n in range(n_all):
                    pe.wait_ge(s["n_sq"], b * n_all + n + 1)
                    if n >= 2:
                        pe.wait_ge(s["n_rt"], b * n_all + n - 1)
                    pe.matmul(bank(n % 2, C), head_ones[:, :], nsq[n % 2], start=True, stop=True)\
                      .then_inc(s["n_ss"], 1)
                for j in range(5):
                    if j >= 2:
                        pe.wait_ge(s["v_ev"], b * 5 + j - 1)
                    for m in range(4 * j, min(4 * j + 4, MB)):
                        col = (m % 4) * C
                        ins = pe.transpose(ps[:, 2 + j % 2, col:col + C], qkv[2][:, m * 128:(m + 1) * 128],
                                           ident[:, :])
                    ins.then_inc(s["v_tr"], 1)
                pe.wait_ge(s["v_ev"], (b + 1) * 5)
                pe.wait_ge(s["v_ones"], b + 1)
                pe.wait_ge(s["pv_zero"], b + 1)
                pe.wait_ge(s["n_rt"], (b + 1) * n_all)

            def attention(ab):
                for kk in range(K):
                    stretches(pe, lambda q, first: stretch(None, kk, q, first, ab, False))
                last_leftover(ab)

            batches(pe, front, directions, back, attention)


def kernel(**inputs):
    import ml_dtypes
    import numpy as np
    import concourse.bacc as bacc
    from concourse.bass_utils import run_bass_kernel_spmd

    x = np.asarray(inputs["x"])
    NB = x.shape[0]
    w = {n.replace("L0_conv_", "").replace("L1_conv_", "l1_"): np.asarray(v) for n, v in inputs.items()}

    def cols(m):
        return m[0:DA], np.concatenate([m[DA:DI], m[DA:DI]])

    f32 = np.float32
    arrays = {"x": x.reshape(NB, C, L), "in_projT": w["in_proj_w"].T}
    arrays["taps_a"], arrays["taps_b"] = cols(w["conv_w"].reshape(DI, 9))
    arrays["conv_b_a"], arrays["conv_b_b"] = cols(w["conv_b"].reshape(DI, 1))
    xdt, xbc = np.zeros((DI, K, 32), f32), np.zeros((DI, K, 32), f32)
    dt_a, dt_b = np.zeros((128, K, DA), f32), np.zeros((128, K, 192), f32)
    for k in range(K):
        xdt[:, k, 0:R] = w["x_proj_w"][k, 0:R].T
        xbc[:, k, :] = w["x_proj_w"][k, R:R + 2 * N].T
        dt_a[32 * k:32 * k + R, k, :] = w["dt_w"][k, 0:DA].T
        dt_b[32 * k:32 * k + R, k, 64:128] = w["dt_w"][k, DA:DI].T
    arrays["xdt_a"], arrays["xdt_b"] = cols(xdt.reshape(DI, K * 32))
    arrays["xbc_a"], arrays["xbc_b"] = cols(xbc.reshape(DI, K * 32))
    arrays["dt_proj_a"], arrays["dt_proj_b"] = dt_a.reshape(128, K * DA), dt_b.reshape(128, K * 192)
    arrays["dt_b_a"], arrays["dt_b_b"] = cols(w["dt_b"].T)
    arrays["a_logs"] = w["A_logs"].reshape(K * NG * TG, 128).T
    arrays["ds_a"], arrays["ds_b"] = cols(w["Ds"].reshape(K, DI).T)
    arrays["ln_w_a"], arrays["ln_w_b"] = cols(w["ln_w"].reshape(DI, 1))
    arrays["ln_b_a"], arrays["ln_b_b"] = cols(w["ln_b"].reshape(DI, 1))
    arrays["out_proj_a"], arrays["out_proj_b"] = cols(w["out_proj_w"].T)
    arrays["qkv_wT"] = w["l1_w_qkv"].T
    arrays["qkv_taps"] = w["l1_w_dw"].reshape(3, C, 9).transpose(1, 0, 2).reshape(C, 27)
    proj = np.zeros((128, 2, C), f32)
    for h in range(HEADS):
        r = 32 * (h % HG)
        proj[r:r + HD, h // HG, :] = w["l1_w_proj"][:, h * HD:(h + 1) * HD].T
    arrays["proj_wT"] = proj.reshape(128, 2 * C)
    pick = np.zeros((3, 32, TG, 8, N), f32)
    states = np.zeros((8, N, TG, 32), f32)
    for i in range(TG):
        for d in range(8):
            pick[:, 8 * i + d, i, d, :] = 1
            states[d, :, i, 8 * i + d] = 1
    arrays["pick_channel"] = pick.reshape(96, TG * 128).astype(ml_dtypes.bfloat16)
    arrays["sum_states"] = states.reshape(128, TG * 32)
    per = C // 32
    arrays["group_mean"] = np.kron(np.eye(32), np.full((per, per), 1.0 / per)).astype(f32)
    arrays["mean192"] = np.full((128, 128), 1.0 / DI, f32)
    arrays["head_ones"] = np.kron(np.eye(HEADS), np.ones((HD, HD))).astype(f32)
    arrays["ident"] = np.eye(C, dtype=f32)
    den = np.zeros((128, 128), f32)
    for h in range(HG):
        den[32 * h + HD, 32 * h:32 * h + 32] = 1
    arrays["pick_den"] = den
    arrays = {f"in_{n}": np.ascontiguousarray(v) for n, v in arrays.items()}

    nc = bacc.Bacc("TRN2", target_bir_lowering=False, num_devices=1)
    aps = {n[3:]: nc.dram_tensor(n, v.shape, mybir.dt.from_np(v.dtype), kind="ExternalInput").ap()
           for n, v in arrays.items()}
    out = nc.dram_tensor("out", (NB, C, L), F32, kind="ExternalOutput").ap()
    build(nc, NB, aps, out)
    got = run_bass_kernel_spmd(nc, [arrays], core_ids=[0]).results[0]["out"]
    return got.reshape(NB, C, H, W)
```

```python
from contextlib import ExitStack

import numpy as np

import concourse.bass as bass
from concourse import mybir

F32 = mybir.dt.float32
BF16 = mybir.dt.bfloat16
ALU = mybir.AluOpType
ACT = mybir.ActivationFunctionType

C, H, W = 96, 48, 48
L = H * W
HL = L // 2
DI, DA, DB = 192, 128, 64
K, N, R = 4, 16, 12
PC = 384
NPC = L // PC
SC = 2 * PC
NG = DI // 32
TG = 4
SPT = L // SC
SPG = TG * SPT
DSTEPS = NG * SPG
BODY = 2 * SPG
NS = NG // 2
NT = NG * TG
YP = L // 16
HEADS, HD = 8, 12
HG = 4
MB = L // 128
TERMS = 9
KS_ORDER = (0, 2, 1, 3)
NORMS = 4
DT_ROWS = {0: 0, 2: 32, 1: 64, 3: 96}
BC_ROWS = {1: 0, 3: 32, 0: 64, 2: 96}
SCALE = float(HD) ** -0.5
NEAR_1 = 2.0 ** -round(np.log2(L))
GN_EPS, LN_EPS, NORM_EPS = 1e-5, 1e-5, 1e-12
PADW = W + 2
PADL = (H + 2) * PADW
PAD2 = (H // 2 + 2) * PADW
LN_EXP_TABLES = "natural_log_exp_and_others"
DVE_CHAIN, ACT_CHAIN = 47, 2

PIECES = MB * HG
PER_STEP = PIECES // BODY
STRETCHES = K * NS
COPY_O, DEN_MM, DEN_LN, DEN_EXP, DIVIDE, PROJ_MM, PROJ_EV, RESIDUAL = 1, 2, 2, 3, 5, 7, 7, 8

JOBS = 3
JOB_START = (1, 9, 13)
ACT_STAGES = {"abs": 0, "relu": 0, "exp": 1, "ln": 2, "d0": 4, "u0": 5, "d1": 6, "u1": 7}
DVE_STAGES = {"add": 3, "times_u": 4, "d_rest": 5, "u_rest": 6, "d2": 7, "u2": 8}
ACT_JOBS = sorted((JOB_START[j] + t, j, i, n) for j in range(JOBS) for i, (n, t) in enumerate(ACT_STAGES.items()))
DVE_JOBS = sorted((JOB_START[j] + t, j, i, n) for j in range(JOBS) for i, (n, t) in enumerate(DVE_STAGES.items()))
NA, ND = len(ACT_JOBS), len(DVE_JOBS)


def place(jobs, j, name):
    return 1 + next(i for i, x in enumerate(jobs) if x[1] == j and x[3] == name)


def ring_slots(att, prev, prep, scan=True):
    order = []
    for t in range(BODY):
        scores = [("score", PER_STEP * t + i) for i in range(PER_STEP)] if att else []
        if scan:
            order += [("delta", 2 * t), ("delta", 2 * t + 1)]
        order += scores[:2]
        if prev and t == DEN_MM:
            order.append(("den", 0))
        if prev and t == PROJ_MM:
            order.append(("proj", 0))
        if prep and t in JOB_START:
            order.append(("job", JOB_START.index(t)))
        order += scores[2:]
    slots, before, held = {}, {}, [None] * (4 if scan else RING)
    age = [i - len(held) for i in range(len(held))]
    for i, x in enumerate(order):
        if x[0] == "delta" and x[1] % 2:
            b = slots["delta", x[1] - 1] + 1
        elif x[0] == "delta":
            b = min(range(len(held) - 1), key=lambda j: max(age[j], age[j + 1]))
        else:
            b = min(range(len(held)), key=lambda j: age[j])
        slots[x], before[x], held[b], age[b] = b, held[b], x, i
    return slots, before, order


RING = 7


class Chain:

    def __init__(self, engine, sem, b, count):
        self.engine, self.sem, self.base, self.count, self.n = engine, sem, b * count, count, 0

    def mark(self, ins):
        ins.then_inc(self.sem, 1)
        self.n += 1
        return self.n

    def wait(self, n=None):
        self.engine.wait_ge(self.sem, self.base + (self.n if n is None else n))

    def link(self, ins):
        self.mark(ins)
        self.wait()

    def end(self):
        assert self.n == self.count, (self.n, self.count)


def build(nc, NB, a, out):
    ctx = ExitStack()
    with ctx:
        def sb(name, shape, dt=F32):
            return ctx.enter_context(nc.sbuf_tensor(name, shape, dt))

        def sem(name):
            return ctx.enter_context(nc.semaphore(name))

        in_proj = sb("in_proj", [C, 2 * DI])
        taps = [sb("taps_a", [128, 9]), sb("taps_b", [128, 9])]
        conv_bias = [sb("conv_bias_a", [128, 1]), sb("conv_bias_b", [128, 1])]
        x_proj = [sb("x_proj_a", [128, 2 * 128]), sb("x_proj_b", [128, 2 * 128])]
        dt_proj = [sb("dt_proj_a", [128, K * DA]), sb("dt_proj_b", [128, K * 192])]
        dt_bias = [sb("dt_bias_a", [128, K]), sb("dt_bias_b", [128, K])]
        a_cols = sb("a_cols", [128, K * NG * TG])
        skip = [sb("skip_a", [128, K]), sb("skip_b", [128, K])]
        skip_sum = [sb("skip_sum_a", [128, 1]), sb("skip_sum_b", [128, 1])]
        ln_w = [sb("ln_w_a", [128, 1]), sb("ln_w_b", [128, 1])]
        ln_b = [sb("ln_b_a", [128, 1]), sb("ln_b_b", [128, 1])]
        out_proj = [sb("out_proj_a", [128, C]), sb("out_proj_b", [128, C])]
        qkv_w = sb("qkv_w", [C, 3 * C])
        qkv_taps = sb("qkv_taps", [C, 27])
        proj_w = sb("proj_w", [128, 2 * C])
        pick_channel = sb("pick_channel", [96, TG * 128], BF16)
        sum_states = sb("sum_states", [128, TG * 32])
        group_mean = sb("group_mean", [C, C])
        mean192 = sb("mean192", [128, 128])
        head_ones = sb("head_ones", [C, C])
        ident = sb("ident", [C, C])
        pick_den = sb("pick_den", [128, 128])
        gn_eps = sb("gn_eps", [128, 1])

        xres = sb("xres", [C, L])
        u_buf = sb("u_buf", [128, 2 * L])
        dts = sb("dts", [128, L])
        rep = sb("rep", [128, 2 * (SPT + 1) * SC])
        st_buf = sb("st_buf", [128, 2 * L])
        rings = sb("rings", [128, 9 * PC])
        hc_buf = sb("hc_buf", [128, 2 * L])
        y_acc = sb("y_acc", [128, NT * YP])
        job_buf = sb("job_buf", [128, 10 * PC])
        kp_buf = sb("kp_buf", [TERMS * HD, HG * L], BF16)
        qp_buf = sb("qp_buf", [TERMS * HD, NS * HG * PC], BF16)
        probs_buf = sb("probs_buf", [128, 2 * HG * PC])
        v_buf = sb("v_buf", [128, MB * HEADS * 13])
        att_buf = sb("att_buf", [128, 3 * PC])
        stats = sb("stats", [C, NPC * 6])
        mv = sb("mv", [C, 2])
        gn = sb("gn", [C, 6])

        u = [u_buf[:, 0:L], u_buf[:, L:L + HL]]
        ut_b = u_buf[:, L + HL:2 * L]
        xin = y_acc[0:C, 0:L]
        bc_stage = st_buf[:, 0:L]
        pads = [hc_buf[:, 0:PADL], rings[:, 0:PAD2]]
        xn = job_buf[0:C, 0:L]
        job_p = job_buf[:, 4 * PC:10 * PC].bitcast(BF16)
        jobs_f = [[job_buf[:, (2 * i + q) * PC:(2 * i + q + 1) * PC] for q in range(2)] for i in range(2)]
        jobs_p = [job_p[:, 6 * i * PC:6 * (i + 1) * PC].rearrange("p (r l) -> p r l", r=6) for i in range(2)]
        st = [[st_buf[:, :].bitcast(BF16)[0:96, (2 * i + q) * L:(2 * i + q + 1) * L] for q in range(2)]
              for i in range(2)]
        da_ring = [rings[:, i * SC:(i + 1) * SC] for i in range(2)]
        b_ring = [rings[:, (4 + i) * PC:(5 + i) * PC] for i in range(3)]
        h_ring = [rings[:, (7 + i) * PC:(8 + i) * PC] for i in range(2)]
        hc = [hc_buf[:, i * L:(i + 1) * L] for i in range(2)]
        y = [st_buf[:, 0:L], st_buf[:, L:L + HL]]
        yt = [hc_buf[:, 0:L], hc_buf[:, L:2 * L]]
        rstd = y_acc[:, 0:L]
        sq = [[rings[:, (2 * i + t) * PC:(2 * i + t + 1) * PC] for t in range(2)] for i in range(2)]
        zg = [[rep[:, (2 * i + t) * PC:(2 * i + t + 1) * PC] for t in range(2)] for i in range(2)]
        qkv_pads = [u_buf[0:C, 0:PADL], hc_buf[0:C, 0:PADL], st_buf[0:C, 0:PADL]]
        qkv = [dts[0:C, :], rep[0:C, 0:L], rep[0:C, L:2 * L]]
        nsq = [rings[0:C, i * HL:(i + 1) * HL] for i in range(2)]
        nrt = [y_acc[0:C, i * HL:(i + 1) * HL] for i in range(2)]
        half = [hc_buf[:, :].bitcast(BF16), st_buf[:, :].bitcast(BF16)]
        parts = [[half[q][0:C, r * L:(r + 1) * L] for r in range(3)] for q in range(2)]
        k_parts = kp_buf[:, :].rearrange("p (h l) -> p h l", h=HG)
        q_ring = qp_buf[:, :].rearrange("p (s h l) -> p s h l", s=NS, h=HG)
        probs = [probs_buf[:, i * PC:(i + 1) * PC] for i in range(2 * HG)]
        v_cols = v_buf[:, :].rearrange("p (m d) -> p m d", d=13)
        att_o, att_r, att_n = (att_buf[:, i * PC:(i + 1) * PC] for i in range(3))

        ps = ctx.enter_context(nc.psum_tensor("ps", [128, 8, 512], F32))
        BANK_U, BANK_Y, BANK_PV = (4, 5), 6, 7

        bc_dram = nc.dram_tensor("bc_scratch", [128, L], F32).ap()
        xn_dram = nc.dram_tensor("xn_scratch", [C, L], F32).ap()
        part_dram = nc.dram_tensor("part_scratch", [2, NG, 6, 32, L], BF16).ap()
        y_dram = nc.dram_tensor("y_scratch", [2, DI, L], F32).ap()
        qk_dram = nc.dram_tensor("qk_scratch", [2, 3, C, L], BF16).ap()

        names = """w_loaded const_set eps_set skip_summed x_loaded xr_loaded gn_stat gn_mean gn_dev gn_var
            gn_std xn_ready xn_stored xn_loaded inp_mm inp_ev pads_zero tap_mult tap_added conv_done u_ready xd_mm xd_ev bc_stored
            dt_mm job_act job_dve dbc ubc da_ready b_ready h_ready hc_ready hc_used y_ev y_stored y_loaded
            y_summed ln_mean ln_cent ln_sq ln_var ln_log ln_rstd z_mm z_act g_ready o_mm o_ev
            qkv_mm qkv_ev qkv_zero qkv_conv n_sq n_ss n_max n_ln n_rt n_mul a_s1 a_r1 a_s2 a_s3 a_stored
            v_tr v_ev v_ones pv_zero qs_loaded s_done exp_done pv_done o_copied den_done den_act on_ready
            pj_done pj_ev xo_done out_stored dve_chain act_chain""".split()
        s = {n: sem(n) for n in names}
        passed = {e.engine: sem(f"passed_{n}") for n, e in (("act", nc.scalar), ("dve", nc.vector),
                                                            ("pool", nc.gpsimd), ("sp", nc.sync))}
        part_stored = [sem(f"part_stored{i}") for i in range(2)]
        st_loaded = [sem(f"st_loaded{i}") for i in range(2)]
        rep_loaded = [sem(f"rep_loaded{i}") for i in range(SPT)]
        ks_loaded = [sem(f"ks_loaded{i}") for i in range(SPT)]

        def piece(c):
            return slice(c * PC, (c + 1) * PC)

        def bank(i, p=128, n=PC):
            return ps[0:p, i, 0:n]

        def rows(c):
            hf = c // (NPC // 2)
            return slice(64 * hf, 64 * hf + 64), piece(c % (NPC // 2))

        def square(ap):
            return ap.rearrange("p (h w) -> p h w", w=W)

        def swapped(ap):
            return ap.rearrange("p (h w) -> p w h", w=W)

        def window(pad, tap, n=H):
            dy, dx = divmod(tap, 3)
            return pad.rearrange("p (h w) -> p h w", w=PADW)[:, dy:dy + n, dx:dx + W]

        def pad_rows(pad, r, n=PC // W):
            return pad.rearrange("p (h w) -> p h w", w=PADW)[:, r:r + n, 1:1 + W]

        def front_units():
            tmp = [rep[:, i * HL:(i + 1) * HL] for i in range(3)]
            work = [(window(pads[1], tap, H // 2), taps[1][:, tap:tap + 1], square(u[1])) for tap in range(9)]
            return work, [square(x) for x in tmp], 1, 0, 0

        def back_units():
            tmp = [job_buf[0:C, i * HL:(i + 1) * HL] for i in range(3)]
            work = [(window(qkv_pads[2], tap)[:, hf * (H // 2):(hf + 1) * (H // 2), :],
                     qkv_taps[:, 18 + tap:19 + tap], square(qkv[2][:, hf * HL:(hf + 1) * HL]))
                    for tap in range(9) for hf in range(2)]
            return work, [square(x) for x in tmp], 2, 9, 8

        def unit_products(act, b, units):
            work, tmp, direct, p0, s0 = units
            for n, (src, w, dst) in enumerate(work):
                i = n - direct
                if i >= 3:
                    act.wait_ge(s["tap_added"], b * 24 + s0 + i - 2)
                act.activation(dst if i < 0 else tmp[i % 3], src, ACT.Copy, scale=w).then_inc(s["tap_mult"], 1)

        def unit_sums(pool, b, units):
            work, tmp, direct, p0, s0 = units
            for n, (_, _, dst) in enumerate(work):
                i = n - direct
                if i < 0:
                    continue
                pool.wait_ge(s["tap_mult"], b * 27 + p0 + n + 1)
                if i >= direct:
                    pool.wait_ge(s["tap_added"], b * 24 + s0 + i - direct + 1)
                pool.tensor_tensor(dst, dst, tmp[i % 3], ALU.add).then_inc(s["tap_added"], 1)

        def natural(kk, v):
            return 2 * SPT - 1 - v if KS_ORDER[kk] >= 2 else v

        def rep_third(j, kk, i):
            slot = j * (SPT + 1) + (i - kk) % (SPT + 1)
            return rep[:, slot * SC:(slot + 1) * SC]

        def rep_piece(j, kk, v):
            return rep_third(j, kk, v // 2)[:, piece(natural(kk, v) % 2)]

        loads = [(in_proj, "in_projT"), (taps[0], "taps_a"), (taps[1], "taps_b"),
                 (conv_bias[0], "conv_b_a"), (conv_bias[1], "conv_b_b"), (x_proj[0], "x_proj_a"),
                 (x_proj[1], "x_proj_b"), (dt_proj[0], "dt_proj_a"), (dt_proj[1], "dt_proj_b"),
                 (dt_bias[0], "dt_b_a"), (dt_bias[1], "dt_b_b"), (a_cols, "a_logs"), (skip[0], "ds_a"),
                 (skip[1], "ds_b"), (ln_w[0], "ln_w_a"), (ln_w[1], "ln_w_b"), (ln_b[0], "ln_b_a"),
                 (ln_b[1], "ln_b_b"), (out_proj[0], "out_proj_a"), (out_proj[1], "out_proj_b"),
                 (qkv_w, "qkv_wT"), (qkv_taps, "qkv_taps"), (proj_w, "proj_wT"),
                 (pick_channel, "pick_channel"), (sum_states, "sum_states"), (group_mean, "group_mean"),
                 (mean192, "mean192"), (head_ones, "head_ones"), (ident, "ident"), (pick_den, "pick_den")]
        W_LOADED = 16 * len(loads)

        def apart(engine):
            engine.sem_inc(passed[engine.engine], 1)

        def batches(engine, front, directions, back, attention):
            front(0)
            directions(0, None)
            back(0)
            if NB > 1:
                with engine.Fori(1, NB) as b:
                    front(b)
                    directions(b, b - 1)
                    back(b)
            attention(NB - 1)

        def stretches(engine, body):
            body(0, True)
            with engine.Fori(1, NS) as q:
                body(q, False)

        block = ctx.enter_context(nc.Block())

        @block.sync
        def _(sp):
            for dst, name in loads:
                sp.dma_start(dst[:, :], a[name]).then_inc(s["w_loaded"], 16)

            def load_st(kk, g):
                for q in range(2):
                    src = part_dram[kk % 2, g, 3 * q:3 * q + 3, :, :].rearrange("s d l -> (s d) l")
                    sp.dma_start(st[g % 2][q], src).then_inc(st_loaded[g % 2], 16)

            def load_rep(kk, i):
                k = KS_ORDER[kk]
                cc = SPT - 1 - i if k >= 2 else i
                for j in range(2):
                    r = BC_ROWS[k] + N * j
                    row = bc_dram[r:r + N, cc * SC:(cc + 1) * SC]
                    sp.dma_start(rep_third(j, kk, i), bass.AP(row.tensor, row.offset, [[0, 8], [L, N], [1, SC]]))\
                      .then_inc(rep_loaded[i], 16)

            def store_y(kk, q):
                for j in range(16):
                    rows8 = y_dram[kk // 2, 8 * 2 * TG * q:8 * 2 * TG * (q + 1), j * YP:(j + 1) * YP]
                    src = y_acc[8 * j:8 * j + 8, 2 * TG * YP * q:2 * TG * YP * (q + 1)]
                    sp.dma_start(rows8.rearrange("(t d) r -> d t r", d=8),
                                 src.rearrange("p (t r) -> p t r", r=YP)).then_inc(s["y_stored"], 16)

            def store_job(b, kk, q, j):
                BI = (b * K + kk) * NS + q
                sp.wait_ge(s["job_dve"], BI * ND + place(DVE_JOBS, j, "u2"))
                for g in range(4):
                    src = jobs_p[j % 2][32 * g:32 * g + 32, :, :]
                    if j < 2:
                        group, col = g, (2 * q + j) * PC
                    else:
                        group, col = 4 + g % 2, (g // 2) * HL + q * PC
                    dst = part_dram[kk % 2, group, :, :, col:col + PC].rearrange("r d l -> d r l")
                    sp.dma_start(dst, src).then_inc(part_stored[j % 2], 16)

            def load_keys(hg, c):
                for t in range(TERMS):
                    src = qk_dram[1, t % 3, hg * HG * HD:(hg + 1) * HG * HD, c * SC:(c + 1) * SC]\
                        .rearrange("(h d) l -> d h l", d=HD)
                    sp.dma_start(k_parts[t * HD:(t + 1) * HD, :, c * SC:(c + 1) * SC], src)\
                      .then_inc(ks_loaded[c], 16)

            def load_queries(i):
                hg, n = divmod(i, NPC)
                for t in range(TERMS):
                    src = qk_dram[0, t // 3, hg * HG * HD:(hg + 1) * HG * HD, piece(n)]\
                        .rearrange("(h d) l -> d h l", d=HD)
                    sp.dma_start(q_ring[t * HD:(t + 1) * HD, i % NS, :, :], src).then_inc(s["qs_loaded"], 16)

            def next_keys(ab, i, c):
                sp.wait_ge(s["s_done"], (ab * STRETCHES + i) * PIECES + (c + 1) * (PIECES // SPT))
                load_keys(1, c)

            def stretch(b, kk, q, ab):
                kidx, i = b * K + kk, kk * NS + q
                prep = kk + 1 < K and b is not None
                if ab is not None and i + 1 < STRETCHES:
                    sp.wait_ge(s["s_done"], (ab * STRETCHES + i) * PIECES + 1)
                    load_queries(i + 1)
                turn = ab is not None and i + 1 == NPC
                if turn:
                    next_keys(ab, i, 0)
                if prep:
                    store_job(b, kk + 1, q, 0)
                if kk + 1 < K and q == 1:
                    if kk:
                        sp.wait_ge(s["hc_ready"], kidx * (2 * DSTEPS))
                    load_rep(kk + 1, 0)
                if q + 1 < NS:
                    sp.wait_ge(s["ubc"], (kidx * DSTEPS + q * BODY + SPG) * 2)
                    load_st(kk, 2 * q + 2)
                if kk % 2 and q:
                    sp.wait_ge(s["y_ev"], kidx * NT + q * (2 * TG))
                    store_y(kk, q - 1)
                if turn:
                    next_keys(ab, i, 1)
                if prep:
                    store_job(b, kk + 1, q, 1)
                    if q + 1 == NS:
                        BI = (kidx + 1) * NS + q
                        sp.wait_ge(s["ubc"], (kidx * DSTEPS + q * BODY + SPG) * 2)
                        sp.wait_ge(part_stored[0], BI * 128 + 64)
                        sp.wait_ge(part_stored[1], (BI + 1) * 64)
                        load_st(kk + 1, 0)
                    store_job(b, kk + 1, q, 2)
                if q + 1 < NS:
                    sp.wait_ge(s["ubc"], (kidx * DSTEPS + (q + 1) * BODY) * 2)
                    load_st(kk, 2 * q + 3)
                elif prep:
                    for c in range(1, SPT):
                        sp.wait_ge(s["hc_ready"], (kidx + 1) * (2 * DSTEPS) - 2 * (SPT - c))
                        load_rep(kk + 1, c)
                    sp.wait_ge(s["ubc"], (kidx + 1) * (2 * DSTEPS))
                    sp.wait_ge(part_stored[0], (kidx + 2) * NS * 128)
                    load_st(kk + 1, 1)
                if turn:
                    next_keys(ab, i, 2)

            def store_parts(b):
                for t in range(2):
                    sp.wait_ge(s["a_s3"], b * 2 + t + 1)
                    for r in range(3):
                        sp.dma_start(qk_dram[t, r], parts[t][r]).then_inc(s["a_stored"], 16)
                sp.wait_ge(s["a_stored"], (b + 1) * 96)
                apart(sp)

            def first_queries_keys():
                load_queries(0)
                for c in range(SPT):
                    load_keys(0, c)

            def front(b):
                later = not (isinstance(b, int) and b == 0)
                if later:
                    sp.wait_ge(s["n_mul"], b * NORMS)
                    apart(sp)
                sp.dma_start(xin, a["x"][bass.ds(b, 1), :, :].rearrange("b c l -> (b c) l"))\
                  .then_inc(s["x_loaded"], 16)
                if later:
                    store_parts(b - 1)
                    first_queries_keys()
                sp.wait_ge(s["xn_ready"], b * 2 + 1)
                apart(sp)
                sp.dma_start(xn_dram, xn).then_inc(s["xn_stored"], 16)
                sp.wait_ge(s["xd_ev"], (b + 1) * NPC)
                apart(sp)
                sp.dma_start(bc_dram, bc_stage).then_inc(s["bc_stored"], 16)
                sp.wait_ge(s["bc_stored"], 16 * (b + 1))
                apart(sp)
                for i in range(SPT):
                    load_rep(0, i)
                for q in range(NS):
                    for j in range(JOBS):
                        store_job(b, 0, q, j)
                sp.wait_ge(part_stored[0], (b * K + 1) * NS * 128)
                apart(sp)
                sp.wait_ge(part_stored[1], (b * K + 1) * NS * 64)
                apart(sp)
                for g in range(2):
                    load_st(0, g)

            def directions(b, ab):
                for kk in range(K):
                    kidx = b * K + kk
                    if kk + 1 == K:
                        sp.dma_start(xn, xn_dram).then_inc(s["xn_loaded"], 16)
                    for q in range(NS):
                        stretch(b, kk, q, ab)
                    if kk % 2:
                        sp.wait_ge(s["y_ev"], (kidx + 1) * NT)
                        store_y(kk, NS - 1)
                if ab is not None:
                    store_out(ab)

            def store_out(ab):
                sp.wait_ge(s["xo_done"], (ab + 1) * STRETCHES)
                apart(sp)
                sp.dma_start(out[bass.ds(ab, 1), :, :].rearrange("b c l -> (b c) l"), xres[:, :])\
                  .then_inc(s["out_stored"], 16)
                sp.wait_ge(s["out_stored"], (ab + 1) * 16)
                apart(sp)

            def back(b):
                sp.wait_ge(s["y_stored"], (b + 1) * (2 * NS * 256))
                apart(sp)
                sp.dma_start(y[0], y_dram[0, 0:DA, :]).then_inc(s["y_loaded"], 16)
                sp.dma_start(yt[0], y_dram[1, 0:DA, :]).then_inc(s["y_loaded"], 16)
                for hf in range(2):
                    p = slice(64 * hf, 64 * hf + 64)
                    sp.dma_start(y[1][p, :], y_dram[0, DA:DI, hf * HL:(hf + 1) * HL]).then_inc(s["y_loaded"], 16)
                    sp.dma_start(yt[1][p, :], y_dram[1, DA:DI, :]).then_inc(s["y_loaded"], 16)
                sp.dma_start(xres[:, :], a["x"][bass.ds(b, 1), :, :].rearrange("b c l -> (b c) l"))\
                  .then_inc(s["xr_loaded"], 16)

            def attention(ab):
                store_parts(ab)
                first_queries_keys()
                for i in range(STRETCHES):
                    if i + 1 < STRETCHES:
                        sp.wait_ge(s["s_done"], (ab * STRETCHES + i) * PIECES + 1)
                        load_queries(i + 1)
                    if i + 1 == NPC:
                        for c in range(SPT):
                            next_keys(ab, i, c)
                store_out(ab)

            batches(sp, front, directions, back, attention)

        @block.gpsimd
        def _(pool):
            def front(b):
                pool.memset(pads[0], 0.0)
                pool.memset(pads[1], 0.0).then_inc(s["pads_zero"], 1)
                unit_sums(pool, b, front_units())

            def directions(b, ab):
                for kk in range(K):
                    kidx = b * K + kk

                    def stretch(q, first):
                        for x in range(2 * BODY):
                            X = kidx * (2 * DSTEPS) + q * (2 * BODY) + x
                            tile, v = divmod(x, 2 * SPT)
                            cols = piece(natural(kk, v))
                            if first and tile == 0 and v % 2 == 0:
                                pool.wait_ge(rep_loaded[v // 2], 32 * (kidx + 1))
                            if v == 0 and not (first and tile < 2):
                                pool.wait_ge(s["hc_used"], kidx * (NG * TG) + q * (2 * TG) + (tile - 1))
                            pool.wait_ge(s["h_ready"], X + 1)
                            pool.tensor_tensor(hc[tile % 2][:, cols], h_ring[x % 2], rep_piece(1, kk, v), ALU.mult)\
                                .then_inc(s["hc_ready"], 1)

                    stretches(pool, stretch)

            def back(b):
                pool.wait_ge(s["y_summed"], b + 1)
                apart(pool)
                pool.memset(qkv_pads[0], 0.0)
                pool.memset(qkv_pads[1], 0.0)
                pool.wait_ge(s["o_mm"], (b + 1) * NPC)
                apart(pool)
                pool.memset(qkv_pads[2], 0.0).then_inc(s["qkv_zero"], 1)
                unit_sums(pool, b, back_units())
                pool.wait_ge(s["a_stored"], (b + 1) * 96)
                apart(pool)

            batches(pool, front, directions, back, lambda ab: None)

        @block.scalar
        def _(act):
            act.wait_ge(s["w_loaded"], W_LOADED)
            act.activation(a_cols[:, :], a_cols[:, :], ACT.Exp).then_inc(s["const_set"], 1)
            act.wait_ge(s["const_set"], 1)
            act.mul(a_cols[:, :], a_cols[:, :], -1.0).then_inc(s["const_set"], 1)
            act.wait_ge(s["const_set"], 2)
            act.wait_ge(s["eps_set"], 1)

            def group_std(b, t):
                act.wait_ge(s["gn_var"], b * 2 + t + 1)
                act.activation(gn[:, 2:3], ps[0:C, 6, 0:1], ACT.Sqrt, bias=gn_eps[0:C, :]).then_inc(s["gn_std"], 1)

            def job_stage(kidx, k, q, j, name, bk, first):
                BI = kidx * NS + q
                d, m = jobs_f[j % 2]
                bias = dt_bias[j // 2][:, k:k + 1]

                def own(stage):
                    act.wait_ge(s["job_act"], BI * NA + place(ACT_JOBS, j, stage))

                def dve_done(stage):
                    act.wait_ge(s["job_dve"], BI * ND + place(DVE_JOBS, j, stage))

                if name == "abs":
                    if j == 2:
                        act.wait_ge(s["job_dve"], BI * ND + place(DVE_JOBS, 0, "u2"))
                    elif not first:
                        act.wait_ge(s["job_dve"], BI * ND)
                    act.wait_ge(s["dt_mm"], BI * JOBS + j + 1)
                    ins = act.activation(d, bank(bk), ACT.Abs, bias=bias)
                elif name == "relu":
                    ins = act.activation(m, bank(bk), ACT.Relu, bias=bias)
                elif name == "exp":
                    own("abs")
                    ins = act.activation(d, d, ACT.Exp, scale=-1.0)
                elif name == "ln":
                    own("exp")
                    ins = act.activation(d, d, ACT.Ln, bias=1.0)
                elif name in ("d0", "u0"):
                    if j == 2:
                        act.wait_ge(part_stored[0], BI * 128 + 64)
                    elif not first:
                        act.wait_ge(part_stored[j], BI * (128, 64)[j])
                    dve_done("add" if name == "d0" else "times_u")
                    r, src = (0, d) if name == "d0" else (3, m)
                    ins = act.copy(jobs_p[j % 2][:, r, :], src)
                else:
                    dve_done("d_rest" if name == "d1" else "u_rest")
                    r, src = (1, d) if name == "d1" else (4, m)
                    ins = act.copy(jobs_p[j % 2][:, r, :], src)
                ins.then_inc(s["job_act"], 1)

            def stretch(b, kk, q, first, ab, scan=True):
                kidx, k = b * K + kk if scan else None, KS_ORDER[kk]
                att, att_first = ab is not None, first and kk == 0
                prep = scan and kk + 1 < K
                slots, _, _ = ring_slots(att, att and not att_first, prep, scan)
                if att:
                    f = ab * STRETCHES + kk * NS + q
                for t in range(BODY):
                    if scan:
                        n = kidx * DSTEPS + q * BODY + t
                        if not (first and t < 2):
                            act.wait_ge(s["h_ready"], n * 2 - 2)
                        act.wait_ge(s["dbc"], n + 1)
                        apart(act)
                        bk = slots["delta", 2 * t]
                        act.activation(da_ring[t % 2].rearrange("p (a r) -> p a r", a=2), ps[:, bk:bk + 2, 0:PC],
                                       ACT.Exp, scale=a_cols[:, bass.ds(q * (2 * TG) + (k * NG * TG + t // SPT), 1)])\
                            .then_inc(s["da_ready"], 1)
                    for p in range(PER_STEP * t, PER_STEP * (t + 1) if att else 0):
                        m, h = divmod(p, HG)
                        if h == 0 and not (att_first and m < 2):
                            act.wait_ge(s["pv_done"], f * MB + (m - 1))
                        act.wait_ge(s["s_done"], f * PIECES + (p + 1))
                        act.activation(probs[(m % 2) * HG + h], bank(slots["score", p]), ACT.Exp, scale=SCALE)\
                            .then_inc(s["exp_done"], 1)
                    if att and not att_first:
                        leftover(f, t, slots["den", 0], slots["proj", 0])
                    if prep:
                        for when, j, _, name in ACT_JOBS:
                            if when == t:
                                job_stage(kidx + 1, KS_ORDER[kk + 1], q, j, name, slots["job", j], False)

            def leftover(f, t, den_bank, proj_bank):
                if t == DEN_LN:
                    act.wait_ge(s["den_done"], f)
                    act.activation(att_r, bank(den_bank), ACT.Ln, scale=NEAR_1).then_inc(s["den_act"], 1)
                if t == DEN_EXP:
                    act.wait_ge(s["den_act"], f * 2 - 1)
                    act.activation(att_r, att_r, ACT.Exp, scale=-1.0).then_inc(s["den_act"], 1)
                if t == PROJ_EV:
                    act.wait_ge(s["pj_done"], f)
                    act.copy(att_r[0:C, :], bank(proj_bank, C)).then_inc(s["pj_ev"], 1)

            def last_leftover(ab):
                for t in (DEN_LN, DEN_EXP, PROJ_EV):
                    leftover((ab + 1) * STRETCHES, t, 0, 1)

            def front(b):
                chain = Chain(act, s["act_chain"], b, ACT_CHAIN)
                group_std(b, 0)
                act.wait_ge(s["pads_zero"], b + 1)
                for c in range(NPC):
                    act.wait_ge(s["inp_mm"], b * NPC + c + 1)
                    act.copy(pad_rows(pads[0], 1 + 8 * c), square(bank(2 * (c % 2))))
                    part, _ = rows(c)
                    src = square(ps[part, 2 * (c % 2) + 1, 0:PC])
                    if c == 2:
                        act.copy(pad_rows(pads[1][64:128, :], 0, 1), src[:, 7:8, :])
                    if c == 3:
                        act.copy(pad_rows(pads[1][0:64, :], H // 2 + 1, 1), src[:, 0:1, :])
                    act.copy(pad_rows(pads[1][part, :], 1 + 8 * (c % 3)), src).then_inc(s["inp_ev"], 1)
                act.wait_ge(s["inp_ev"], (b + 1) * NPC)
                unit_products(act, b, front_units())
                act.wait_ge(s["tap_added"], b * 24 + 8)
                chain.mark(act.activation(u[1], u[1], ACT.Gelu, bias=conv_bias[1][:, :]))
                act.wait_ge(s["conv_done"], b + 1)
                chain.mark(act.activation(u[0], u[0], ACT.Gelu, bias=conv_bias[0][:, :]))
                chain.wait(1)
                for hh in range(2):
                    for wh in range(2):
                        dst = ut_b[64 * wh:64 * wh + 64, :].rearrange("p (w h) -> p w h", h=H)
                        src = square(u[1][64 * hh:64 * hh + 64, :])[:, :, 24 * wh:24 * wh + 24]
                        ins = act.copy(dst[:, :, 24 * hh:24 * hh + 24], src.rearrange("p h w -> p w h"))
                chain.wait()
                ins.then_inc(s["u_ready"], 1)
                for c in range(NPC):
                    act.wait_ge(s["xd_mm"], b * NPC + c + 1)
                    for dst, odd, p in ((dts, 0, 0), (bc_stage, 0, 64), (bc_stage, 1, 0), (dts, 1, 64)):
                        ins = act.copy(dst[p:p + 64, piece(c)], ps[p:p + 64, 2 * (c % 2) + odd, 0:PC])
                    ins.then_inc(s["xd_ev"], 1)
                chain.end()
                act.preload_act_table_set(LN_EXP_TABLES)
                act.wait_ge(s["xn_stored"], 16 * (b + 1))
                apart(act)

                def first_jobs(q, first):
                    for when, j, _, name in ACT_JOBS:
                        job_stage(b * K, KS_ORDER[0], q, j, name, 5 + j % 2, first)

                stretches(act, first_jobs)

            def directions(b, ab):
                for kk in range(K):
                    stretches(act, lambda q, first: stretch(b, kk, q, first, ab))
                if ab is not None:
                    last_leftover(ab)

            def back(b):
                for c in range(NPC + 1):
                    if c < NPC:
                        act.wait_ge(s["ln_cent"], b * NPC + c + 1)
                        if c >= 2:
                            act.wait_ge(s["ln_var"], b * NPC + c - 1)
                        part, cols = rows(c)
                        act.activation(sq[c % 2][0], y[0][:, piece(c)], ACT.Square)
                        act.activation(sq[c % 2][1][part, :], y[1][part, cols], ACT.Square).then_inc(s["ln_sq"], 1)
                    if c:
                        act.wait_ge(s["ln_var"], b * NPC + c)
                        act.activation(rstd[:, piece(c - 1)], bank(2 + (c - 1) % 2), ACT.Ln, bias=gn_eps[:, :])\
                            .then_inc(s["ln_log"], 1)
                for j in range(3):
                    act.wait_ge(s["ln_log"], b * NPC + 2 * j + 2)
                    x = rstd[:, 2 * j * PC:(2 * j + 2) * PC]
                    act.activation(x, x, ACT.Exp, scale=-0.5).then_inc(s["ln_rstd"], 1)
                for c in range(NPC):
                    act.wait_ge(s["z_mm"], b * NPC + c + 1)
                    if c >= 2:
                        act.wait_ge(s["g_ready"], b * NPC + c - 1)
                    part, _ = rows(c)
                    j = 4 + 2 * (c % 2)
                    act.activation(zg[c % 2][0], bank(j), ACT.Gelu)
                    act.activation(zg[c % 2][1][part, :], ps[part, j + 1, 0:PC], ACT.Gelu).then_inc(s["z_act"], 1)
                group_std(b, 1)
                act.wait_ge(s["qkv_zero"], b + 1)
                for c in range(NPC):
                    act.wait_ge(s["qkv_mm"], b * NPC + c + 1)
                    for t in range(3):
                        ins = act.copy(pad_rows(qkv_pads[t], 1 + 8 * c), square(bank(3 * (c % 2) + t, C)))
                    ins.then_inc(s["qkv_ev"], 1)
                act.wait_ge(s["qkv_ev"], (b + 1) * NPC)
                unit_products(act, b, back_units())
                act.wait_ge(s["qkv_conv"], b + 1)
                apart(act)
                act.preload_act_table_set(LN_EXP_TABLES)
                for n in range(NORMS + 1):
                    if n < NORMS:
                        if n >= 2:
                            act.wait_ge(s["n_ss"], b * NORMS + n - 1)
                        act.activation(nsq[n % 2], qkv[n // 2][:, (n % 2) * HL:(n % 2 + 1) * HL], ACT.Square)\
                            .then_inc(s["n_sq"], 1)
                    if n:
                        x = nrt[(n - 1) % 2]
                        act.wait_ge(s["n_max"], b * NORMS + n)
                        act.activation(x, x, ACT.Ln).then_inc(s["n_ln"], 1)
                        act.wait_ge(s["n_ln"], b * NORMS + n)
                        act.activation(x, x, ACT.Exp, scale=-0.5).then_inc(s["n_rt"], 1)
                act.wait_ge(s["tap_added"], (b + 1) * 24)
                for t in range(2):
                    act.wait_ge(s["n_mul"], b * NORMS + 2 * (t + 1))
                    act.copy(parts[t][0], qkv[t]).then_inc(s["a_s1"], 1)
                for t in range(2):
                    act.wait_ge(s["a_r1"], b * 2 + t + 1)
                    act.copy(parts[t][1], qkv[t]).then_inc(s["a_s2"], 1)

            def attention(ab):
                for kk in range(K):
                    stretches(act, lambda q, first: stretch(None, kk, q, first, ab, False))
                last_leftover(ab)

            batches(act, front, directions, back, attention)

        @block.vector
        def _(dve):
            dve.memset(gn_eps[:, :], GN_EPS).then_inc(s["eps_set"], 1)
            dve.wait_ge(s["w_loaded"], W_LOADED)
            for t in range(2):
                dve.tensor_reduce(skip_sum[t][:, :], skip[t][:, :], mybir.AxisListType.X, ALU.add)\
                   .then_inc(s["skip_summed"], 1)
            dve.wait_ge(s["skip_summed"], 2)

            def group_norm(b, t, chain, x):
                for c in range(NPC):
                    ins = dve.bn_stats(stats[:, 6 * c:6 * c + 6], x[:, piece(c)])
                chain.link(ins)
                apart(dve)
                dve.bn_aggr(mv[:, :], stats[:, :]).then_inc(s["gn_stat"], 1)
                dve.wait_ge(s["gn_mean"], b * 2 + t + 1)
                chain.link(dve.tensor_copy(gn[:, 0:1], ps[0:C, 7, 0:1]))
                chain.link(dve.tensor_tensor(gn[:, 1:2], mv[:, 0:1], gn[:, 0:1], ALU.subtract))
                dve.scalar_tensor_tensor(out=gn[:, 3:4], in0=gn[:, 1:2], scalar=gn[:, 1:2], in1=mv[:, 1:2],
                                         op0=ALU.mult, op1=ALU.add).then_inc(s["gn_dev"], 1)
                dve.wait_ge(s["gn_std"], b * 2 + t + 1)
                chain.link(dve.reciprocal(gn[:, 4:5], gn[:, 2:3]))
                dve.tensor_scalar(xn, x, gn[:, 0:1], gn[:, 4:5], ALU.subtract, ALU.mult)\
                   .then_inc(s["xn_ready"], 1)

            def conv(chain, work, done):
                marks = {}
                for tap in range(9):
                    for j, (dst, pad, w) in enumerate(work):
                        if tap == 0:
                            ins = dve.tensor_scalar(square(dst), window(pad, 0), w[:, 0:1], None, ALU.mult)
                        else:
                            chain.wait(marks[j])
                            ins = dve.scalar_tensor_tensor(out=square(dst), in0=window(pad, tap),
                                                           scalar=w[:, tap:tap + 1], in1=square(dst),
                                                           op0=ALU.mult, op1=ALU.add)
                        if tap == 8 and j == len(work) - 1:
                            ins.then_inc(s[done], 1)
                        else:
                            marks[j] = chain.mark(ins)
                chain.wait()

            def job_stage(kidx, k, q, j, name):
                BI = kidx * NS + q
                d, m = jobs_f[j % 2]
                P = jobs_p[j % 2]

                def own(stage):
                    dve.wait_ge(s["job_dve"], BI * ND + place(DVE_JOBS, j, stage))

                def act_done(stage):
                    dve.wait_ge(s["job_act"], BI * NA + place(ACT_JOBS, j, stage))

                if name == "add":
                    act_done("ln")
                    ins = dve.tensor_tensor(d, d, m, ALU.add)
                elif name == "times_u":
                    own("add")
                    if j == 2:
                        x = (ut_b if k % 2 else u[1])[:, bass.ds(q * PC, PC)]
                        ins = dve.tensor_tensor(m, d, x, ALU.mult)
                    elif k % 2:
                        x = swapped(u[0])[:, bass.ds(q * 16 + 8 * j, 8), :]
                        ins = dve.tensor_tensor(square(m), square(d), x, ALU.mult)
                    else:
                        ins = dve.tensor_tensor(m, d, u[0][:, bass.ds(q * (2 * PC) + j * PC, PC)], ALU.mult)
                elif name == "d_rest":
                    act_done("d0")
                    own("times_u")
                    ins = dve.tensor_tensor(d, d, P[:, 0, :], ALU.subtract)
                elif name == "u_rest":
                    act_done("u0")
                    ins = dve.tensor_tensor(m, m, P[:, 3, :], ALU.subtract)
                elif name == "d2":
                    act_done("d1")
                    ins = dve.tensor_tensor(P[:, 2, :], d, P[:, 1, :], ALU.subtract)
                else:
                    act_done("u1")
                    ins = dve.tensor_tensor(P[:, 5, :], m, P[:, 4, :], ALU.subtract)
                ins.then_inc(s["job_dve"], 1)

            def mult_b(kidx, kk, q, x, first):
                X = kidx * (2 * DSTEPS) + q * (2 * BODY) + x
                v = x % (2 * SPT)
                if first and x < 2 * SPT and x % 2 == 0:
                    dve.wait_ge(rep_loaded[v // 2], 32 * (kidx + 1))
                if not (first and x < 3):
                    dve.wait_ge(s["h_ready"], X - 2)
                dve.wait_ge(s["ubc"], X + 1)
                dve.tensor_tensor(b_ring[x % 3], bank(BANK_U[x % 2]), rep_piece(0, kk, v), ALU.mult)\
                   .then_inc(s["b_ready"], 1)

            def scan_half(kidx, kk, q, x, first):
                X = kidx * (2 * DSTEPS) + q * (2 * BODY) + x
                back = KS_ORDER[kk] >= 2
                v = natural(kk, x % (2 * SPT))
                if x % 2 == 0:
                    dve.wait_ge(s["da_ready"], kidx * DSTEPS + q * BODY + (x // 2 + 1))
                if not (first and x < 2):
                    dve.wait_ge(s["hc_ready"], X - 1)
                if not (first and x == 0):
                    dve.wait_ge(s["h_ready"], X)
                dve.wait_ge(s["b_ready"], X + 1)
                init = 0.0
                if x % (2 * SPT):
                    prev = h_ring[(x + 1) % 2]
                    init = prev[:, 0:1] if back else prev[:, PC - 1:PC]
                o, d0, d1 = h_ring[x % 2], da_ring[x // 2 % 2][:, piece(v % 2)], b_ring[x % 3]
                if back:
                    o, d0, d1 = o[:, ::-1], d0[:, ::-1], d1[:, ::-1]
                dve.tensor_tensor_scan(o, d0, d1, init, ALU.mult, ALU.add).then_inc(s["h_ready"], 1)

            def y_evacuate(kidx, q, T, add):
                dve.wait_ge(s["hc_used"], kidx * NT + q * (2 * TG) + (T + 1))
                dst = y_acc[:, bass.ds(q * (2 * TG * YP) + T * YP, YP)]
                if add:
                    dve.tensor_tensor(dst, bank(BANK_Y, n=YP), dst, ALU.add).then_inc(s["y_ev"], 1)
                else:
                    dve.tensor_copy(dst, bank(BANK_Y, n=YP)).then_inc(s["y_ev"], 1)

            def leftover(f, t, n):
                if t == COPY_O:
                    dve.wait_ge(s["pv_done"], f * MB)
                    dve.tensor_copy(att_o, bank(BANK_PV)).then_inc(s["o_copied"], 1)
                if t == DIVIDE:
                    dve.wait_ge(s["den_act"], f * 2)
                    dve.scalar_tensor_tensor(out=att_n, in0=att_o, scalar=NEAR_1, in1=att_r,
                                             op0=ALU.mult, op1=ALU.mult).then_inc(s["on_ready"], 1)
                if t == RESIDUAL:
                    dve.wait_ge(s["pj_ev"], f)
                    x = xres[:, bass.ds(n * PC, PC)]
                    dve.tensor_tensor(x, x, att_r[0:C, :], ALU.add).then_inc(s["xo_done"], 1)

            def last_leftover(ab):
                for t in (COPY_O, DIVIDE, RESIDUAL):
                    leftover((ab + 1) * STRETCHES, t, NPC - 1)

            def stretch(b, kk, q, first, ab, scan=True):
                kidx = b * K + kk if scan else None
                att, att_first = ab is not None, first and kk == 0
                if scan:
                    mult_b(kidx, kk, q, 0, first)
                for t in range(BODY):
                    if scan:
                        for x in (2 * t, 2 * t + 1):
                            if x + 1 < 2 * BODY:
                                mult_b(kidx, kk, q, x + 1, first)
                            scan_half(kidx, kk, q, x, first)
                        if kk == 2 and first and t == 2 * SPT:
                            dve.wait_ge(s["y_stored"], b * (2 * NS * 256) + NS * 256)
                        if t % SPT == 0 and not (first and t < 2 * SPT):
                            y_evacuate(kidx, q, t // SPT - 2, kk % 2)
                    if att and not att_first:
                        n = (kk % 2) * NS + q - 1 if not (first and kk == 2) else NPC - 1
                        leftover(ab * STRETCHES + kk * NS + q, t, n)
                    if scan and kk + 1 < K:
                        for when, j, _, name in DVE_JOBS:
                            if when == t:
                                job_stage(kidx + 1, KS_ORDER[kk + 1], q, j, name)

            def front(b):
                chain = Chain(dve, s["dve_chain"], b, DVE_CHAIN)
                dve.wait_ge(s["x_loaded"], 16 * (b + 1))
                group_norm(b, 0, chain, xin)
                dve.wait_ge(s["inp_ev"], (b + 1) * NPC)
                conv(chain, [(u[0], pads[0], taps[0])], "conv_done")
                fronts[0] = chain.n

                def first_jobs(q, first):
                    for when, j, _, name in DVE_JOBS:
                        job_stage(b * K, KS_ORDER[0], q, j, name)

                stretches(dve, first_jobs)

            fronts = [0]

            def directions(b, ab):
                for kk in range(K):
                    kidx = b * K + kk
                    stretches(dve, lambda q, first: stretch(b, kk, q, first, ab))
                    for T in (2 * TG - 2, 2 * TG - 1):
                        y_evacuate(kidx, NS - 1, T, kk % 2)
                if ab is not None:
                    last_leftover(ab)

            def back(b):
                chain = Chain(dve, s["dve_chain"], b, DVE_CHAIN)
                chain.n = fronts[0]
                dve.wait_ge(s["y_loaded"], 96 * (b + 1))
                marks = [chain.mark(dve.tensor_tensor(square(y[0]), square(y[0]), swapped(yt[0]), ALU.add))]
                for hf in range(2):
                    p = slice(64 * hf, 64 * hf + 64)
                    x = square(y[1][p, :])
                    ins = dve.tensor_tensor(x, x, swapped(yt[1][p, :])[:, 24 * hf:24 * hf + 24, :], ALU.add)
                marks.append(chain.mark(ins))
                for t in range(2):
                    chain.wait(marks[t])
                    ins = dve.scalar_tensor_tensor(out=y[t], in0=u[t], scalar=skip_sum[t][:, :], in1=y[t],
                                                   op0=ALU.mult, op1=ALU.add)
                ins.then_inc(s["y_summed"], 1)
                dve.wait_ge(s["y_summed"], b + 1)

                def both(c):
                    part, cols = rows(c)
                    return ((0, slice(0, 128), y[0][:, piece(c)]), (1, part, y[1][part, cols]))

                for c in range(NPC):
                    dve.wait_ge(s["ln_mean"], b * NPC + c + 1)
                    for t, p, x in both(c):
                        ins = dve.tensor_tensor(x, x, ps[p, c % 2, 0:PC], ALU.subtract)
                    ins.then_inc(s["ln_cent"], 1)
                dve.wait_ge(s["ln_cent"], (b + 1) * NPC)
                dve.wait_ge(s["xr_loaded"], (b + 1) * 16)
                for c in range(NPC):
                    dve.wait_ge(s["ln_rstd"], b * 3 + c // 2 + 1)
                    for t, p, x in both(c):
                        ins = dve.tensor_tensor(x, x, rstd[p, piece(c)], ALU.mult)
                    chain.link(ins)
                    for t, p, x in both(c):
                        ins = dve.tensor_scalar(x, x, ln_w[t][p, :], ln_b[t][p, :], ALU.mult, ALU.add)
                    chain.link(ins)
                    dve.wait_ge(s["z_act"], b * NPC + c + 1)
                    for t, p, x in both(c):
                        ins = dve.tensor_tensor(x, x, zg[c % 2][t][p, :], ALU.mult)
                    ins.then_inc(s["g_ready"], 1)
                    if c:
                        dve.wait_ge(s["o_mm"], b * NPC + c)
                        x = xres[:, piece(c - 1)]
                        dve.tensor_tensor(x, x, bank((c - 1) % 2, C), ALU.add).then_inc(s["o_ev"], 1)
                dve.wait_ge(s["o_mm"], (b + 1) * NPC)
                x = xres[:, piece(NPC - 1)]
                dve.tensor_tensor(x, x, bank((NPC - 1) % 2, C), ALU.add).then_inc(s["o_ev"], 1)
                dve.wait_ge(s["o_ev"], (b + 1) * NPC)
                group_norm(b, 1, chain, xres[:, :])
                dve.wait_ge(s["qkv_ev"], (b + 1) * NPC)
                conv(chain, [(qkv[t], qkv_pads[t], qkv_taps[:, 9 * t:9 * t + 9]) for t in range(2)], "qkv_conv")
                dve.memset(bank(BANK_PV), 0.0).then_inc(s["pv_zero"], 1)
                dve.memset(v_cols[:, :, HD:HD + 1], 1.0).then_inc(s["v_ones"], 1)
                for n in range(NORMS + 1):
                    if n < NORMS:
                        dve.wait_ge(s["n_ss"], b * NORMS + n + 1)
                        if n >= 2:
                            dve.wait_ge(s["n_mul"], b * NORMS + n - 1)
                        dve.tensor_scalar(nrt[n % 2].rearrange("p (a r) -> p a r", a=3),
                                          ps[0:C, 3 * (n % 2):3 * (n % 2) + 3, 0:PC], NORM_EPS ** 2, None, ALU.max)\
                           .then_inc(s["n_max"], 1)
                    if n:
                        dve.wait_ge(s["n_rt"], b * NORMS + n)
                        x = qkv[(n - 1) // 2][:, ((n - 1) % 2) * HL:((n - 1) % 2 + 1) * HL]
                        dve.tensor_tensor(x, x, nrt[(n - 1) % 2], ALU.mult).then_inc(s["n_mul"], 1)
                dve.wait_ge(s["n_mul"], (b + 1) * NORMS)
                for t in range(2):
                    dve.wait_ge(s["a_s1"], b * 2 + t + 1)
                    dve.tensor_tensor(qkv[t], qkv[t], parts[t][0], ALU.subtract).then_inc(s["a_r1"], 1)
                for t in range(2):
                    dve.wait_ge(s["a_r1"], b * 2 + t + 1)
                    dve.wait_ge(s["a_s2"], b * 2 + t + 1)
                    dve.tensor_tensor(parts[t][2], qkv[t], parts[t][1], ALU.subtract).then_inc(s["a_s3"], 1)
                for j in range(5):
                    m0, m1 = 4 * j, min(4 * j + 4, MB)
                    dve.wait_ge(s["v_tr"], b * 5 + j + 1)
                    src = ps[:, 6 - j % 2, 0:(m1 - m0) * C].rearrange("p (m d) -> p m d", d=HD)
                    dve.tensor_copy(v_cols[:, m0 * HEADS:m1 * HEADS, 0:HD], src).then_inc(s["v_ev"], 1)
                chain.end()

            def attention(ab):
                for kk in range(K):
                    stretches(dve, lambda q, first: stretch(None, kk, q, first, ab, False))
                last_leftover(ab)

            batches(dve, front, directions, back, attention)

        @block.tensor
        def _(pe):
            pe.wait_ge(s["w_loaded"], W_LOADED)

            def group_stats(b, t):
                pe.wait_ge(s["gn_stat"], b * 2 + t + 1)
                pe.matmul(ps[0:C, 7, 0:1], group_mean[:, :], mv[:, 0:1], start=True, stop=True)\
                  .then_inc(s["gn_mean"], 1)
                pe.wait_ge(s["gn_dev"], b * 2 + t + 1)
                pe.matmul(ps[0:C, 6, 0:1], group_mean[:, :], gn[:, 3:4], start=True, stop=True)\
                  .then_inc(s["gn_var"], 1)
                pe.wait_ge(s["xn_ready"], b * 2 + t + 1)

            def pick(t):
                i = t // SPT % TG
                return pick_channel[:, i * 128:(i + 1) * 128]

            def broadcast_delta(kk, t, slots):
                x = 2 * t % (2 * SPT)
                for v in sorted((natural(kk, x), natural(kk, x + 1))):
                    ins = pe.matmul(bank(slots["delta", 2 * t + v % 2]), pick(t), st[t // SPG][0][:, piece(v)],
                                    start=True, stop=True)
                ins.then_inc(s["dbc"], 1)

            def broadcast_u(kidx, kk, q, x, first):
                X = kidx * (2 * DSTEPS) + q * (2 * BODY) + x
                if not (first and x < 2):
                    pe.wait_ge(s["b_ready"], X - 1)
                v = natural(kk, x % (2 * SPT))
                pe.matmul(bank(BANK_U[x % 2]), pick(x // 2), st[x // 2 // SPG][1][:, piece(v)], start=True, stop=True)\
                  .then_inc(s["ubc"], 1)

            def sum_tile(kidx, q, T, i, first=False):
                if i == 0:
                    pe.wait_ge(s["hc_ready"], (kidx * DSTEPS + q * BODY + (T + 1) * SPT) * 2)
                    if not (first and T == 0):
                        pe.wait_ge(s["y_ev"], kidx * NT + q * (2 * TG) + T)
                for j in range(4):
                    col = (4 * j + i) * YP
                    ins = pe.matmul(ps[32 * j:32 * j + 32, BANK_Y, 0:YP], sum_states[:, 32 * i:32 * i + 32],
                                    hc[T % 2][:, col:col + YP], start=(i == 0), stop=(i == 3))
                if i == 3:
                    ins.then_inc(s["hc_used"], 1)

            def values(hg, f, m, wait_copied):
                pe.wait_ge(s["exp_done"], f * PIECES + (m + 1) * HG)
                if wait_copied:
                    pe.wait_ge(s["o_copied"], f)
                for h in range(HG):
                    ins = pe.matmul(ps[32 * h:32 * h + 13, BANK_PV, 0:PC], v_cols[:, m * HEADS + hg * HG + h, :],
                                    probs[(m % 2) * HG + h], start=(m == 0), stop=(m == MB - 1))
                ins.then_inc(s["pv_done"], 1)

            def denominators(f, bk):
                pe.wait_ge(s["o_copied"], f)
                pe.matmul(bank(bk), pick_den[:, :], att_o, start=True, stop=True).then_inc(s["den_done"], 1)

            def project(hg, f, bk):
                pe.wait_ge(s["on_ready"], f)
                pe.matmul(bank(bk, C), proj_w[:, hg * C:(hg + 1) * C], att_n, start=True, stop=True)\
                  .then_inc(s["pj_done"], 1)

            def job(k, j, q, bk):
                if j < 2:
                    ins = pe.matmul(bank(bk), dt_proj[0][:, k * DA:(k + 1) * DA],
                                    dts[:, bass.ds(q * (2 * PC) + j * PC, PC)], start=True, stop=True)
                else:
                    for hf in range(2):
                        col = k * 192 + 64 * (1 - hf)
                        ins = pe.matmul(bank(bk), dt_proj[1][:, col:col + 128],
                                        dts[:, bass.ds(q * PC + hf * HL, PC)], start=(hf == 0), stop=(hf == 1))
                ins.then_inc(s["dt_mm"], 1)

            def stretch(b, kk, q, first, ab, scan=True):
                kidx, hg = b * K + kk if scan else None, kk // 2
                att, att_first = ab is not None, first and kk == 0
                prev = att and not att_first
                prev_hg = (kk * NS - 1) // NPC if first else hg
                prep = scan and kk + 1 < K
                slots, before, order = ring_slots(att, prev, prep, scan)
                f = ab * STRETCHES + kk * NS + q if att else None
                BI = (kidx + 1) * NS + q if prep else None

                def free(item):
                    if before[item] is None:
                        if scan and not first:
                            pe.wait_ge(s["da_ready"], kidx * DSTEPS + q * BODY)
                        if prev:
                            i = order.index(item)
                            last = PIECES if scan else 1 + max(
                                x - y for y in (0, 2) for x in range(PIECES - RING + y, PIECES + y)
                                if x % RING == i)
                            pe.wait_ge(s["exp_done"], (f - 1) * PIECES + last)
                        return
                    kind, n = before[item]
                    if kind == "delta":
                        pe.wait_ge(s["da_ready"], kidx * DSTEPS + q * BODY + (n // 2 + 1))
                    elif kind == "score":
                        pe.wait_ge(s["exp_done"], f * PIECES + (n + 1))
                    elif kind == "den":
                        pe.wait_ge(s["den_act"], f * 2 - 1)
                    elif kind == "proj":
                        pe.wait_ge(s["pj_ev"], f)
                    else:
                        pe.wait_ge(s["job_act"], BI * NA + place(ACT_JOBS, n, "relu"))

                def score(p):
                    m, h = divmod(p, HG)
                    free(("score", p))
                    if h == 0 and m % (MB // SPT) == 0 and (first and kk % 2 == 0):
                        pe.wait_ge(ks_loaded[m // (MB // SPT)], (ab * 2 + hg + 1) * (16 * TERMS))
                    pe.matmul(bank(slots["score", p]), k_parts[:, h, m * 128:(m + 1) * 128],
                              q_ring[:, bass.ds(q, 1), h, :].rearrange("p s l -> p (s l)"),
                              start=True, stop=True).then_inc(s["s_done"], 1)

                if scan:
                    pe.wait_ge(st_loaded[0], (kidx * NS + q + 1) * 32)
                if att:
                    pe.wait_ge(s["qs_loaded"], (f + 1) * (16 * TERMS))
                def sum_part(t, n):
                    T, i = (t // SPT - 1, n) if t % SPT else (t // SPT - 2, 2 + n)
                    if T >= 0:
                        sum_tile(kidx, q, T, i, first)
                    elif not first:
                        sum_tile(kidx, q - 1, T + 2 * TG, i)

                next_m = 0
                for t in range(BODY):
                    if scan and t == SPG:
                        pe.wait_ge(st_loaded[1], (kidx * NS + q + 1) * 32)
                    if scan:
                        broadcast_u(kidx, kk, q, 2 * t, first)
                    if scan and t % SPT != 1:
                        sum_part(t, 0)
                    if scan:
                        free(("delta", 2 * t))
                        free(("delta", 2 * t + 1))
                        broadcast_delta(kk, t, slots)
                    if att:
                        score(PER_STEP * t)
                    if scan and t % SPT != 1:
                        sum_part(t, 1)
                    if att:
                        score(PER_STEP * t + 1)
                    if scan:
                        broadcast_u(kidx, kk, q, 2 * t + 1, first)
                    if prev and t == DEN_MM:
                        free(("den", 0))
                        denominators(f, slots["den", 0])
                    if prev and t == PROJ_MM:
                        free(("proj", 0))
                        project(prev_hg, f, slots["proj", 0])
                    if prep and t in JOB_START:
                        j = JOB_START.index(t)
                        free(("job", j))
                        job(KS_ORDER[kk + 1], j, q, slots["job", j])
                    if att and t == 0 and prev:
                        values(prev_hg, f - 1, MB - 1, False)
                    while att and next_m * HG + HG - 1 < PER_STEP * t:
                        values(hg, f, next_m, next_m == 0 and prev)
                        next_m += 1
                    if att:
                        score(PER_STEP * t + 2)

            def last_leftover(ab):
                f = (ab + 1) * STRETCHES
                values(1, f - 1, MB - 1, False)
                denominators(f, 0)
                project(1, f, 1)

            def front(b):
                group_stats(b, 0)
                for c in range(NPC):
                    if c >= 2:
                        pe.wait_ge(s["inp_ev"], b * NPC + c - 1)
                    part, _ = rows(c)
                    pe.matmul(bank(2 * (c % 2)), in_proj[:, 0:DA], xn[:, piece(c)], start=True, stop=True)
                    pe.matmul(ps[part, 2 * (c % 2) + 1, 0:PC], in_proj[:, DA:DI], xn[:, piece(c)],
                              start=True, stop=True).then_inc(s["inp_mm"], 1)
                pe.wait_ge(s["u_ready"], b + 1)
                for c in range(NPC):
                    if c >= 2:
                        pe.wait_ge(s["xd_ev"], b * NPC + c - 1)
                    part, cols = rows(c)
                    for odd in range(2):
                        for t in range(2):
                            w = x_proj[t][:, odd * 128:(odd + 1) * 128]
                            if t:
                                w, x = w[part, :], square((ut_b if odd else u[1])[part, cols])
                            else:
                                x = (swapped if odd else square)(u[0])[:, 8 * c:8 * c + 8, :]
                            ins = pe.matmul(square(bank(2 * (c % 2) + odd)), w, x, start=(t == 0), stop=(t == 1))
                    ins.then_inc(s["xd_mm"], 1)
                pe.wait_ge(s["xd_ev"], (b + 1) * NPC)

                def first_jobs(q, first):
                    BI = b * (K * NS) + q
                    for j in range(JOBS):
                        if j == 2:
                            pe.wait_ge(s["job_act"], BI * NA + place(ACT_JOBS, 0, "relu"))
                        elif not first:
                            pe.wait_ge(s["job_act"], BI * NA)
                        job(KS_ORDER[0], j, q, 5 + j % 2)

                stretches(pe, first_jobs)

            def directions(b, ab):
                for kk in range(K):
                    stretches(pe, lambda q, first: stretch(b, kk, q, first, ab))
                    for n in range(8 * TG - 6, 8 * TG):
                        sum_tile(b * K + kk, NS - 1, n // 4, n % 4)
                if ab is not None:
                    last_leftover(ab)

            def back(b):
                pe.wait_ge(s["y_summed"], b + 1)

                def over_channels(dst, w, x, c):
                    part, cols = rows(c)
                    pe.matmul(dst, w[0], x[0], start=True, stop=False)
                    return pe.matmul(dst, w[1][part, :], x[1], start=False, stop=True)

                for c in range(NPC + 1):
                    if c < NPC:
                        if c >= 2:
                            pe.wait_ge(s["ln_cent"], b * NPC + c - 1)
                        part, cols = rows(c)
                        over_channels(bank(c % 2), (mean192[:, :], mean192), (y[0][:, piece(c)], y[1][part, cols]),
                                      c).then_inc(s["ln_mean"], 1)
                    if c:
                        pe.wait_ge(s["ln_sq"], b * NPC + c)
                        if c >= 3:
                            pe.wait_ge(s["ln_log"], b * NPC + c - 2)
                        j = (c - 1) % 2
                        part, _ = rows(c - 1)
                        over_channels(bank(2 + j), (mean192[:, :], mean192), (sq[j][0], sq[j][1][part, :]), c - 1)\
                            .then_inc(s["ln_var"], 1)
                pe.wait_ge(s["ln_cent"], (b + 1) * NPC)
                pe.wait_ge(s["xn_loaded"], 16 * (b + 1))
                for c in range(NPC + 1):
                    if c < NPC:
                        if c >= 2:
                            pe.wait_ge(s["z_act"], b * NPC + c - 1)
                        part, _ = rows(c)
                        j = 4 + 2 * (c % 2)
                        pe.matmul(bank(j), in_proj[:, DI:DI + DA], xn[:, piece(c)], start=True, stop=True)
                        pe.matmul(ps[part, j + 1, 0:PC], in_proj[:, DI + DA:2 * DI], xn[:, piece(c)],
                                  start=True, stop=True).then_inc(s["z_mm"], 1)
                    if c:
                        pe.wait_ge(s["g_ready"], b * NPC + c)
                        if c >= 3:
                            pe.wait_ge(s["o_ev"], b * NPC + c - 2)
                        part, cols = rows(c - 1)
                        over_channels(bank((c - 1) % 2, C), (out_proj[0][:, :], out_proj[1]),
                                      (y[0][:, piece(c - 1)], y[1][part, cols]), c - 1).then_inc(s["o_mm"], 1)
                group_stats(b, 1)
                for c in range(NPC):
                    if c >= 2:
                        pe.wait_ge(s["qkv_ev"], b * NPC + c - 1)
                    for t in range(3):
                        ins = pe.matmul(bank(3 * (c % 2) + t, C), qkv_w[:, t * C:(t + 1) * C], xn[:, piece(c)],
                                        start=True, stop=True)
                    ins.then_inc(s["qkv_mm"], 1)
                for n in range(NORMS):
                    pe.wait_ge(s["n_sq"], b * NORMS + n + 1)
                    if n >= 2:
                        pe.wait_ge(s["n_max"], b * NORMS + n - 1)
                    for i in range(3):
                        ins = pe.matmul(bank(3 * (n % 2) + i, C), head_ones[:, :], nsq[n % 2][:, piece(i)],
                                        start=True, stop=True)
                    ins.then_inc(s["n_ss"], 1)
                pe.wait_ge(s["n_max"], (b + 1) * NORMS)
                pe.wait_ge(s["tap_added"], (b + 1) * 24)
                for j in range(5):
                    if j >= 2:
                        pe.wait_ge(s["v_ev"], b * 5 + j - 1)
                    for m in range(4 * j, min(4 * j + 4, MB)):
                        col = (m % 4) * C
                        ins = pe.transpose(ps[:, 6 - j % 2, col:col + C], qkv[2][:, m * 128:(m + 1) * 128],
                                           ident[:, :])
                    ins.then_inc(s["v_tr"], 1)
                pe.wait_ge(s["v_ev"], (b + 1) * 5)
                pe.wait_ge(s["v_ones"], b + 1)
                pe.wait_ge(s["pv_zero"], b + 1)

            def attention(ab):
                for kk in range(K):
                    stretches(pe, lambda q, first: stretch(None, kk, q, first, ab, False))
                last_leftover(ab)

            batches(pe, front, directions, back, attention)


def kernel(**inputs):
    import ml_dtypes
    import numpy as np
    import concourse.bacc as bacc
    from concourse.bass_utils import run_bass_kernel_spmd

    x = np.asarray(inputs["x"])
    NB = x.shape[0]
    w = {n.replace("L0_conv_", "").replace("L1_conv_", "l1_"): np.asarray(v) for n, v in inputs.items()}

    def cols(m):
        return m[0:DA], np.concatenate([m[DA:DI], m[DA:DI]])

    f32 = np.float32
    arrays = {"x": x.reshape(NB, C, L), "in_projT": w["in_proj_w"].T}
    arrays["taps_a"], arrays["taps_b"] = cols(w["conv_w"].reshape(DI, 9))
    arrays["conv_b_a"], arrays["conv_b_b"] = cols(w["conv_b"].reshape(DI, 1))
    x_proj = np.zeros((DI, 2, 128), f32)
    dt_a, dt_b = np.zeros((128, K, DA), f32), np.zeros((128, K, 192), f32)
    for k in range(K):
        r, r_bc = DT_ROWS[k], BC_ROWS[k]
        x_proj[:, k % 2, r:r + R] = w["x_proj_w"][k, 0:R].T
        x_proj[:, k % 2, r_bc:r_bc + 2 * N] = w["x_proj_w"][k, R:R + 2 * N].T
        dt_a[r:r + R, k, :] = w["dt_w"][k, 0:DA].T
        dt_b[r:r + R, k, 64:128] = w["dt_w"][k, DA:DI].T
    arrays["x_proj_a"], arrays["x_proj_b"] = cols(x_proj.reshape(DI, 2 * 128))
    arrays["dt_proj_a"], arrays["dt_proj_b"] = dt_a.reshape(128, K * DA), dt_b.reshape(128, K * 192)
    arrays["dt_b_a"], arrays["dt_b_b"] = cols(w["dt_b"].T)
    arrays["a_logs"] = w["A_logs"].reshape(K * NG * TG, 128).T
    arrays["ds_a"], arrays["ds_b"] = cols(w["Ds"].reshape(K, DI).T)
    arrays["ln_w_a"], arrays["ln_w_b"] = cols(w["ln_w"].reshape(DI, 1))
    arrays["ln_b_a"], arrays["ln_b_b"] = cols(w["ln_b"].reshape(DI, 1))
    arrays["out_proj_a"], arrays["out_proj_b"] = cols(w["out_proj_w"].T)
    arrays["qkv_wT"] = w["l1_w_qkv"].T
    arrays["qkv_taps"] = w["l1_w_dw"].reshape(3, C, 9).transpose(1, 0, 2).reshape(C, 27)
    proj = np.zeros((128, 2, C), f32)
    for h in range(HEADS):
        r = 32 * (h % HG)
        proj[r:r + HD, h // HG, :] = w["l1_w_proj"][:, h * HD:(h + 1) * HD].T
    arrays["proj_wT"] = proj.reshape(128, 2 * C)
    pick = np.zeros((3, 32, TG, 8, N), f32)
    states = np.zeros((8, N, TG, 32), f32)
    for i in range(TG):
        for d in range(8):
            pick[:, 8 * i + d, i, d, :] = 1
            states[d, :, i, 8 * i + d] = 1
    arrays["pick_channel"] = pick.reshape(96, TG * 128).astype(ml_dtypes.bfloat16)
    arrays["sum_states"] = states.reshape(128, TG * 32)
    per = C // 32
    arrays["group_mean"] = np.kron(np.eye(32), np.full((per, per), 1.0 / per)).astype(f32)
    arrays["mean192"] = np.full((128, 128), 1.0 / DI, f32)
    arrays["head_ones"] = np.kron(np.eye(HEADS), np.ones((HD, HD))).astype(f32)
    arrays["ident"] = np.eye(C, dtype=f32)
    den = np.zeros((128, 128), f32)
    for h in range(HG):
        den[32 * h + HD, 32 * h:32 * h + 32] = 1
    arrays["pick_den"] = den
    arrays = {f"in_{n}": np.ascontiguousarray(v) for n, v in arrays.items()}

    nc = bacc.Bacc("TRN2", target_bir_lowering=False, num_devices=1)
    aps = {n[3:]: nc.dram_tensor(n, v.shape, mybir.dt.from_np(v.dtype), kind="ExternalInput").ap()
           for n, v in arrays.items()}
    out = nc.dram_tensor("out", (NB, C, L), F32, kind="ExternalOutput").ap()
    build(nc, NB, aps, out)
    got = run_bass_kernel_spmd(nc, [arrays], core_ids=[0]).results[0]["out"]
    return got.reshape(NB, C, H, W)
```
